# Optimizing a Trainium2 kernel written in Bass

```python
import numpy as np
import jax
import jax.numpy as jnp

def _softmax(x, axis=-1):
    return jax.nn.softmax(x, axis=axis)

def _gelu(x):
    return jax.nn.gelu(x, approximate=True)

def _silu(x):
    return jax.nn.silu(x)

def _sigmoid(x):
    return jax.nn.sigmoid(x)

def _layernorm(x, axis=-1, eps=1e-05):
    m = jnp.mean(x, axis=axis, keepdims=True)
    v = jnp.var(x, axis=axis, keepdims=True)
    return (x - m) / jnp.sqrt(v + eps)

def _scatter_add(tgt, idx, src, axis=0):
    return tgt.at[idx].add(src)

def _segment_sum(src, seg, n):
    return jax.ops.segment_sum(src, seg, n)
kernel_name = 'mk_adaln_d1_jaxref_r4_a360af'

def setup_inputs(seed: int=0):
    np.random.seed(seed)
    _w = jnp.asarray

    def _L0_attn_setup():
        import jax, jax.numpy as jnp
        import numpy as np
        EPS = 1e-15
        HEAD_DIM = 32
        PAD_VAL = 1.0
        key = jax.random.key(seed)
        k1, k2, k3, k4 = jax.random.split(key, 4)
        B, N, C = (2, 1024, 512)
        s = 1.0 / np.sqrt(C).astype(np.float32)
        x = jax.random.normal(k1, (B, N, C), jnp.float32)
        w_qkv = jax.random.normal(k2, (3 * C, C), jnp.float32) * s
        w_proj = jax.random.normal(k3, (C, C), jnp.float32) * s
        b_proj = jax.random.normal(k4, (C,), jnp.float32) * 0.01
        return {'x': x, 'w_qkv': w_qkv, 'w_proj': w_proj, 'b_proj': b_proj}
    _L0_attn_in = _L0_attn_setup()

    def _L0_ffn_setup():
        import jax, jax.numpy as jnp
        import numpy as np
        E = 8
        K = 2
        DIM = 512
        INTER = 352
        N_SHARED = 2
        STD = 0.02
        key = jax.random.key(seed)
        ks = jax.random.split(key, 9)
        B, S = (2, 512)
        return {'x': jax.random.normal(ks[0], (B, S, DIM), dtype=jnp.float32), 'gate_w': jax.random.normal(ks[1], (E, DIM), dtype=jnp.float32) * STD, 'router_bias': jnp.zeros((E,), dtype=jnp.float32), 'W1': jax.random.normal(ks[2], (E, DIM, INTER), dtype=jnp.float32) * STD, 'W3': jax.random.normal(ks[3], (E, DIM, INTER), dtype=jnp.float32) * STD, 'W2': jax.random.normal(ks[4], (E, INTER, DIM), dtype=jnp.float32) * STD, 'sw1': jax.random.normal(ks[5], (N_SHARED * INTER, DIM), dtype=jnp.float32) * STD, 'sw3': jax.random.normal(ks[6], (N_SHARED * INTER, DIM), dtype=jnp.float32) * STD, 'sw2': jax.random.normal(ks[7], (DIM, N_SHARED * INTER), dtype=jnp.float32) * STD}
    _L0_ffn_in = _L0_ffn_setup()
    _L0_c = _w((lambda *s: np.random.randn(*s).astype(np.float32) * 0.05)(4, 512))
    _L0_wmod = _w((lambda *s: np.random.randn(*s).astype(np.float32) * 0.05)(512, 6 * 512) * 512 ** (-0.5))
    _d = {'L0_attn_x': _L0_attn_in['x'], 'L0_attn_w_qkv': _L0_attn_in['w_qkv'], 'L0_attn_w_proj': _L0_attn_in['w_proj'], 'L0_attn_b_proj': _L0_attn_in['b_proj'], 'L0_ffn_gate_w': _L0_ffn_in['gate_w'], 'L0_ffn_router_bias': _L0_ffn_in['router_bias'], 'L0_ffn_W1': _L0_ffn_in['W1'], 'L0_ffn_W3': _L0_ffn_in['W3'], 'L0_ffn_W2': _L0_ffn_in['W2'], 'L0_ffn_sw1': _L0_ffn_in['sw1'], 'L0_ffn_sw3': _L0_ffn_in['sw3'], 'L0_ffn_sw2': _L0_ffn_in['sw2'], 'L0_c': _L0_c, 'L0_wmod': _L0_wmod}
    _x0 = _d['L0_attn_x']
    _d['L0_attn_x'] = jax.random.normal(jax.random.fold_in(jax.random.key(seed), 1), (4, 1024, 512), dtype=_x0.dtype)
    del _x0
    return _d

def reference(L0_attn_x, L0_attn_w_qkv, L0_attn_w_proj, L0_attn_b_proj, L0_ffn_gate_w, L0_ffn_router_bias, L0_ffn_W1, L0_ffn_W3, L0_ffn_W2, L0_ffn_sw1, L0_ffn_sw3, L0_ffn_sw2, L0_c, L0_wmod):

    def _L0_attn_ref(x, w_qkv, w_proj, b_proj):
        import jax, jax.numpy as jnp
        import numpy as np
        EPS = 1e-15
        HEAD_DIM = 32
        PAD_VAL = 1.0
        B, N, C = x.shape
        d = HEAD_DIM
        h = C // d
        qkv = (x @ w_qkv.T).reshape(B, N, 3, C)
        q, k, v = (qkv[:, :, 0], qkv[:, :, 1], qkv[:, :, 2])

        def to_heads(t):
            return t.reshape(B, N, h, d).transpose(0, 2, 3, 1)
        q = jax.nn.relu(to_heads(q))
        k = jax.nn.relu(to_heads(k))
        v = to_heads(v)
        v_pad = jnp.pad(v, ((0, 0), (0, 0), (0, 1), (0, 0)), constant_values=PAD_VAL)
        vk = jnp.einsum('bhen,bhdn->bhed', v_pad, k)
        out = jnp.einsum('bhed,bhdn->bhen', vk, q)
        out = out[:, :, :-1] / (out[:, :, -1:] + EPS)
        out = out.reshape(B, C, N).transpose(0, 2, 1)
        return out @ w_proj.T + b_proj

    def _L0_ffn_ref(x, gate_w, router_bias, W1, W3, W2, sw1, sw3, sw2):
        import jax, jax.numpy as jnp
        import numpy as np
        E = 8
        K = 2
        DIM = 512
        INTER = 352
        N_SHARED = 2
        STD = 0.02
        B, S, D = x.shape
        X = x.reshape(-1, D)
        T = X.shape[0]
        logits = jnp.einsum('td,ed->te', X, gate_w)
        scores = jax.nn.sigmoid(logits)
        sel = scores + router_bias[None, :]
        _, idx = jax.lax.top_k(sel, K)
        w = jnp.take_along_axis(scores, idx, axis=1)
        w = w / jnp.clip(jnp.sum(w, axis=-1, keepdims=True), 1e-12)
        gate_full = jnp.zeros((T, E), dtype=w.dtype).at[jnp.arange(T)[:, None], idx].set(w)
        h1 = jnp.einsum('td,edh->eth', X, W1)
        h3 = jnp.einsum('td,edh->eth', X, W3)
        y = jnp.einsum('eth,ehd->etd', jax.nn.silu(h1) * h3, W2)
        out = jnp.einsum('etd,te->td', y, gate_full)
        shared = jnp.einsum('th,dh->td', jax.nn.silu(jnp.einsum('td,hd->th', X, sw1)) * jnp.einsum('td,hd->th', X, sw3), sw2)
        out = out + shared
        return out.reshape(B, S, D)
    x = L0_attn_x
    mod = (_silu(L0_c) @ L0_wmod).reshape(L0_c.shape[0], 6, 1, -1)
    sa, ca, ga, sb, cb, gb = (mod[:, 0], mod[:, 1], mod[:, 2], mod[:, 3], mod[:, 4], mod[:, 5])
    ga = (2 * (ga >= 0) - 1) * jnp.maximum(jnp.abs(ga), 0.25)
    gb = (2 * (gb >= 0) - 1) * jnp.maximum(jnp.abs(gb), 0.25)
    h = _layernorm(x, axis=-1) * (1 + ca) + sa
    x = x + ga * _L0_attn_ref(h, L0_attn_w_qkv, L0_attn_w_proj, L0_attn_b_proj)
    h = _layernorm(x, axis=-1) * (1 + cb) + sb
    x = x + gb * _L0_ffn_ref(h, L0_ffn_gate_w, L0_ffn_router_bias, L0_ffn_W1, L0_ffn_W3, L0_ffn_W2, L0_ffn_sw1, L0_ffn_sw3, L0_ffn_sw2)
    return x

_drawn_inputs = setup_inputs


def setup_inputs(seed=0):
    import zlib

    import numpy as np

    out = dict(_drawn_inputs(seed))
    spreads = {'L0_ffn_router_bias': (0.0, 0.8)}
    factors = {'L0_attn_w_qkv': 5.444,
     'L0_attn_w_proj': 5.11,
     'L0_attn_b_proj': 8.0,
     'L0_ffn_gate_w': 8.0,
     'L0_ffn_W1': 7.974,
     'L0_ffn_W3': 7.808,
     'L0_ffn_W2': 7.806,
     'L0_ffn_sw1': 4.003,
     'L0_ffn_sw3': 3.918,
     'L0_ffn_sw2': 3.91,
     'L0_c': 2.848,
     'L0_wmod': 2.84}
    for name, (base, spread) in spreads.items():
        noise = np.random.default_rng([zlib.crc32(name.encode()), seed]).standard_normal(out[name].shape)
        drawn = base * np.exp(spread * noise) if base else spread * noise
        out[name] = jnp.asarray(drawn.astype(out[name].dtype))
    for name, factor in factors.items():
        out[name] = (out[name] * factor).astype(out[name].dtype)
    return out
```

```python
from contextlib import ExitStack

import concourse.bass as bass
from concourse import mybir

F32 = mybir.dt.float32
F16 = mybir.dt.float16
I32 = mybir.dt.int32
U32 = mybir.dt.uint32
ALU = mybir.AluOpType
ACT = mybir.ActivationFunctionType
AX = mybir.AxisListType

P = 128
B, N, C = 4, 1024, 512
HEAD = 32
T = B * N
TILES = T // P
BT = N // P
KC = C // P
E, TOP = 8, 2
INTER = 352
SHARED = 704
SH_TILES = 6
SH_HALF = SHARED - 5 * P
SLOT_TILES = (T * TOP + E * (P - 1)) // P
SLOTS = SLOT_TILES * P
SCALE = 64.0
VK_SCALE = 1.0 / 64.0
GRP = 4
VKW = P + 4
LN_EPS, DEN_EPS, SUM_EPS = 1e-5, 1e-15, 1e-12
SA, CA = range(2)
GA, GAB, SB, CB = range(4)
PIECE = (KC * 2 * SHARED + SH_TILES * C) // TILES


class Parts:
    pass


def split_matmul(nc, out, lhs, rhs, first, last):
    (lh, ll), (rh, rl) = lhs, rhs
    nc.tensor.matmul(out, lh, rh, start=first, stop=False, skip_group_check=True)
    nc.tensor.matmul(out, lh, rl, start=False, stop=False, skip_group_check=True)
    return nc.tensor.matmul(out, ll, rh, start=False, stop=last, skip_group_check=True)


def setup(nc, m):
    with ExitStack() as ctx:
        sb = lambda name, shape, dt: ctx.enter_context(nc.sbuf_tensor(name, shape, dt))
        ct = sb("ct", [P, KC, B], F32)
        sct = sb("sct", [P, KC, B], F32)
        wmod = m.qt_flat[:, 0:KC * 6 * C * 2].bitcast(F32).rearrange("p (k n) -> p k n", k=KC)
        stage = sb("stage", [P, 2, 3 * C], F32)
        mod = sb("mod", [B, 6 * C], F32)
        gate_tmp = sb("gate_tmp", [B, 2 * C], F32)
        bproj = sb("bproj", [B, C], F32)
        gstage = sb("gstage", [P, KC, E], F32)
        zero = sb("zero", [P, SLOT_TILES], I32)
        ps = [ctx.enter_context(nc.psum_tensor(f"ps_mod{j}", [B, C], F32)) for j in range(6)]
        sem = m.sem
        c_loaded, silu_done = sem("c_loaded"), sem("silu_done")
        wmod_loaded = [sem(f"wmod_loaded{k}") for k in range(KC)]
        stage_loaded = [sem(f"stage_loaded{k}") for k in range(2)]
        stage_hi, stage_lo = sem("stage_hi"), sem("stage_lo")
        small_loaded, mod_done, mod_step = sem("small_loaded"), sem("mod_done"), sem("mod_step")
        mod_ready, mod_stored = sem("mod_ready"), sem("mod_stored")
        rows_loaded, zeroed, table_cleared = sem("rows_loaded"), sem("zeroed"), sem("table_cleared")
        const_step = sem("const_step")
        pieces = [(m.wqkv_t[k * P:(k + 1) * P, :], m.wqkv[:, k, :, :], 3 * C) for k in range(KC)]
        pieces += [(m.wproj_t[k * P:(k + 1) * P, :], m.wproj[:, k, :, :], C) for k in range(KC)]

        with nc.Block() as block:
            @block.sync
            def _(sp):
                sp.dma_start(ct[:, :, :], m.c_t.rearrange("(k p) b -> p k b", p=P)).then_inc(c_loaded, 16)
                for k in range(KC):
                    sp.dma_start(wmod[:, k, :], m.wmod_d[k * P:(k + 1) * P, :]).then_inc(wmod_loaded[k], 16)
                sp.dma_start(bproj[:, :], m.b_proj.partition_broadcast(B)).then_inc(small_loaded, 16)
                sp.dma_start(gstage[:, :, :], m.gate_t.rearrange("(k p) e -> p k e", p=P)).then_inc(small_loaded, 16)
                for n, (src, _, w) in enumerate(pieces):
                    if n >= 2:
                        sp.wait_ge(stage_hi, n - 1)
                        sp.wait_ge(stage_lo, n - 1)
                    sp.dma_start(stage[:, n % 2, 0:w], src).then_inc(stage_loaded[n % 2], 16)
                sp.wait_ge(mod_ready, 1)
                sp.dma_start(m.mod_d, mod[:, :]).then_inc(mod_stored, 16)
                sp.dma_start(m.gab_d, gate_tmp[:, 0:C]).then_inc(mod_stored, 16)
                sp.wait_ge(zeroed, 1)
                sp.dma_start(m.table.rearrange("(p t) o -> p (t o)", p=P), zero[:, :]).then_inc(table_cleared, 16)
                sp.wait_ge(mod_stored, 32)
                for b in range(B):
                    for r, src in ((SA, m.mod_d[b, 0:C]), (CA, m.mod_d[b, C:2 * C])):
                        sp.dma_start(m.rows[:, b, r, :], src.partition_broadcast(P)).then_inc(rows_loaded, 16)
                sp.wait_ge(rows_loaded, 16 * 2 * B)
                sp.wait_ge(table_cleared, 16)

            @block.scalar
            def _(act):
                act.wait_ge(c_loaded, 16)
                act.activation(sct[:, :, :], ct[:, :, :], ACT.Silu).then_inc(silu_done, 1)
                for n, (_, dst, w) in enumerate(pieces):
                    act.wait_ge(stage_loaded[n % 2], 16 * (n // 2 + 1))
                    act.activation(dst[:, 0, :], stage[:, n % 2, 0:w], ACT.Copy, scale=SCALE).then_inc(stage_hi, 1)
                act.wait_ge(small_loaded, 32)
                act.activation(m.gate[:, :, 0, :], gstage[:, :, :], ACT.Copy, scale=SCALE).then_inc(stage_hi, 1)

            @block.vector
            def _(v):
                for n, (_, dst, w) in enumerate(pieces):
                    v.wait_ge(stage_hi, n + 1)
                    v.scalar_tensor_tensor(out=dst[:, 1, :], in0=stage[:, n % 2, 0:w], scalar=SCALE, in1=dst[:, 0, :],
                                           op0=ALU.mult, op1=ALU.subtract).then_inc(stage_lo, 1)
                v.wait_ge(stage_hi, len(pieces) + 1)
                v.scalar_tensor_tensor(out=m.gate[:, :, 1, :], in0=gstage[:, :, :], scalar=SCALE, in1=m.gate[:, :, 0, :],
                                       op0=ALU.mult, op1=ALU.subtract).then_inc(stage_lo, 1)
                v.wait_ge(mod_done, 6)
                steps = 0

                def step(instruction):
                    nonlocal steps
                    steps += 1
                    instruction.then_inc(mod_step, 1)
                    v.wait_ge(mod_step, steps)

                for j in range(6):
                    if j in (1, 4):
                        step(v.tensor_scalar(mod[:, j * C:(j + 1) * C], ps[j][:, :], 1.0, None, ALU.add))
                    elif j in (0, 3):
                        step(v.tensor_copy(mod[:, j * C:(j + 1) * C], ps[j][:, :]))
                    else:
                        mag, sgn = gate_tmp[:, 0:C], gate_tmp[:, C:2 * C]
                        step(v.tensor_scalar(mag, ps[j][:, :], -1.0, None, ALU.mult))
                        step(v.tensor_tensor(mag, ps[j][:, :], mag, ALU.max))
                        step(v.tensor_scalar(mag, mag, 0.25, None, ALU.max))
                        step(v.tensor_scalar(sgn, ps[j][:, :], 0.0, 2.0, ALU.is_ge, ALU.mult))
                        step(v.tensor_scalar(sgn, sgn, -1.0, None, ALU.add))
                        step(v.tensor_tensor(mod[:, j * C:(j + 1) * C], mag, sgn, ALU.mult))
                v.wait_ge(small_loaded, 32)
                v.tensor_tensor(gate_tmp[:, 0:C], mod[:, 2 * C:3 * C], bproj[:, :], ALU.mult).then_inc(mod_ready, 1)

            @block.tensor
            def _(pe):
                pe.wait_ge(silu_done, 1)
                for k in range(KC):
                    pe.wait_ge(wmod_loaded[k], 16)
                    for j in range(6):
                        mm = nc.tensor.matmul(ps[j][:, :], sct[:, k, :], wmod[:, k, j * C:(j + 1) * C],
                                              start=k == 0, stop=k == KC - 1)
                        if k == KC - 1:
                            mm.then_inc(mod_done, 1)

            @block.gpsimd
            def _(pool):
                steps = 0

                def step(instruction):
                    nonlocal steps
                    steps += 1
                    instruction.then_inc(const_step, 1)
                    pool.wait_ge(const_step, steps)

                pool.memset(zero[:, :], 0).then_inc(zeroed, 1)
                step(pool.memset(m.ident[:, :], 0.0))
                step(pool.affine_select(out=m.ident[:, :], in_=m.ident[:, :], compare_op=ALU.not_equal, fill=1.0,
                                        base=0, pattern=[[-1, P]], channel_multiplier=1))
                step(pool.memset(m.heads[:, :], VK_SCALE))
                step(pool.affine_select(out=m.heads[:, :], in_=m.heads[:, :], compare_op=ALU.is_ge, fill=0.0,
                                        base=0, pattern=[[-HEAD, 4]], channel_multiplier=1))
                step(pool.affine_select(out=m.heads[:, :], in_=m.heads[:, :], compare_op=ALU.is_ge, fill=0.0,
                                        base=HEAD - 1, pattern=[[HEAD, 4]], channel_multiplier=-1))
                step(pool.tensor_copy(m.head_mask[:, :].rearrange("p (h e) -> p h e", h=4),
                                      m.heads[:, :].unsqueeze(2).to_broadcast([P, 4, HEAD])))
                step(pool.memset(m.minus_half[:, :], -0.5))
                step(pool.memset(m.spare[:, :], 0.0))
                step(pool.memset(m.v_sb[:, :, :, P:P + 1], 1.0))


def front(nc, m):
    with ExitStack() as ctx:
        sb = lambda name, shape, dt: ctx.enter_context(nc.sbuf_tensor(name, shape, dt))
        pb = lambda name, shape: ctx.enter_context(nc.psum_tensor(name, shape, F32))
        sem = m.sem
        xb = sb("xb", [P, 4, C], F32)
        st = sb("st", [P, 4, 6], F32)
        mv = sb("mv", [P, 4, 2], F32)
        rstd = sb("rstd", [P, 4, 1], F32)
        centred = sb("centred", [P, C], F32)
        spare = sb("spare_f", [P, 1], F32)
        h = sb("h", [P, 2, C], F32)
        ht = sb("ht", [P, 2, 2, KC, P], F16)
        k_sb = sb("k_sb", [P, 2, C], F32)
        vk_tmp = sb("vk_tmp", [P, GRP, VKW], F32)
        ps_t, ps_k, ps_v, ps_q = pb("ps_t", [P, KC, P]), pb("ps_k", [P, C]), pb("ps_v", [P, C]), pb("ps_q", [P, GRP, P])
        ps_vk = [pb(f"ps_vk{j}", [P, 2, P + 1]) for j in range(2)]
        sstage = sb("sstage", [P, 2, PIECE], F32)
        x_loaded = [sem(f"x_loaded{j}") for j in range(4)]
        s_loaded = [sem(f"s_loaded{j}") for j in range(2)]
        s_hi, s_lo = sem("s_hi"), sem("s_lo")
        bn_done, stats_ready, eps_added, rstd_ready = sem("bn_done"), sem("stats_ready"), sem("eps_added"), sem("rstd_ready")
        centred_ready, h_ready, t_done, ht_hi, ht_ready = sem("centred_ready"), sem("h_ready"), sem("t_done"), sem("ht_hi"), sem("ht_ready")
        k_done, v_done, q_done = sem("k_done"), sem("v_done"), sem("q_done")
        k_ready, v_ready, q_hi, q_ready = sem("k_ready"), sem("v_ready"), sem("q_hi"), sem("q_ready")
        vk_done, vk_step, vk_hi, vk_ready = sem("vk_done"), sem("vk_step"), sem("vk_hi"), sem("vk_ready")

        def there(b, c):
            return not isinstance(b, int) or 8 * b + c < TILES

        def over_batches(eng, slot):
            with eng.Fori(0, B - 1) as b:
                for c in range(1, BT + 1):
                    slot(b, c)
            for c in range(1, BT + 1):
                slot(B - 1, c)

        with nc.Block() as block:
            @block.sync
            def _(sp):
                def load(b, c):
                    if not there(b, c):
                        return
                    i = 8 * b + c
                    if not (isinstance(b, int) and i < 4):
                        sp.wait_ge(centred_ready, i - 3)
                    sp.dma_start(xb[:, c % 4, :], m.x[bass.ds(i * P, P), :]).then_inc(x_loaded[c % 4], 16)

                def load_piece(b, c):
                    if not there(b, c):
                        return
                    i = 8 * b + c
                    if not (isinstance(b, int) and i < 2):
                        sp.wait_ge(s_lo, i - 1)
                    sp.dma_start(sstage[:, c % 2, :], m.sh_flat[:, bass.ds(i * PIECE, PIECE)]).then_inc(s_loaded[c % 2], 16)

                def slot(b, c):
                    load(b, c + 3)
                    load_piece(b, c)

                for c in range(4):
                    load(0, c)
                load_piece(0, 0)
                over_batches(sp, slot)

            @block.gpsimd
            def _(pool):
                def reciprocal_deviation(b, c):
                    if not there(b, c):
                        return
                    i = 8 * b + c
                    pool.wait_ge(eps_added, i + 1)
                    pool.tensor_tensor(rstd[:, c % 4, :], rstd[:, c % 4, :], m.minus_half[:, :], ALU.pow).then_inc(rstd_ready, 1)

                for c in range(4):
                    reciprocal_deviation(0, c)
                over_batches(pool, lambda b, c: reciprocal_deviation(b, c + 3))

            @block.vector
            def _(v):
                def stats(b, c):
                    if not there(b, c):
                        return
                    i = 8 * b + c
                    v.wait_ge(x_loaded[c % 4], 16 * ((c // 4) + 1 + 2 * b))
                    if not (isinstance(b, int) and i < 4):
                        v.wait_ge(h_ready, i - 3)
                    v.bn_stats(st[:, c % 4, :], xb[:, c % 4, :]).then_inc(bn_done, 1)
                    v.wait_ge(bn_done, i + 1)
                    v.memset(spare[:, :], 0.0)
                    v.bn_aggr(mv[:, c % 4, :], st[:, c % 4, :]).then_inc(stats_ready, 1)
                    v.wait_ge(stats_ready, i + 1)
                    v.tensor_scalar(rstd[:, c % 4, :], mv[:, c % 4, 1:2], LN_EPS, None, ALU.add).then_inc(eps_added, 1)

                def normalise(b, c):
                    if not there(b, c):
                        return
                    i = 8 * b + c
                    batch = b + c // BT
                    v.wait_ge(stats_ready, i + 1)
                    if not (isinstance(b, int) and i < 1):
                        v.wait_ge(h_ready, i)
                    v.scalar_tensor_tensor(out=centred[:, :], in0=xb[:, c % 4, :], scalar=mv[:, c % 4, 0:1],
                                           in1=m.rows[:, batch, CA, :], op0=ALU.subtract, op1=ALU.mult).then_inc(centred_ready, 1)
                    v.wait_ge(rstd_ready, i + 1)
                    v.wait_ge(centred_ready, i + 1)
                    if not (isinstance(b, int) and i < 2):
                        v.wait_ge(t_done, i - 1)
                    v.scalar_tensor_tensor(out=h[:, c % 2, :], in0=centred[:, :], scalar=rstd[:, c % 4, :],
                                           in1=m.rows[:, batch, SA, :], op0=ALU.mult, op1=ALU.add).then_inc(h_ready, 1)

                def low_part(b, c):
                    if not there(b, c):
                        return
                    v.wait_ge(ht_hi, 8 * b + c + 1)
                    v.tensor_tensor(ht[:, c % 2, 1, :, :], ps_t[:, :, :], ht[:, c % 2, 0, :, :], ALU.subtract).then_inc(ht_ready, 1)

                def values(b, c):
                    if not there(b, c):
                        return
                    i = 8 * b + c
                    v.wait_ge(v_done, i + 1)
                    if not (isinstance(b, int) and i < 2):
                        v.wait_ge(vk_done, i - 1)
                    v.tensor_scalar(m.v_sb[:, c % 2, :, 0:P], ps_v[:, :].rearrange("p (g n) -> p g n", g=GRP),
                                    1.0 / SCALE, None, ALU.mult).then_inc(v_ready, 1)
                    v.wait_ge(q_hi, i + 1)
                    v.scalar_tensor_tensor(out=m.qt[:, i, 1, :, :], in0=ps_q[:, :, :], scalar=0.0, in1=m.qt[:, i, 0, :, :],
                                           op0=ALU.max, op1=ALU.subtract).then_inc(q_ready, 1)

                def key_value_sums(b):
                    v.wait_ge(vk_done, 8 * b + 8)
                    if not (isinstance(b, int) and b == 0):
                        v.wait_ge(vk_ready, 1 * b)
                    for g in range(GRP):
                        v.tensor_tensor(vk_tmp[:, g, 0:P], ps_vk[g // 2][:, g % 2, 0:P], m.head_mask[:, :], ALU.mult).then_inc(vk_step, 1)
                        v.tensor_scalar(vk_tmp[:, g, P:VKW], m.heads[:, :], ps_vk[g // 2][:, g % 2, P:P + 1], None, ALU.mult).then_inc(vk_step, 1)
                    v.wait_ge(vk_step, 8 * b + 8)
                    v.tensor_copy(m.vk[:, b, 0, :, :], vk_tmp[:, :, :]).then_inc(vk_hi, 1)
                    v.wait_ge(vk_hi, b + 1)
                    v.tensor_tensor(m.vk[:, b, 1, :, :], vk_tmp[:, :, :], m.vk[:, b, 0, :, :], ALU.subtract).then_inc(vk_ready, 1)

                def piece_low(b, c):
                    if not there(b, c):
                        return
                    i = 8 * b + c
                    v.wait_ge(s_hi, i + 1)
                    v.scalar_tensor_tensor(out=m.sh[:, 1, bass.ds(i * PIECE, PIECE)], in0=sstage[:, c % 2, :], scalar=SCALE,
                                           in1=m.sh[:, 0, bass.ds(i * PIECE, PIECE)], op0=ALU.mult, op1=ALU.subtract).then_inc(s_lo, 1)

                def slot(b, c):
                    stats(b, c + 3)
                    normalise(b, c + 2)
                    low_part(b, c + 1)
                    values(b, c)
                    piece_low(b, c)
                    if c == BT:
                        key_value_sums(b)

                stats(0, 0)
                stats(0, 1)
                stats(0, 2)
                normalise(0, 0)
                normalise(0, 1)
                low_part(0, 0)
                slot(0, 0)
                over_batches(v, slot)

            @block.scalar
            def _(act):
                def high_part(b, c):
                    if not there(b, c):
                        return
                    i = 8 * b + c
                    act.wait_ge(t_done, i + 1)
                    if not (isinstance(b, int) and i < 2):
                        act.wait_ge(q_done, i - 1)
                    act.activation(ht[:, c % 2, 0, :, :], ps_t[:, :, :], ACT.Copy).then_inc(ht_hi, 1)

                def slot(b, c):
                    high_part(b, c + 1)
                    if not there(b, c):
                        return
                    i = 8 * b + c
                    act.wait_ge(k_done, i + 1)
                    if not (isinstance(b, int) and i < 2):
                        act.wait_ge(vk_done, i - 1)
                    act.activation(k_sb[:, c % 2, :], ps_k[:, :], ACT.Relu, scale=1.0 / SCALE).then_inc(k_ready, 1)
                    act.wait_ge(q_done, i + 1)
                    act.activation(m.qt[:, i, 0, :, :], ps_q[:, :, :], ACT.Relu).then_inc(q_hi, 1)
                    act.wait_ge(s_loaded[c % 2], 16 * ((c // 2) + 1 + 4 * b))
                    act.activation(m.sh[:, 0, bass.ds(i * PIECE, PIECE)], sstage[:, c % 2, :], ACT.Copy, scale=SCALE).then_inc(s_hi, 1)

                high_part(0, 0)
                slot(0, 0)
                over_batches(act, slot)

            @block.tensor
            def _(pe):
                def transposes(b, c):
                    if not there(b, c):
                        return
                    i = 8 * b + c
                    pe.wait_ge(h_ready, i + 1)
                    if not (isinstance(b, int) and i < 1):
                        pe.wait_ge(ht_ready, i)
                    for k in range(KC):
                        mm = nc.tensor.transpose(ps_t[:, k, :], h[:, c % 2, k * P:(k + 1) * P], m.ident[:, :])
                    mm.then_inc(t_done, 1)

                def project(b, c):
                    if not there(b, c):
                        return
                    i = 8 * b + c
                    first = isinstance(b, int) and i == 0
                    hk = [(ht[:, c % 2, 0, k, :], ht[:, c % 2, 1, k, :]) for k in range(KC)]
                    w = lambda k, lo, n: (m.wqkv[:, k, 0, lo:lo + n], m.wqkv[:, k, 1, lo:lo + n])
                    pe.wait_ge(ht_ready, i + 1)
                    if not first:
                        pe.wait_ge(k_ready, i)
                    for k in range(KC):
                        mm = split_matmul(nc, ps_k[:, :], hk[k], w(k, C, C), k == 0, k == KC - 1)
                    mm.then_inc(k_done, 1)
                    if not first:
                        pe.wait_ge(v_ready, i)
                    for k in range(KC):
                        mm = split_matmul(nc, ps_v[:, :], hk[k], w(k, 2 * C, C), k == 0, k == KC - 1)
                    mm.then_inc(v_done, 1)
                    if not first:
                        pe.wait_ge(q_ready, i)
                    for g in range(GRP):
                        for k in range(KC):
                            mm = split_matmul(nc, ps_q[:, g, :], w(k, g * P, P), hk[k], k == 0, k == KC - 1)
                    mm.then_inc(q_done, 1)

                def sum_keys_values(b, c):
                    i = 8 * b + c
                    pe.wait_ge(k_ready, i + 1)
                    pe.wait_ge(v_ready, i + 1)
                    if c == 0 and not (isinstance(b, int) and b == 0):
                        pe.wait_ge(vk_ready, b)
                    for g in range(GRP):
                        mm = nc.tensor.matmul(ps_vk[g // 2][:, g % 2, :], k_sb[:, c % 2, g * P:(g + 1) * P],
                                              m.v_sb[:, c % 2, g, 0:P + 1], start=c == 0 and g % 2 == 0,
                                              stop=c == BT - 1, skip_group_check=True)
                    mm.then_inc(vk_done, 1)

                def slot(b, c):
                    transposes(b, c + 1)
                    project(b, c)
                    if c >= 1:
                        sum_keys_values(b, c - 1)

                transposes(0, 0)
                slot(0, 0)
                over_batches(pe, slot)


def back(nc, m):
    with ExitStack() as ctx:
        sb = lambda name, shape, dt: ctx.enter_context(nc.sbuf_tensor(name, shape, dt))
        pb = lambda name, shape: ctx.enter_context(nc.psum_tensor(name, shape, F32))
        sem = m.sem
        R = 4
        xr = sb("xr", [P, 2, C], F32)
        xg = sb("xg", [P, 2, C], F32)
        den = sb("den", [P, 4 * GRP], F32)
        o_sb = sb("o_sb", [P, 2, C], F32)
        ot = sb("ot", [P, 2, 2, KC, P], F16)
        x2 = sb("x2", [P, 2, C], F32)
        t1 = sb("t1", [P, C], F32)
        st = sb("st_b", [P, 2, 6], F32)
        mv = sb("mv_b", [P, 2, 2], F32)
        rstd = sb("rstd_b", [P, 2, 1], F32)
        centred = sb("centred_b", [P, C], F32)
        spare = sb("spare_b", [P, 1], F32)
        h2 = sb("h2", [P, 2, C], F32)
        h2t = sb("h2t", [P, 2, 2, KC, P], F16)
        ps_o = [pb(f"ps_o{j}", [P, 2, VKW]) for j in range(2)]
        ps_ot, ps_y, ps_ht, ps_l = pb("ps_ot", [P, KC, P]), pb("ps_y", [P, C]), pb("ps_ht", [P, KC, P]), pb("ps_l", [P, E])
        m.rows = sb("rows_b", [P, B, 4, C], F32)
        rows_b0, rows_b = sem("rows_b0"), sem("rows_b")
        xr_loaded = [sem(f"xr_loaded{j}") for j in range(2)]
        xg_ready, o_done, den_ready, rden_ready, o_ready = sem("xg_ready"), sem("o_done"), sem("den_ready"), sem("rden_ready"), sem("o_ready")
        ot_done, ot_hi, ot_ready, y_done, t1_ready, x2_ready = sem("ot_done"), sem("ot_hi"), sem("ot_ready"), sem("y_done"), sem("t1_ready"), sem("x2_ready")
        bn2_done, stats2_ready, eps2_added, rstd2_ready = sem("bn2_done"), sem("stats2_ready"), sem("eps2_added"), sem("rstd2_ready")
        centred2_ready, h2_ready, h2t_done, h2t_hi, h2t_ready = sem("centred2_ready"), sem("h2_ready"), sem("h2t_done"), sem("h2t_hi"), sem("h2t_ready")
        l_done, l_ready = sem("l_done"), sem("l_ready")
        x2_stored = [sem(f"x2_stored{j}") for j in range(2)]
        h2_stored = [sem(f"h2_stored{j}") for j in range(2)]
        h2t_stored = [sem(f"h2t_stored{j}") for j in range(2)]
        LAST = 5

        def there(t):
            return not isinstance(t, int) or 0 <= t < TILES

        def later(t, n):
            return not isinstance(t, int) or t >= n

        def over_tiles(eng, slot, rows=False):
            if rows:
                eng.wait_ge(rows_b0, 16 * 4)
            for i in range(LAST + 1):
                slot(i, i)
            if rows:
                eng.wait_ge(rows_b, 16 * 4 * (B - 1))
            with eng.Fori(0, (TILES - LAST - 1) // 2) as pair:
                for c in range(2):
                    slot(2 * pair + (LAST + 1 + c), LAST + 1 + c)
            for i in range(TILES, TILES + LAST):
                slot(i, i)

        def uses(t, c):
            return 16 * (t // 2 + 1)

        with nc.Block() as block:
            @block.sync
            def _(sp):
                for b in range(B):
                    for r, src in ((GA, m.mod_d[b, 2 * C:3 * C]), (GAB, m.gab_d[b, :]), (SB, m.mod_d[b, 3 * C:4 * C]),
                                   (CB, m.mod_d[b, 4 * C:5 * C])):
                        sp.dma_start(m.rows[:, b, r, :], src.partition_broadcast(P)).then_inc(rows_b if b else rows_b0, 16)

                def slot(t, c):
                    if there(t):
                        if later(t, 2):
                            sp.wait_ge(xg_ready, t - 1)
                        sp.dma_start(xr[:, c % 2, :], m.x[bass.ds(t * P, P), :]).then_inc(xr_loaded[c % 2], 16)
                    u, d = t - 2, c - 2
                    if there(u):
                        sp.wait_ge(x2_ready, u + 1)
                        sp.dma_start(m.x2_d[bass.ds(u * P, P), :], x2[:, d % 2, :]).then_inc(x2_stored[d % 2], 16)
                    u, d = t - 3, c - 3
                    if there(u):
                        sp.wait_ge(h2_ready, u + 1)
                        sp.dma_start(m.h2_d[bass.ds(u * P, P), :], h2[:, d % 2, :]).then_inc(h2_stored[d % 2], 16)
                    u, d = t - 4, c - 4
                    if there(u):
                        sp.wait_ge(h2t_ready, u + 1)
                        sp.dma_start(m.h2t_d[bass.ds(u, 1), :, :].rearrange("o p n -> (o p) n"),
                                     h2t[:, d % 2, :, :, :].rearrange("p s k n -> p (s k n)")).then_inc(h2t_stored[d % 2], 16)

                over_tiles(sp, slot)
                for s in x2_stored + h2_stored + h2t_stored:
                    sp.wait_ge(s, 16 * TILES // 2)

            @block.gpsimd
            def _(pool):
                def slot(t, c):
                    if there(t):
                        pool.wait_ge(xr_loaded[c % 2], uses(t, c))
                        if later(t, 2):
                            pool.wait_ge(x2_ready, t - 1)
                        pool.tensor_tensor(xg[:, c % 2, :], xr[:, c % 2, :], m.rows[:, t // BT, GAB, :], ALU.add).then_inc(xg_ready, 1)
                    u, d = t - 2, c - 2
                    if there(u):
                        pool.wait_ge(eps2_added, u + 1)
                        pool.tensor_tensor(rstd[:, d % 2, :], rstd[:, d % 2, :], m.minus_half[:, :], ALU.pow).then_inc(rstd2_ready, 1)

                over_tiles(pool, slot, rows=True)

            @block.vector
            def _(v):
                def divide(t, c):
                    v.wait_ge(o_done, t + 1)
                    if later(t, 1):
                        v.wait_ge(o_ready, 2 * t)
                    for j in range(2):
                        v.tensor_scalar(den[:, 8 * j:8 * j + 8].rearrange("p (g h) -> p g h", g=2), ps_o[j][:, :, P:VKW],
                                        DEN_EPS, None, ALU.add).then_inc(den_ready, 1)
                    v.wait_ge(den_ready, 2 * t + 2)
                    v.reciprocal(den[:, :], den[:, :]).then_inc(rden_ready, 1)
                    v.wait_ge(rden_ready, t + 1)
                    if later(t, 2):
                        v.wait_ge(ot_done, t - 1)
                    for j in range(2):
                        for g in range(2):
                            lo = (2 * j + g) * P
                            inst = v.tensor_tensor(o_sb[:, c % 2, lo:lo + P].rearrange("p (h e) -> p h e", h=4),
                                                   ps_o[j][:, g, 0:P].rearrange("p (h e) -> p h e", h=4),
                                                   den[:, 8 * j + 4 * g:8 * j + 4 * g + 4].unsqueeze(2).to_broadcast([P, 4, HEAD]),
                                                   ALU.mult)
                        inst.then_inc(o_ready, 1)

                def slot(t, c):
                    if there(t):
                        divide(t, c)
                    u, d = t - 1, c - 1
                    if there(u):
                        v.wait_ge(ot_hi, u + 1)
                        v.tensor_tensor(ot[:, d % 2, 1, :, :], ps_ot[:, :, :], ot[:, d % 2, 0, :, :], ALU.subtract).then_inc(ot_ready, 1)
                    u, d = t - 4, c - 4
                    if there(u):
                        v.wait_ge(h2t_hi, u + 1)
                        v.tensor_tensor(h2t[:, d % 2, 1, :, :], ps_ht[:, :, :], h2t[:, d % 2, 0, :, :], ALU.subtract).then_inc(h2t_ready, 1)
                    u, d = t - 2, c - 2
                    if there(u):
                        v.wait_ge(y_done, u + 1)
                        if later(u, 1):
                            v.wait_ge(x2_ready, u)
                        v.scalar_tensor_tensor(out=t1[:, :], in0=ps_y[:, :], scalar=1.0 / SCALE, in1=m.rows[:, u // BT, GA, :],
                                               op0=ALU.mult, op1=ALU.mult).then_inc(t1_ready, 1)
                        v.wait_ge(t1_ready, u + 1)
                        v.wait_ge(xg_ready, u + 1)
                        if later(u, 2):
                            v.wait_ge(centred2_ready, u - 1)
                            v.wait_ge(x2_stored[d % 2], uses(u - 2, d))
                        v.tensor_tensor(x2[:, d % 2, :], t1[:, :], xg[:, d % 2, :], ALU.add).then_inc(x2_ready, 1)
                        v.wait_ge(x2_ready, u + 1)
                        v.bn_stats(st[:, d % 2, :], x2[:, d % 2, :]).then_inc(bn2_done, 1)
                        v.wait_ge(bn2_done, u + 1)
                        if later(u, 2):
                            v.wait_ge(h2_ready, u - 1)
                        v.memset(spare[:, :], 0.0)
                        v.bn_aggr(mv[:, d % 2, :], st[:, d % 2, :]).then_inc(stats2_ready, 1)
                        v.wait_ge(stats2_ready, u + 1)
                        v.tensor_scalar(rstd[:, d % 2, :], mv[:, d % 2, 1:2], LN_EPS, None, ALU.add).then_inc(eps2_added, 1)
                    u, d = t - 3, c - 3
                    if there(u):
                        if later(u, 1):
                            v.wait_ge(h2_ready, u)
                        v.wait_ge(stats2_ready, u + 1)
                        v.scalar_tensor_tensor(out=centred[:, :], in0=x2[:, d % 2, :], scalar=mv[:, d % 2, 0:1],
                                               in1=m.rows[:, u // BT, CB, :], op0=ALU.subtract, op1=ALU.mult).then_inc(centred2_ready, 1)
                        v.wait_ge(rstd2_ready, u + 1)
                        v.wait_ge(centred2_ready, u + 1)
                        if later(u, 2):
                            v.wait_ge(h2t_done, u - 1)
                            v.wait_ge(h2_stored[d % 2], uses(u - 2, d))
                        v.scalar_tensor_tensor(out=h2[:, d % 2, :], in0=centred[:, :], scalar=rstd[:, d % 2, :],
                                               in1=m.rows[:, u // BT, SB, :], op0=ALU.mult, op1=ALU.add).then_inc(h2_ready, 1)

                over_tiles(v, slot, rows=True)

            @block.scalar
            def _(act):
                def slot(t, c):
                    u, d = t - 1, c - 1
                    if there(u):
                        act.wait_ge(ot_done, u + 1)
                        if later(u, 2):
                            act.wait_ge(y_done, u - 1)
                        act.activation(ot[:, d % 2, 0, :, :], ps_ot[:, :, :], ACT.Copy).then_inc(ot_hi, 1)
                    u, d = t - 4, c - 4
                    if there(u):
                        act.wait_ge(h2t_done, u + 1)
                        if later(u, 2):
                            act.wait_ge(l_done, u - 1)
                            act.wait_ge(h2t_stored[d % 2], uses(u - 2, d))
                        act.activation(h2t[:, d % 2, 0, :, :], ps_ht[:, :, :], ACT.Copy).then_inc(h2t_hi, 1)
                    u, d = t - 5, c - 5
                    if there(u):
                        act.wait_ge(l_done, u + 1)
                        act.activation(m.logits[:, u, :], ps_l[:, :], ACT.Copy, scale=1.0 / SCALE).then_inc(l_ready, 1)

                over_tiles(act, slot)

            @block.tensor
            def _(pe):
                def slot(t, c):
                    if there(t):
                        if later(t, 1):
                            pe.wait_ge(o_ready, 2 * t)
                        for g in range(GRP):
                            mm = split_matmul(nc, ps_o[g // 2][:, g % 2, :], (m.qt[:, t, 0, g, :], m.qt[:, t, 1, g, :]),
                                              (m.vk[:, t // BT, 0, g, :], m.vk[:, t // BT, 1, g, :]), True, True)
                        mm.then_inc(o_done, 1)
                    u, d = t - 1, c - 1
                    if there(u):
                        pe.wait_ge(o_ready, 2 * u + 2)
                        if later(u, 1):
                            pe.wait_ge(ot_ready, u)
                        for k in range(KC):
                            mm = nc.tensor.transpose(ps_ot[:, k, :], o_sb[:, d % 2, k * P:(k + 1) * P], m.ident[:, :])
                        mm.then_inc(ot_done, 1)
                    u, d = t - 4, c - 4
                    if there(u):
                        pe.wait_ge(h2_ready, u + 1)
                        if later(u, 1):
                            pe.wait_ge(h2t_ready, u)
                        for k in range(KC):
                            mm = nc.tensor.transpose(ps_ht[:, k, :], h2[:, d % 2, k * P:(k + 1) * P], m.ident[:, :])
                        mm.then_inc(h2t_done, 1)
                    u, d = t - 2, c - 2
                    if there(u):
                        pe.wait_ge(ot_ready, u + 1)
                        if later(u, 1):
                            pe.wait_ge(t1_ready, u)
                        for k in range(KC):
                            mm = split_matmul(nc, ps_y[:, :], (ot[:, d % 2, 0, k, :], ot[:, d % 2, 1, k, :]),
                                              (m.wproj[:, k, 0, :], m.wproj[:, k, 1, :]), k == 0, k == KC - 1)
                        mm.then_inc(y_done, 1)
                    u, d = t - 5, c - 5
                    if there(u):
                        pe.wait_ge(h2t_ready, u + 1)
                        if later(u, 1):
                            pe.wait_ge(l_ready, u)
                        for k in range(KC):
                            mm = split_matmul(nc, ps_l[:, :], (h2t[:, d % 2, 0, k, :], h2t[:, d % 2, 1, k, :]),
                                              (m.gate[:, k, 0, :], m.gate[:, k, 1, :]), k == 0, k == KC - 1)
                        mm.then_inc(l_done, 1)

                over_tiles(pe, slot)


def carry_waits(pool, spare):
    pool.tensor_tensor(spare, spare, spare, ALU.add)


def shared_steps(nc, m, ctx, tag, first):
    sb = lambda name, shape, dt: ctx.enter_context(nc.sbuf_tensor(name + tag, shape, dt))
    sem = lambda name: m.sem(name + tag)
    CH = 2 * P
    s = Parts()
    ht = sb("s_ht", [P, 2, 2, 2, KC, P], F16)
    act_sb = sb("s_act", [P, 2, CH], F32)
    h3c = sb("s_h3c", [P, CH], F32)
    at = sb("s_at", [P, SH_TILES, 2, CH], F16)
    xs = sb("s_xs", [P, C], F32)
    t1 = sb("s_t1", [P, C], F32)
    ps_h = [ctx.enter_context(nc.psum_tensor(f"s_ps_h{j}{tag}", [P, 2, CH], F32)) for j in range(2)]
    ps_y = [ctx.enter_context(nc.psum_tensor(f"s_ps_y{j}{tag}", [P, C], F32)) for j in range(2)]
    ht_loaded = [sem(f"s_ht_loaded{j}") for j in range(2)]
    up_done, silu_done, h3c_done, act_done, at_hi, at_ready = sem("s_up_done"), sem("s_silu"), sem("s_h3c"), sem("s_act"), sem("s_at_hi"), sem("s_at_ready")
    y_done, t1_done, xs_loaded, xs_ready, s.xs_stored = sem("s_y_done"), sem("s_t1"), sem("s_xs_loaded"), sem("s_xs_ready"), sem("s_xs_stored")
    J = SH_TILES

    def is_first(n, j=0):
        return isinstance(n, int) and n == 0 and j == 0

    def load_h(sp, n, c):
        if not (isinstance(n, int) and n < 2):
            sp.wait_ge(up_done, J * (n - 1))
        for t in range(2):
            sp.dma_start(ht[:, c % 2, t, :, :, :].rearrange("p s k n -> p (s k n)"),
                         m.h2t_d[bass.ds(2 * (n + first) + t, 1), :, :].rearrange("o p n -> (o p) n")).then_inc(ht_loaded[c % 2], 16)

    def residual(sp, n, c):
        for t in range(2):
            rows = bass.ds((2 * (n + first) + t) * P, P)
            if not is_first(n, t):
                sp.wait_ge(s.xs_stored, 16 * (2 * n + t))
            sp.dma_start(xs[:, :], m.x2_d[rows, :]).then_inc(xs_loaded, 16)
            sp.wait_ge(xs_ready, 2 * n + t + 1)
            sp.dma_start(m.x2s_d[rows, :], xs[:, :]).then_inc(s.xs_stored, 16)

    def activate(act, n, c, j):
        i = J * n + j
        act.wait_ge(up_done, i + 1)
        if not (isinstance(n, int) and i < 2):
            act.wait_ge(at_ready, i - 1)
        if j < J - 1:
            act.activation(act_sb[:, j % 2, :], ps_h[j % 2][:, 0, :], ACT.Silu, scale=1.0 / SCALE).then_inc(silu_done, 1)
        else:
            if not is_first(n):
                act.wait_ge(act_done, J * n)
            act.activation(h3c[0:SH_HALF, :], ps_h[j % 2][SH_HALF:P, 0, :], ACT.Copy, scale=1.0 / SCALE).then_inc(h3c_done, 1)
            act.activation(act_sb[0:SH_HALF, j % 2, :], ps_h[j % 2][0:SH_HALF, 0, :], ACT.Silu, scale=1.0 / SCALE).then_inc(silu_done, 1)

    def high(act, n, c, j):
        i = J * n + j
        w = P if j < J - 1 else SH_HALF
        act.wait_ge(act_done, i + 1)
        if j == 0 and not is_first(n):
            act.wait_ge(y_done, 2 * n)
        act.activation(at[0:w, j, 0, :], act_sb[0:w, j % 2, :], ACT.Copy).then_inc(at_hi, 1)

    def multiply(v, n, c, j):
        i = J * n + j
        v.wait_ge(silu_done, i + 1)
        if j < J - 1:
            v.scalar_tensor_tensor(out=act_sb[:, j % 2, :], in0=ps_h[j % 2][:, 1, :], scalar=1.0 / SCALE,
                                   in1=act_sb[:, j % 2, :], op0=ALU.mult, op1=ALU.mult).then_inc(act_done, 1)
        else:
            v.wait_ge(h3c_done, n + 1)
            v.tensor_tensor(act_sb[0:SH_HALF, j % 2, :], h3c[0:SH_HALF, :], act_sb[0:SH_HALF, j % 2, :], ALU.mult).then_inc(act_done, 1)

    def low(v, n, c, j):
        w = P if j < J - 1 else SH_HALF
        v.wait_ge(at_hi, J * n + j + 1)
        v.tensor_tensor(at[0:w, j, 1, :], act_sb[0:w, j % 2, :], at[0:w, j, 0, :], ALU.subtract).then_inc(at_ready, 1)

    def add(v, n, c, t):
        i = 2 * n + t
        v.wait_ge(y_done, i + 1)
        if not is_first(n, t):
            v.wait_ge(xs_ready, i)
        v.scalar_tensor_tensor(out=t1[:, :], in0=ps_y[t][:, :], scalar=1.0 / SCALE, in1=s.gb_row(n),
                               op0=ALU.mult, op1=ALU.mult).then_inc(t1_done, 1)
        v.wait_ge(t1_done, i + 1)
        v.wait_ge(xs_loaded, 16 * (i + 1))
        v.tensor_tensor(xs[:, :], t1[:, :], xs[:, :], ALU.add).then_inc(xs_ready, 1)

    def up(pe, n, c, j):
        i = J * n + j
        if j == 0:
            pe.wait_ge(ht_loaded[c % 2], 32 * (n // 2 + 1))
        if not (isinstance(n, int) and i < 2):
            pe.wait_ge(act_done, i - 1)
        parts = 2 if j < J - 1 else 1
        for part in range(parts):
            for k in range(KC):
                lo = k * 2 * SHARED + (2 * j + part) * P
                mm = split_matmul(nc, ps_h[j % 2][:, part, :].rearrange("p (t n) -> p t n", t=2),
                                  (m.sh[:, 0, lo:lo + P], m.sh[:, 1, lo:lo + P]),
                                  (ht[:, c % 2, :, 0, k, :], ht[:, c % 2, :, 1, k, :]), k == 0, k == KC - 1)
        mm.then_inc(up_done, 1)

    def down(pe, n, c):
        for j0, j1 in ((0, J - 1), (J - 1, J)):
            pe.wait_ge(at_ready, J * n + j1)
            for t in range(2):
                if j0 == 0 and not is_first(n):
                    pe.wait_ge(t1_done, 2 * n - 1 + t)
                for j in range(j0, j1):
                    w = P if j < J - 1 else SH_HALF
                    lo = KC * 2 * SHARED + j * C
                    tok = slice(t * P, (t + 1) * P)
                    mm = split_matmul(nc, ps_y[t][:, :], (at[0:w, j, 0, tok], at[0:w, j, 1, tok]),
                                      (m.sh[0:w, 0, lo:lo + C], m.sh[0:w, 1, lo:lo + C]), j == 0, j == J - 1)
                if j1 == J:
                    mm.then_inc(y_done, 1)

    s.load_h, s.residual, s.activate, s.high, s.multiply, s.low, s.add, s.up, s.down = (
        load_h, residual, activate, high, multiply, low, add, up, down)
    return s


def route(nc, m):
    with ExitStack() as ctx:
        sb = lambda name, shape, dt: ctx.enter_context(nc.sbuf_tensor(name, shape, dt))
        sem = m.sem
        s = shared_steps(nc, m, ctx, "_b", 0)
        gb = sb("gb_b", [P, 2, C], F32)
        s.gb_row = lambda n: gb[:, n // 4, :]
        stage = sb("w_stage", [P, 2, C], F32)
        bias = sb("bias", [P, E], F32)
        places = {e: [m.w2[:, e, :, :, :].rearrange("p k s n -> p (k s n)"), 0] for e in (E - 2, E - 1)}

        def view(e, shape, dt, rows=P):
            flat, used = places[e]
            size = shape[0] * (shape[1] if len(shape) > 1 else 1) * (shape[2] if len(shape) > 2 else 1) * (1 if dt == F16 else 2)
            places[e][1] += size
            assert places[e][1] <= 3 * 2 * C
            piece = flat[0:rows, used:used + size]
            piece = piece if dt == F16 else piece.bitcast(dt)
            names = "abc"[:len(shape)]
            return piece.rearrange(f"p ({' '.join(names)}) -> p {' '.join(names)}", **dict(zip(names, shape)))

        scores = view(E - 1, (TILES, E), F32)
        sel = view(E - 1, (TILES, E), F32)
        top = view(E - 1, (TILES, 8), F32)
        index = view(E - 1, (TILES, 8), U32)
        choice = view(E - 1, (TOP, TILES, E), F32)
        both = view(E - 2, (TILES, E), F16)
        before = view(E - 2, (P,), F16)
        ones = view(E - 2, (P,), F16)
        passed = view(E - 2, (SLOT_TILES, E), F32, 1)
        indexf = sb("indexf", [P, TOP, TILES], F32)
        expert_no = sb("expert_no", [P, E], F32)
        onesf = sb("onesf", [P, TILES], F32)
        wsum = sb("wsum", [P, TILES], F32)
        count_i = sb("count_i", [P, E], I32)
        padded = sb("padded", [P, E], F32)
        ends = sb("ends", [P, E], F32)
        starts = sb("starts", [P, E], F32)
        slotf = sb("slotf", [P, TOP, TILES], F32)
        tile_at = sb("tile_at", [1, SLOT_TILES], F32)
        eidf = sb("eidf", [1, SLOT_TILES], F32)
        token = sb("token", [P, TILES], I32)
        entry = sb("entry", [P, TOP, TILES], I32)
        entry_tile = sb("entry_tile", [P, TOP, TILES], I32)
        sc_idx = sb("sc_idx", [P, 2, 1], I32)
        sc_tok = sb("sc_tok", [P, 2, 1], I32)
        ps_r = ctx.enter_context(nc.psum_tensor("ps_r", [P, 2, TILES * E], F32))
        gb_loaded = sem("gb_loaded")
        w_loaded = [sem(f"w_loaded{j}") for j in range(2)]
        w_hi, w_lo = sem("w_hi"), sem("w_lo")
        scores_ready, r_step, both_ready, ranks_done = sem("scores_ready"), sem("r_step"), sem("both_ready"), sem("ranks_done")
        consts, slots_ready = sem("consts"), sem("slots_ready")
        idx_copied = sem("idx_copied")
        scattered = [sem(f"scattered{j}") for j in range(2)]
        table_loaded = sem("table_loaded")
        CHUNKS = TILES // 4
        WP = 2 * KC + 3

        def piece(e, q):
            if q < 2 * KC:
                k, which = q // 2, q % 2
                src = (m.w1_d, m.w3_d)[which][bass.ds(e, 1), k * P:(k + 1) * P, :].rearrange("o p n -> (o p) n")
                return src, m.w13[:, e, k, :, which * INTER:(which + 1) * INTER], P, INTER
            k = q - 2 * KC
            rows = min(P, INTER - k * P)
            src = m.w2_d[bass.ds(e, 1), k * P:k * P + rows, :].rearrange("o p n -> (o p) n")
            return src, m.w2[0:rows, e, k, :, :], rows, C

        def over_chunks(eng, chunk):
            for n in (0, 1):
                chunk(n, n)
            with eng.Fori(1, CHUNKS // 2 - 1) as pair:
                for c in range(2):
                    chunk(2 * pair + c, c)
            for c in range(2):
                chunk(CHUNKS - 2 + c, c)

        def pieces_beside(j):
            return range(2 * j, min(2 * j + 2, WP))

        with nc.Block() as block:
            @block.sync
            def _(sp):
                for b in range(2):
                    sp.dma_start(gb[:, b, :], m.mod_d[b, 5 * C:6 * C].partition_broadcast(P)).then_inc(gb_loaded, 16)
                sp.dma_start(bias[:, :], m.router_bias.partition_broadcast(P)).then_inc(gb_loaded, 16)
                s.load_h(sp, 0, 0)

                def chunk(n, c):
                    if not (isinstance(n, int) and n == CHUNKS - 1):
                        s.load_h(sp, n + 1, c + 1)
                    s.residual(sp, n, c)

                over_chunks(sp, chunk)
                sp.wait_ge(s.xs_stored, 16 * 2 * CHUNKS)

            @block.scalar
            def _(act):
                def load_piece(n, c, q):
                    g, gc = WP * n + q, WP * c + q
                    if not (isinstance(n, int) and g < 2):
                        act.wait_ge(w_lo, g - 1)
                    src, _, rows, cols = piece(n, q)
                    act.dma_start(stage[0:rows, gc % 2, 0:cols], src).then_inc(w_loaded[gc % 2], 16)

                def piece_high(n, c, q):
                    g, gc = WP * n + q, WP * c + q
                    if q + 1 < WP:
                        load_piece(n, c, q + 1)
                    elif not (isinstance(n, int) and n == CHUNKS - 1):
                        load_piece(n + 1, c + 1, 0)
                    _, dst, rows, cols = piece(n, q)
                    act.wait_ge(w_loaded[gc % 2], 16 * ((WP * c + q) // 2 + 1) + 16 * WP * ((n - c) // 2))
                    act.activation(dst[:, 0, :], stage[0:rows, gc % 2, 0:cols], ACT.Copy, scale=SCALE).then_inc(w_hi, 1)

                def chunk(n, c):
                    for j in range(SH_TILES):
                        s.activate(act, n, c, j)
                        s.high(act, n, c, j)
                        for q in pieces_beside(j):
                            piece_high(n, c, q)

                load_piece(0, 0, 0)
                act.activation(scores[:, :, :], m.logits[:, :, :], ACT.Sigmoid).then_inc(scores_ready, 1)
                over_chunks(act, chunk)

            @block.vector
            def _(v):
                steps = 0

                def step(instruction):
                    nonlocal steps
                    steps += 1
                    instruction.then_inc(r_step, 1)
                    v.wait_ge(r_step, steps)

                def choose():
                    v.wait_ge(scores_ready, 1)
                    v.wait_ge(gb_loaded, 48)
                    step(v.tensor_tensor(sel[:, :, :], scores[:, :, :], bias[:, :].unsqueeze(1).to_broadcast([P, TILES, E]), ALU.add))
                    nonlocal steps
                    for t in range(TILES):
                        v.max(top[:, t, :], sel[:, t, :]).then_inc(r_step, 1)
                    steps += TILES
                    v.wait_ge(r_step, steps)
                    for t in range(TILES):
                        v.max_index(index[:, t, :], top[:, t, :], sel[:, t, :]).then_inc(r_step, 1)
                    steps += TILES
                    v.wait_ge(r_step, steps)
                    v.wait_ge(consts, 5)
                    for k in range(TOP):
                        step(v.tensor_copy(indexf[:, k, :], index[:, :, k]))
                        step(v.tensor_tensor(choice[:, k, :, :], expert_no[:, :].unsqueeze(1).to_broadcast([P, TILES, E]),
                                             indexf[:, k, :].unsqueeze(2).to_broadcast([P, TILES, E]), ALU.is_equal))
                        step(v.tensor_tensor(sel[:, :, :], choice[:, k, :, :], scores[:, :, :], ALU.mult))
                        step(v.reduce_sum(m.weight[:, k, :], sel[:, :, :], AX.X))
                    step(v.tensor_tensor(wsum[:, :], m.weight[:, 0, :], m.weight[:, 1, :], ALU.add))
                    step(v.tensor_scalar(wsum[:, :], wsum[:, :], SUM_EPS, None, ALU.max))
                    step(v.reciprocal(wsum[:, :], wsum[:, :]))
                    for k in range(TOP):
                        step(v.tensor_tensor(m.weight[:, k, :], m.weight[:, k, :], wsum[:, :], ALU.mult))
                    v.tensor_tensor(both[:, :, :], choice[:, 0, :, :], choice[:, 1, :, :], ALU.add).then_inc(both_ready, 1)

                def place():
                    v.wait_ge(ranks_done, 2)
                    rank = ps_r[:, 0, :].rearrange("p (t e) -> p t e", e=E)
                    total = ps_r[:, 1, :].rearrange("p (t e) -> p e t", e=E)
                    pos = sel
                    run = top[:, :, :].rearrange("p t e -> p (t e)").rearrange("p (e t) -> p e t", e=E)
                    for e in range(E):
                        step(v.tensor_tensor_scan(run[:, e, :], onesf[:, :], total[:, e, :], 0.0, ALU.mult, ALU.add))
                    step(v.tensor_scalar(padded[:, :], run[:, :, TILES - 1], float(P - 1), None, ALU.add))
                    step(v.tensor_copy(count_i[:, :], padded[:, :]))
                    step(v.tensor_scalar(count_i[:, :], count_i[:, :], -P, None, ALU.bitwise_and))
                    step(v.tensor_copy(padded[:, :], count_i[:, :]))
                    step(v.tensor_tensor_scan(ends[:, :], onesf[:, 0:E], padded[:, :], 0.0, ALU.mult, ALU.add))
                    step(v.tensor_tensor(starts[:, :], ends[:, :], padded[:, :], ALU.subtract))
                    step(v.tensor_tensor(run, run, starts[:, :].unsqueeze(2).to_broadcast([P, E, TILES]), ALU.add))
                    step(v.tensor_tensor(run, run, total, ALU.subtract))
                    step(v.tensor_tensor(pos[:, :, :], rank, run.rearrange("p e t -> p t e"), ALU.add))
                    for k in range(TOP):
                        step(v.tensor_tensor(scores[:, :, :], choice[:, k, :, :], pos[:, :, :], ALU.mult))
                        step(v.reduce_sum(slotf[:, k, :], scores[:, :, :], AX.X))
                    step(v.tensor_copy(m.slot[:, :, :], slotf[:, :, :]))
                    step(v.tensor_scalar(entry[:, :, :], m.slot[:, :, :], P - 1, None, ALU.bitwise_and))
                    step(v.tensor_scalar(entry[:, :, :], entry[:, :, :], float(SLOT_TILES), None, ALU.mult))
                    step(v.tensor_scalar(entry_tile[:, :, :], m.slot[:, :, :], P.bit_length() - 1, None, ALU.logical_shift_right))
                    v.tensor_tensor(entry[:, :, :], entry[:, :, :], entry_tile[:, :, :], ALU.add).then_inc(slots_ready, 1)
                    step(v.tensor_tensor(passed[:, :, :], ends[0:1, :].unsqueeze(1).to_broadcast([1, SLOT_TILES, E]),
                                         tile_at[:, :].unsqueeze(2).to_broadcast([1, SLOT_TILES, E]), ALU.is_le))
                    step(v.reduce_sum(eidf[:, :], passed[:, :, :], AX.X))
                    step(v.tensor_scalar(eidf[:, :], eidf[:, :], float(E - 1), None, ALU.min))
                    step(v.tensor_copy(m.eid[:, :], eidf[:, :]))

                def piece_low(n, c, q):
                    g, gc = WP * n + q, WP * c + q
                    _, dst, rows, cols = piece(n, q)
                    v.wait_ge(w_hi, g + 1)
                    v.scalar_tensor_tensor(out=dst[:, 1, :], in0=stage[0:rows, gc % 2, 0:cols], scalar=SCALE, in1=dst[:, 0, :],
                                           op0=ALU.mult, op1=ALU.subtract).then_inc(w_lo, 1)

                def chunk(n, c):
                    for j in range(SH_TILES):
                        s.multiply(v, n, c, j)
                        s.low(v, n, c, j)
                        for q in pieces_beside(j):
                            piece_low(n, c, q)
                    for t in range(2):
                        s.add(v, n, c, t)
                    if isinstance(n, int) and n == 0:
                        place()

                choose()
                over_chunks(v, chunk)

            @block.tensor
            def _(pe):
                def chunk(n, c):
                    for j in range(SH_TILES):
                        s.up(pe, n, c, j)
                    s.down(pe, n, c)
                    if isinstance(n, int) and n == 0:
                        pe.wait_ge(both_ready, 1)
                        pe.wait_ge(consts, 6)
                        for part, lhs in ((0, before), (1, ones)):
                            nc.tensor.matmul(ps_r[:, part, :], lhs[:, :], both[:, :, :].rearrange("p t e -> p (t e)"),
                                             start=True, stop=True).then_inc(ranks_done, 1)

                over_chunks(pe, chunk)

            @block.gpsimd
            def _(pool):
                pool.iota(expert_no[:, :], [[1, E]], base=0, channel_multiplier=0, allow_small_or_imprecise_dtypes=True).then_inc(consts, 1)
                pool.iota(tile_at[:, :], [[P, SLOT_TILES]], base=0, channel_multiplier=0, allow_small_or_imprecise_dtypes=True).then_inc(consts, 1)
                pool.iota(token[:, :], [[P, TILES]], base=0, channel_multiplier=1).then_inc(consts, 1)
                pool.memset(ones[:, :], 1.0).then_inc(consts, 1)
                pool.memset(onesf[:, :], 1.0).then_inc(consts, 1)
                pool.wait_ge(consts, 5)
                pool.affine_select(out=before[:, :], in_=ones[:, :], compare_op=ALU.is_gt, fill=0.0,
                                   base=0, pattern=[[1, P]], channel_multiplier=-1).then_inc(consts, 1)
                pool.wait_ge(consts, 6)
                pool.wait_ge(slots_ready, 1)

                def scatter(t, k, first):
                    if not first:
                        pool.wait_ge(scattered[k], 16 * t)
                    pool.tensor_copy(sc_idx[:, k, :], entry[:, k, bass.ds(t, 1)]).then_inc(idx_copied, 1)
                    pool.tensor_copy(sc_tok[:, k, :], token[:, bass.ds(t, 1)]).then_inc(idx_copied, 1)
                    pool.wait_ge(idx_copied, 2 * (TOP * t + k + 1))
                    carry_waits(pool, m.spare[:, :])
                    pool.indirect_dma_start(m.table, bass.IndirectOffsetOnAxis(ap=sc_idx[:, k, :], axis=0),
                                            sc_tok[:, k, :], None).then_inc(scattered[k], 16)

                for k in range(TOP):
                    scatter(0, k, True)
                with pool.Fori(1, TILES) as t:
                    for k in range(TOP):
                        scatter(t, k, False)
                for k in range(TOP):
                    pool.wait_ge(scattered[k], 16 * TILES)
                pool.dma_start(m.slot_token[:, :], m.table.rearrange("(p t) o -> p (t o)", p=P)).then_inc(table_loaded, 16)
                pool.wait_ge(table_loaded, 16)


def experts(nc, m):
    with ExitStack() as ctx:
        sb = lambda name, shape, dt: ctx.enter_context(nc.sbuf_tensor(name, shape, dt))
        pb = lambda name, shape: ctx.enter_context(nc.psum_tensor(name, shape, F32))
        sem = m.sem
        IT = 3
        g_idx = sb("g_idx", [P, 2, 1], I32)
        g = sb("g", [P, 2, C], F32)
        xt = sb("xt", [P, 2, 2, KC, P], F16)
        a = sb("a", [P, 2, IT * P], F32)
        at = sb("at", [P, 2, 2, IT, P], F16)
        y = sb("y", [P, 2, C], F32)
        ps_x, ps_h1, ps_h3, ps_a, ps_y = pb("ps_x", [P, KC, P]), pb("ps_h1", [P, INTER]), pb("ps_h3", [P, INTER]), pb("ps_a", [P, IT, P]), pb("ps_ey", [P, C])
        g_idx_copied = sem("g_idx_copied")
        gathered = [sem(f"gathered{j}") for j in range(2)]
        xt_done, xt_hi, xt_ready, h1_done, h3_done = sem("xt_done"), sem("xt_hi"), sem("xt_ready"), sem("h1_done"), sem("h3_done")
        e_silu, e_act, a_padded, at_done, e_at_hi, e_at_ready = sem("e_silu"), sem("e_act"), sem("a_padded"), sem("at_done"), sem("e_at_hi"), sem("e_at_ready")
        ey_done, ey_ready = sem("ey_done"), sem("ey_ready")
        y_stored = [sem(f"y_stored{j}") for j in range(2)]

        def later(t, n):
            return not isinstance(t, int) or t >= n

        def there(t):
            return not isinstance(t, int) or 0 <= t < SLOT_TILES

        def over_tiles(eng, slot):
            for t in (0, 1):
                slot(t, t)
            with eng.Fori(1, (SLOT_TILES - 1) // 2) as pair:
                for c in range(2):
                    slot(2 * pair + c, c)
            for t in range(SLOT_TILES - 1 - (SLOT_TILES - 1) % 2, SLOT_TILES + 1):
                slot(t, t)

        with nc.Block() as block:
            @block.gpsimd
            def _(pool):
                def gather(t, c):
                    if not there(t):
                        return
                    if later(t, 2):
                        pool.wait_ge(gathered[c % 2], 16 * (t // 2))
                        pool.wait_ge(xt_done, t - 1)
                    pool.tensor_copy(g_idx[:, c % 2, :], m.slot_token[:, bass.ds(t, 1)]).then_inc(g_idx_copied, 1)
                    pool.wait_ge(g_idx_copied, t + 1)
                    carry_waits(pool, m.spare[:, :])
                    pool.indirect_dma_start(g[:, c % 2, :], None, m.h2_d,
                                            bass.IndirectOffsetOnAxis(ap=g_idx[:, c % 2, :], axis=0)).then_inc(gathered[c % 2], 16)

                over_tiles(pool, gather)

            @block.sync
            def _(sp):
                def slot(t, c):
                    u, d = t - 1, c - 1
                    if there(u):
                        sp.wait_ge(ey_ready, u + 1)
                        sp.dma_start(m.y_d[bass.ds(u * P, P), :], y[:, d % 2, :]).then_inc(y_stored[d % 2], 16)

                over_tiles(sp, slot)
                sp.wait_ge(y_stored[0], 16 * ((SLOT_TILES + 1) // 2))
                sp.wait_ge(y_stored[1], 16 * (SLOT_TILES // 2))

            @block.scalar
            def _(act):
                def x_high(t, c):
                    if not there(t):
                        return
                    act.wait_ge(xt_done, t + 1)
                    if later(t, 2):
                        act.wait_ge(h3_done, t - 1)
                    act.activation(xt[:, c % 2, 0, :, :], ps_x[:, :, :], ACT.Copy).then_inc(xt_hi, 1)

                def slot(t, c):
                    u, d = t - 1, c - 1
                    if there(u):
                        act.wait_ge(at_done, u + 1)
                        if later(u, 2):
                            act.wait_ge(ey_done, u - 1)
                        act.activation(at[:, d % 2, 0, :, :], ps_a[:, :, :], ACT.Copy).then_inc(e_at_hi, 1)
                    x_high(t + 1, c + 1)
                    if there(t):
                        act.wait_ge(h1_done, t + 1)
                        if later(t, 2):
                            act.wait_ge(at_done, t - 1)
                        act.activation(a[:, c % 2, 0:INTER], ps_h1[:, :], ACT.Silu, scale=1.0 / SCALE).then_inc(e_silu, 1)
                    if there(u):
                        act.wait_ge(ey_done, u + 1)
                        if later(u, 2):
                            act.wait_ge(y_stored[d % 2], 16 * (u // 2))
                        act.activation(y[:, d % 2, :], ps_y[:, :], ACT.Copy, scale=1.0 / SCALE).then_inc(ey_ready, 1)

                x_high(0, 0)
                over_tiles(act, slot)

            @block.vector
            def _(v):
                v.memset(a[:, :, INTER:IT * P], 0.0).then_inc(a_padded, 1)

                def x_low(t, c):
                    if not there(t):
                        return
                    v.wait_ge(xt_hi, t + 1)
                    v.tensor_tensor(xt[:, c % 2, 1, :, :], ps_x[:, :, :], xt[:, c % 2, 0, :, :], ALU.subtract).then_inc(xt_ready, 1)

                def slot(t, c):
                    u, d = t - 1, c - 1
                    if there(u):
                        v.wait_ge(e_at_hi, u + 1)
                        v.tensor_tensor(at[:, d % 2, 1, :, :], ps_a[:, :, :], at[:, d % 2, 0, :, :], ALU.subtract).then_inc(e_at_ready, 1)
                    x_low(t + 1, c + 1)
                    if there(t):
                        v.wait_ge(h3_done, t + 1)
                        v.wait_ge(e_silu, t + 1)
                        v.scalar_tensor_tensor(out=a[:, c % 2, 0:INTER], in0=ps_h3[:, :], scalar=1.0 / SCALE, in1=a[:, c % 2, 0:INTER],
                                               op0=ALU.mult, op1=ALU.mult).then_inc(e_act, 1)

                x_low(0, 0)
                over_tiles(v, slot)

            @block.tensor
            def _(pe):
                def transpose_x(t, c):
                    if not there(t):
                        return
                    pe.wait_ge(gathered[c % 2], 16 * (t // 2 + 1))
                    if later(t, 1):
                        pe.wait_ge(xt_ready, t)
                    for k in range(KC):
                        mm = nc.tensor.transpose(ps_x[:, k, :], g[:, c % 2, k * P:(k + 1) * P], m.ident[:, :])
                    mm.then_inc(xt_done, 1)

                def up(t, c):
                    expert = pe.value_load(m.eid[0:1, bass.ds(t, 1)], min_val=0, max_val=E - 1)
                    pe.wait_ge(xt_ready, t + 1)
                    for which, ps, done in ((0, ps_h1, h1_done), (1, ps_h3, h3_done)):
                        if later(t, 1):
                            pe.wait_ge(e_act, t)
                        cols = slice(which * INTER, (which + 1) * INTER)
                        for k in range(KC):
                            mm = split_matmul(nc, ps[:, :], (xt[:, c % 2, 0, k, :], xt[:, c % 2, 1, k, :]),
                                              (m.w13[:, bass.ds(expert, 1), k, 0, cols].rearrange("p o n -> p (o n)"),
                                               m.w13[:, bass.ds(expert, 1), k, 1, cols].rearrange("p o n -> p (o n)")),
                                              k == 0, k == KC - 1)
                        mm.then_inc(done, 1)

                def transpose_a(t, c):
                    pe.wait_ge(a_padded, 1)
                    pe.wait_ge(e_act, t + 1)
                    if later(t, 1):
                        pe.wait_ge(e_at_ready, t)
                    for k in range(IT):
                        mm = nc.tensor.transpose(ps_a[:, k, :], a[:, c % 2, k * P:(k + 1) * P], m.ident[:, :])
                    mm.then_inc(at_done, 1)

                def down(t, c):
                    expert = pe.value_load(m.eid[0:1, bass.ds(t, 1)], min_val=0, max_val=E - 1)
                    pe.wait_ge(e_at_ready, t + 1)
                    if later(t, 1):
                        pe.wait_ge(ey_ready, t)
                    for k in range(IT):
                        w = min(P, INTER - k * P)
                        mm = split_matmul(nc, ps_y[:, :], (at[0:w, c % 2, 0, k, :], at[0:w, c % 2, 1, k, :]),
                                          (m.w2[0:w, bass.ds(expert, 1), k, 0, :].rearrange("p o n -> p (o n)"),
                                           m.w2[0:w, bass.ds(expert, 1), k, 1, :].rearrange("p o n -> p (o n)")),
                                          k == 0, k == IT - 1)
                    mm.then_inc(ey_done, 1)

                def slot(t, c):
                    if there(t - 1):
                        transpose_a(t - 1, c - 1)
                    transpose_x(t + 1, c + 1)
                    if there(t):
                        up(t, c)
                    if there(t - 1):
                        down(t - 1, c - 1)

                transpose_x(0, 0)
                over_tiles(pe, slot)


def combine(nc, m):
    with ExitStack() as ctx:
        sb = lambda name, shape, dt: ctx.enter_context(nc.sbuf_tensor(name, shape, dt))
        sem = m.sem
        CHUNKS = TILES // 4
        PER = TILES // CHUNKS
        s = shared_steps(nc, m, ctx, "_d", CHUNKS)
        gb = sb("gb_d", [P, B, C], F32)
        s.gb_row = lambda n: gb[:, (n + CHUNKS) // 4, :]
        y_idx = sb("y_idx", [P, PER, TOP, 1], I32)
        y = sb("y_rows", [P, PER, TOP, C], F32)
        xc = sb("xc", [P, PER, C], F32)
        gb_loaded = sem("gb_loaded_d")
        y_idx_copied, combined, c_step = sem("y_idx_copied"), sem("combined"), sem("c_step")
        y_loaded = [sem(f"y_loaded{j}") for j in range(PER)]
        xc_loaded = [sem(f"xc_loaded{j}") for j in range(PER)]
        out_stored = [sem(f"out_stored{j}") for j in range(PER)]

        def over_chunks(eng, chunk):
            for n in (0, 1):
                chunk(n, n)
            with eng.Fori(1, CHUNKS // 2 - 1) as pair:
                for c in range(2):
                    chunk(2 * pair + c, c)
            for c in range(2):
                chunk(CHUNKS - 2 + c, c)

        with nc.Block() as block:
            @block.sync
            def _(sp):
                for b in range(B):
                    sp.dma_start(gb[:, b, :], m.mod_d[b, 5 * C:6 * C].partition_broadcast(P)).then_inc(gb_loaded, 16)
                s.load_h(sp, 0, 0)

                def chunk(n, c):
                    if not (isinstance(n, int) and n == CHUNKS - 1):
                        s.load_h(sp, n + 1, c + 1)
                    s.residual(sp, n, c)

                over_chunks(sp, chunk)

            @block.gpsimd
            def _(pool):
                def fetch(n, j):
                    t = PER * n + j
                    if not (isinstance(n, int) and n == 0):
                        pool.wait_ge(out_stored[j], 16 * n)
                    for k in range(TOP):
                        pool.tensor_copy(y_idx[:, j, k, :], m.slot[:, k, bass.ds(t, 1)]).then_inc(y_idx_copied, 1)
                    if j % 2 == 0:
                        if isinstance(n, int) and PER * n + j >= TILES // 2:
                            pool.wait_ge(s.xs_stored, 16 * (PER * n + j + 2 - TILES // 2))
                        elif not isinstance(n, int):
                            pool.wait_ge(s.xs_stored, 16 * (2 * n - 2))
                    pool.wait_ge(y_idx_copied, TOP * (t + 1))
                    carry_waits(pool, m.spare[:, :])
                    for k in range(TOP):
                        pool.indirect_dma_start(y[:, j, k, :], None, m.y_d,
                                                bass.IndirectOffsetOnAxis(ap=y_idx[:, j, k, :], axis=0)).then_inc(y_loaded[j], 16)
                    pool.dma_start(xc[:, j, :], m.x2s_d[bass.ds(t * P, P), :]).then_inc(xc_loaded[j], 16)

                def chunk(n, c):
                    for j in range(PER):
                        fetch(n, j)

                over_chunks(pool, chunk)

            @block.scalar
            def _(act):
                def store(n, j):
                    t = PER * n + j
                    act.wait_ge(combined, t + 1)
                    act.dma_start(m.out[bass.ds(t * P, P), :], y[:, j, 1, :]).then_inc(out_stored[j], 16)

                def chunk(n, c):
                    last = isinstance(n, int) and n == CHUNKS - 1
                    for j in range(SH_TILES):
                        s.activate(act, n, c, j)
                        s.high(act, n, c, j)
                        if 1 <= j <= PER and not last:
                            store(n, j - 1)
                    if last:
                        for j in range(PER):
                            store(n, j)

                over_chunks(act, chunk)
                for j in range(PER):
                    act.wait_ge(out_stored[j], 16 * CHUNKS)

            @block.vector
            def _(v):
                def combine_tile(n, j):
                    t = PER * n + j
                    v.wait_ge(y_loaded[j], 16 * TOP * (n + 1))
                    v.tensor_scalar(y[:, j, 0, :], y[:, j, 0, :], m.weight[:, 0, bass.ds(t, 1)], None, ALU.mult).then_inc(c_step, 1)
                    v.wait_ge(c_step, 3 * t + 1)
                    v.scalar_tensor_tensor(out=y[:, j, 1, :], in0=y[:, j, 1, :], scalar=m.weight[:, 1, bass.ds(t, 1)],
                                           in1=y[:, j, 0, :], op0=ALU.mult, op1=ALU.add).then_inc(c_step, 1)
                    v.wait_ge(c_step, 3 * t + 2)
                    v.tensor_tensor(y[:, j, 1, :], y[:, j, 1, :], gb[:, t // BT, :], ALU.mult).then_inc(c_step, 1)
                    v.wait_ge(c_step, 3 * t + 3)
                    v.wait_ge(xc_loaded[j], 16 * (n + 1))
                    v.tensor_tensor(y[:, j, 1, :], y[:, j, 1, :], xc[:, j, :], ALU.add).then_inc(combined, 1)

                def chunk(n, c):
                    last = isinstance(n, int) and n == CHUNKS - 1
                    for j in range(SH_TILES):
                        s.multiply(v, n, c, j)
                        s.low(v, n, c, j)
                        if j < PER and not last:
                            combine_tile(n, j)
                    for t in range(2):
                        s.add(v, n, c, t)
                    if last:
                        for j in range(PER):
                            combine_tile(n, j)

                v.wait_ge(gb_loaded, 16 * B)
                over_chunks(v, chunk)

            @block.tensor
            def _(pe):
                def chunk(n, c):
                    for j in range(SH_TILES):
                        s.up(pe, n, c, j)
                    s.down(pe, n, c)

                over_chunks(pe, chunk)


def adaln_block(nc, x, wqkv_t, wproj_t, b_proj, gate_t, router_bias, w1_d, w3_d, w2_d, sh_flat, c_t, wmod_d, out):
    m = Parts()
    m.x, m.wqkv_t, m.wproj_t, m.b_proj, m.gate_t, m.router_bias = x, wqkv_t, wproj_t, b_proj, gate_t, router_bias
    m.w1_d, m.w3_d, m.w2_d, m.sh_flat, m.c_t, m.wmod_d, m.out = w1_d, w3_d, w2_d, sh_flat, c_t, wmod_d, out
    with ExitStack() as ctx:
        m.sem = lambda name: ctx.enter_context(nc.semaphore(name))
        dram = lambda name, shape, dt: nc.dram_tensor(name, shape, dt).ap()
        m.x2_d, m.x2s_d, m.h2_d = dram("x2_d", (T, C), F32), dram("x2s_d", (T, C), F32), dram("h2_d", (T, C), F32)
        m.h2t_d, m.y_d = dram("h2t_d", (TILES, P, 2 * C), F16), dram("y_d", (SLOTS, C), F32)
        m.mod_d, m.gab_d, m.table = dram("mod_d", (B, 6 * C), F32), dram("gab_d", (B, C), F32), dram("table", (SLOTS, 1), I32)

        def sb(name, shape, dt, stack=ctx):
            return stack.enter_context(nc.sbuf_tensor(name, shape, dt))

        m.ident = sb("ident", [P, P], F32)
        m.spare = sb("spare", [P, 1], F32)
        m.logits = sb("logits", [P, TILES, E], F32)
        m.weight = sb("weight", [P, TOP, TILES], F32)
        m.slot = sb("slot", [P, TOP, TILES], I32)
        m.slot_token = sb("slot_token", [P, SLOT_TILES], I32)
        m.eid = sb("eid", [1, SLOT_TILES], I32)
        m.sh = sb("sh", [P, 2, KC * 2 * SHARED + SH_TILES * C], F16)
        with ExitStack() as attention:
            m.gate = sb("gate", [P, KC, 2, E], F16, attention)
            m.heads = sb("heads", [P, 4], F32, attention)
            m.head_mask = sb("head_mask", [P, P], F32, attention)
            m.minus_half = sb("minus_half", [P, 1], F32, attention)
            m.wproj = sb("wproj", [P, KC, 2, C], F16, attention)
            m.vk = sb("vk", [P, B, 2, GRP, VKW], F16, attention)
            m.qt_flat = sb("qt", [P, TILES * 2 * GRP * P], F16, attention)
            m.qt = m.qt_flat[:, :].rearrange("p (t s g n) -> p t s g n", t=TILES, s=2, g=GRP)
            with ExitStack() as projections:
                m.wqkv = sb("wqkv", [P, KC, 2, 3 * C], F16, projections)
                m.v_sb = sb("v_sb", [P, 2, GRP, P + 1], F32, projections)
                m.rows = sb("rows", [P, B, 2, C], F32, projections)
                setup(nc, m)
                front(nc, m)
            back(nc, m)
        with ExitStack() as expert_weights:
            m.w13 = sb("w13", [P, E, KC, 2, 2 * INTER], F16, expert_weights)
            m.w2 = sb("w2", [P, E, 3, 2, C], F16, expert_weights)
            route(nc, m)
            experts(nc, m)
        combine(nc, m)


def kernel(L0_attn_x, L0_attn_w_qkv, L0_attn_w_proj, L0_attn_b_proj, L0_ffn_gate_w, L0_ffn_router_bias, L0_ffn_W1,
           L0_ffn_W3, L0_ffn_W2, L0_ffn_sw1, L0_ffn_sw3, L0_ffn_sw2, L0_c, L0_wmod):
    import numpy as np
    import concourse.bacc as bacc
    from concourse.bass_utils import run_bass_kernel_spmd as run

    def t(a):
        return np.ascontiguousarray(np.asarray(a).T)

    sw1, sw3, sw2 = t(L0_ffn_sw1), t(L0_ffn_sw3), t(L0_ffn_sw2)
    turns = [w[:, j * P:(j + 1) * P] for j in range(SH_TILES) for w in (sw1, sw3)]
    up = np.concatenate(turns, axis=1).reshape(KC, P, 2 * SHARED).transpose(1, 0, 2).reshape(P, -1)
    down = np.zeros((SH_TILES * P, C), sw2.dtype)
    down[:SHARED] = sw2
    down = down.reshape(SH_TILES, P, C).transpose(1, 0, 2).reshape(P, -1)
    arrays = {
        "x": np.ascontiguousarray(L0_attn_x).reshape(T, C), "wqkv_t": t(L0_attn_w_qkv), "wproj_t": t(L0_attn_w_proj),
        "b_proj": np.ascontiguousarray(L0_attn_b_proj), "gate_t": t(L0_ffn_gate_w),
        "router_bias": np.ascontiguousarray(L0_ffn_router_bias), "w1_d": np.ascontiguousarray(L0_ffn_W1),
        "w3_d": np.ascontiguousarray(L0_ffn_W3), "w2_d": np.ascontiguousarray(L0_ffn_W2),
        "sh_flat": np.ascontiguousarray(np.concatenate([up, down], axis=1)), "c_t": t(L0_c),
        "wmod_d": np.ascontiguousarray(L0_wmod),
    }
    nc = bacc.Bacc("TRN2", target_bir_lowering=False, num_devices=1)
    handles = {k: nc.dram_tensor(f"in_{k}", v.shape, mybir.dt.from_np(v.dtype), kind="ExternalInput").ap() for k, v in arrays.items()}
    out = nc.dram_tensor("out_0", (T, C), F32, kind="ExternalOutput").ap()
    adaln_block(nc, out=out, **handles)
    r = run(nc, [{f"in_{k}": v for k, v in arrays.items()}], core_ids=[0])
    return r.results[0]["out_0"].reshape(B, N, C)
```

```python
from contextlib import ExitStack

import concourse.bass as bass
from concourse import mybir

F32 = mybir.dt.float32
F16 = mybir.dt.float16
I32 = mybir.dt.int32
U32 = mybir.dt.uint32
ALU = mybir.AluOpType
ACT = mybir.ActivationFunctionType
AX = mybir.AxisListType

P = 128
B, N, C = 4, 1024, 512
HEAD = 32
T = B * N
TILES = T // P
BT = N // P
KC = C // P
E, TOP = 8, 2
INTER = 352
SHARED = 704
SH_TILES = 6
SH_HALF = SHARED - 5 * P
SLOT_TILES = (T * TOP + E * (P - 1)) // P
SLOTS = SLOT_TILES * P
SCALE = 64.0
VK_SCALE = 1.0 / 64.0
GRP = 4
VKW = P + 4
LN_EPS, DEN_EPS, SUM_EPS = 1e-5, 1e-15, 1e-12
SA, CA = range(2)
GA, GAB, SB, CB = range(4)
PIECE = (KC * 2 * SHARED + SH_TILES * C) // TILES


class Parts:
    pass


def split_matmul(nc, out, lhs, rhs, first, last):
    (lh, ll), (rh, rl) = lhs, rhs
    nc.tensor.matmul(out, lh, rh, start=first, stop=False, skip_group_check=True)
    nc.tensor.matmul(out, lh, rl, start=False, stop=False, skip_group_check=True)
    return nc.tensor.matmul(out, ll, rh, start=False, stop=last, skip_group_check=True)


def setup(nc, m):
    with ExitStack() as ctx:
        sb = lambda name, shape, dt: ctx.enter_context(nc.sbuf_tensor(name, shape, dt))
        ct = sb("ct", [P, KC, B], F32)
        sct = sb("sct", [P, KC, B], F32)
        wmod = m.qt_flat[:, 0:KC * 6 * C * 2].bitcast(F32).rearrange("p (k n) -> p k n", k=KC)
        stage = sb("stage", [P, 2, 3 * C], F32)
        mod = sb("mod", [B, 6 * C], F32)
        gate_tmp = sb("gate_tmp", [B, 2 * C], F32)
        bproj = sb("bproj", [B, C], F32)
        gstage = sb("gstage", [P, KC, E], F32)
        zero = sb("zero", [P, SLOT_TILES], I32)
        ps = [ctx.enter_context(nc.psum_tensor(f"ps_mod{j}", [B, C], F32)) for j in range(6)]
        sem = m.sem
        c_loaded, silu_done = sem("c_loaded"), sem("silu_done")
        wmod_loaded = [sem(f"wmod_loaded{k}") for k in range(KC)]
        stage_loaded = [sem(f"stage_loaded{k}") for k in range(2)]
        stage_hi, stage_lo = sem("stage_hi"), sem("stage_lo")
        small_loaded, mod_done, mod_step = sem("small_loaded"), sem("mod_done"), sem("mod_step")
        mod_ready, mod_stored = sem("mod_ready"), sem("mod_stored")
        rows_loaded = sem("rows_loaded")
        const_step = sem("const_step")
        pieces = [(m.wqkv_t[k * P:(k + 1) * P, :], m.wqkv[:, k, :, :], 3 * C) for k in range(KC)]
        pieces += [(m.wproj_t[k * P:(k + 1) * P, :], m.wproj[:, k, :, :], C) for k in range(KC)]

        with nc.Block() as block:
            @block.sync
            def _(sp):
                sp.dma_start(ct[:, :, :], m.c_t.rearrange("(k p) b -> p k b", p=P)).then_inc(c_loaded, 16)
                for k in range(KC):
                    sp.dma_start(wmod[:, k, :], m.wmod_d[k * P:(k + 1) * P, :]).then_inc(wmod_loaded[k], 16)
                sp.dma_start(bproj[:, :], m.b_proj.partition_broadcast(B)).then_inc(small_loaded, 16)
                sp.dma_start(gstage[:, :, :], m.gate_t.rearrange("(k p) e -> p k e", p=P)).then_inc(small_loaded, 16)
                for n, (src, _, w) in enumerate(pieces):
                    if n >= 2:
                        sp.wait_ge(stage_hi, n - 1)
                        sp.wait_ge(stage_lo, n - 1)
                    sp.dma_start(stage[:, n % 2, 0:w], src).then_inc(stage_loaded[n % 2], 16)
                sp.wait_ge(mod_ready, 1)
                sp.dma_start(m.mod_d, mod[:, :]).then_inc(mod_stored, 16)
                sp.dma_start(m.gab_d, gate_tmp[:, 0:C]).then_inc(mod_stored, 16)
                sp.wait_ge(const_step, 1)
                sp.dma_start(m.table.rearrange("(p t) o -> p (t o)", p=P), zero[:, :]).then_inc(rows_loaded, 16)
                sp.wait_ge(mod_stored, 32)
                for b in range(B):
                    for r, src in ((SA, m.mod_d[b, 0:C]), (CA, m.mod_d[b, C:2 * C])):
                        sp.dma_start(m.rows[:, b, r, :], src.partition_broadcast(P)).then_inc(rows_loaded, 16)
                sp.wait_ge(rows_loaded, 16 * (2 * B + 1))

            @block.scalar
            def _(act):
                act.wait_ge(c_loaded, 16)
                act.activation(sct[:, :, :], ct[:, :, :], ACT.Silu).then_inc(silu_done, 1)
                for n, (_, dst, w) in enumerate(pieces):
                    act.wait_ge(stage_loaded[n % 2], 16 * (n // 2 + 1))
                    act.activation(dst[:, 0, :], stage[:, n % 2, 0:w], ACT.Copy, scale=SCALE).then_inc(stage_hi, 1)
                act.wait_ge(small_loaded, 32)
                act.activation(m.gate[:, :, 0, :], gstage[:, :, :], ACT.Copy, scale=SCALE).then_inc(stage_hi, 1)

            @block.vector
            def _(v):
                for n, (_, dst, w) in enumerate(pieces):
                    v.wait_ge(stage_hi, n + 1)
                    v.scalar_tensor_tensor(out=dst[:, 1, :], in0=stage[:, n % 2, 0:w], scalar=SCALE, in1=dst[:, 0, :],
                                           op0=ALU.mult, op1=ALU.subtract).then_inc(stage_lo, 1)
                v.wait_ge(stage_hi, len(pieces) + 1)
                v.scalar_tensor_tensor(out=m.gate[:, :, 1, :], in0=gstage[:, :, :], scalar=SCALE, in1=m.gate[:, :, 0, :],
                                       op0=ALU.mult, op1=ALU.subtract).then_inc(stage_lo, 1)
                v.wait_ge(mod_done, 6)
                steps = 0

                def step(instruction):
                    nonlocal steps
                    steps += 1
                    instruction.then_inc(mod_step, 1)
                    v.wait_ge(mod_step, steps)

                for j in range(6):
                    if j in (1, 4):
                        step(v.tensor_scalar(mod[:, j * C:(j + 1) * C], ps[j][:, :], 1.0, None, ALU.add))
                    elif j in (0, 3):
                        step(v.tensor_copy(mod[:, j * C:(j + 1) * C], ps[j][:, :]))
                    else:
                        mag, sgn = gate_tmp[:, 0:C], gate_tmp[:, C:2 * C]
                        step(v.tensor_scalar(mag, ps[j][:, :], -1.0, None, ALU.mult))
                        step(v.tensor_tensor(mag, ps[j][:, :], mag, ALU.max))
                        step(v.tensor_scalar(mag, mag, 0.25, None, ALU.max))
                        step(v.tensor_scalar(sgn, ps[j][:, :], 0.0, 2.0, ALU.is_ge, ALU.mult))
                        step(v.tensor_scalar(sgn, sgn, -1.0, None, ALU.add))
                        step(v.tensor_tensor(mod[:, j * C:(j + 1) * C], mag, sgn, ALU.mult))
                v.wait_ge(small_loaded, 32)
                v.tensor_tensor(gate_tmp[:, 0:C], mod[:, 2 * C:3 * C], bproj[:, :], ALU.mult).then_inc(mod_ready, 1)

            @block.tensor
            def _(pe):
                pe.wait_ge(silu_done, 1)
                for k in range(KC):
                    pe.wait_ge(wmod_loaded[k], 16)
                    for j in range(6):
                        mm = nc.tensor.matmul(ps[j][:, :], sct[:, k, :], wmod[:, k, j * C:(j + 1) * C],
                                              start=k == 0, stop=k == KC - 1)
                        if k == KC - 1:
                            mm.then_inc(mod_done, 1)

            @block.gpsimd
            def _(pool):
                steps = 0

                def step(instruction):
                    nonlocal steps
                    steps += 1
                    instruction.then_inc(const_step, 1)
                    pool.wait_ge(const_step, steps)

                step(pool.memset(zero[:, :], 0))
                step(pool.memset(m.ident[:, :], 0.0))
                step(pool.affine_select(out=m.ident[:, :], in_=m.ident[:, :], compare_op=ALU.not_equal, fill=1.0,
                                        base=0, pattern=[[-1, P]], channel_multiplier=1))
                step(pool.memset(m.heads[:, :], VK_SCALE))
                step(pool.affine_select(out=m.heads[:, :], in_=m.heads[:, :], compare_op=ALU.is_ge, fill=0.0,
                                        base=0, pattern=[[-HEAD, 4]], channel_multiplier=1))
                step(pool.affine_select(out=m.heads[:, :], in_=m.heads[:, :], compare_op=ALU.is_ge, fill=0.0,
                                        base=HEAD - 1, pattern=[[HEAD, 4]], channel_multiplier=-1))
                step(pool.tensor_copy(m.head_mask[:, :].rearrange("p (h e) -> p h e", h=4),
                                      m.heads[:, :].unsqueeze(2).to_broadcast([P, 4, HEAD])))
                step(pool.memset(m.minus_half[:, :], -0.5))
                step(pool.memset(m.spare[:, :], 0.0))
                step(pool.memset(m.v_sb[:, :, :, P:P + 1], 1.0))


def front(nc, m):
    with ExitStack() as ctx:
        sb = lambda name, shape, dt: ctx.enter_context(nc.sbuf_tensor(name, shape, dt))
        pb = lambda name, shape: ctx.enter_context(nc.psum_tensor(name, shape, F32))
        sem = m.sem
        xb = sb("xb", [P, 4, C], F32)
        st = sb("st", [P, 4, 6], F32)
        mv = sb("mv", [P, 4, 2], F32)
        rstd = sb("rstd", [P, 4, 1], F32)
        centred = sb("centred", [P, C], F32)
        spare = sb("spare_f", [P, 1], F32)
        h = sb("h", [P, 2, C], F32)
        ht = sb("ht", [P, 2, 2, KC, P], F16)
        k_sb = sb("k_sb", [P, 2, C], F32)
        vk_tmp = sb("vk_tmp", [P, GRP, VKW], F32)
        ps_t, ps_k, ps_v, ps_q = pb("ps_t", [P, KC, P]), pb("ps_k", [P, C]), pb("ps_v", [P, C]), pb("ps_q", [P, GRP, P])
        ps_vk = [pb(f"ps_vk{j}", [P, 2, P + 1]) for j in range(2)]
        sstage = sb("sstage", [P, 2, PIECE], F32)
        x_loaded = [sem(f"x_loaded{j}") for j in range(4)]
        s_loaded = [sem(f"s_loaded{j}") for j in range(2)]
        s_hi, s_lo = sem("s_hi"), sem("s_lo")
        bn_done, stats_ready, eps_added, rstd_ready = sem("bn_done"), sem("stats_ready"), sem("eps_added"), sem("rstd_ready")
        centred_ready, h_ready, t_done, ht_hi, ht_ready = sem("centred_ready"), sem("h_ready"), sem("t_done"), sem("ht_hi"), sem("ht_ready")
        k_done, v_done, q_done = sem("k_done"), sem("v_done"), sem("q_done")
        k_ready, v_ready, q_hi, q_ready = sem("k_ready"), sem("v_ready"), sem("q_hi"), sem("q_ready")
        vk_done, vk_step, vk_hi, vk_ready = sem("vk_done"), sem("vk_step"), sem("vk_hi"), sem("vk_ready")

        def there(b, c):
            return not isinstance(b, int) or 8 * b + c < TILES

        def over_batches(eng, slot):
            with eng.Fori(0, B - 1) as b:
                for c in range(1, BT + 1):
                    slot(b, c)
            for c in range(1, BT + 1):
                slot(B - 1, c)

        with nc.Block() as block:
            @block.sync
            def _(sp):
                def load(b, c):
                    if not there(b, c):
                        return
                    i = 8 * b + c
                    if not (isinstance(b, int) and i < 4):
                        sp.wait_ge(centred_ready, i - 3)
                    sp.dma_start(xb[:, c % 4, :], m.x[bass.ds(i * P, P), :]).then_inc(x_loaded[c % 4], 16)

                def load_piece(b, c):
                    if not there(b, c):
                        return
                    i = 8 * b + c
                    if not (isinstance(b, int) and i < 2):
                        sp.wait_ge(s_lo, i - 1)
                    sp.dma_start(sstage[:, c % 2, :], m.sh_flat[:, bass.ds(i * PIECE, PIECE)]).then_inc(s_loaded[c % 2], 16)

                def slot(b, c):
                    load(b, c + 3)
                    load_piece(b, c)

                for c in range(4):
                    load(0, c)
                load_piece(0, 0)
                over_batches(sp, slot)

            @block.gpsimd
            def _(pool):
                def reciprocal_deviation(b, c):
                    if not there(b, c):
                        return
                    i = 8 * b + c
                    pool.wait_ge(eps_added, i + 1)
                    pool.tensor_tensor(rstd[:, c % 4, :], rstd[:, c % 4, :], m.minus_half[:, :], ALU.pow).then_inc(rstd_ready, 1)

                for c in range(4):
                    reciprocal_deviation(0, c)
                over_batches(pool, lambda b, c: reciprocal_deviation(b, c + 3))

            @block.vector
            def _(v):
                def stats(b, c):
                    if not there(b, c):
                        return
                    i = 8 * b + c
                    v.wait_ge(x_loaded[c % 4], 16 * ((c // 4) + 1 + 2 * b))
                    if not (isinstance(b, int) and i < 4):
                        v.wait_ge(h_ready, i - 3)
                    v.bn_stats(st[:, c % 4, :], xb[:, c % 4, :]).then_inc(bn_done, 1)
                    v.wait_ge(bn_done, i + 1)
                    v.memset(spare[:, :], 0.0)
                    v.bn_aggr(mv[:, c % 4, :], st[:, c % 4, :]).then_inc(stats_ready, 1)
                    v.wait_ge(stats_ready, i + 1)
                    v.tensor_scalar(rstd[:, c % 4, :], mv[:, c % 4, 1:2], LN_EPS, None, ALU.add).then_inc(eps_added, 1)

                def normalise(b, c):
                    if not there(b, c):
                        return
                    i = 8 * b + c
                    batch = b + c // BT
                    v.wait_ge(stats_ready, i + 1)
                    if not (isinstance(b, int) and i < 1):
                        v.wait_ge(h_ready, i)
                    v.scalar_tensor_tensor(out=centred[:, :], in0=xb[:, c % 4, :], scalar=mv[:, c % 4, 0:1],
                                           in1=m.rows[:, batch, CA, :], op0=ALU.subtract, op1=ALU.mult).then_inc(centred_ready, 1)
                    v.wait_ge(rstd_ready, i + 1)
                    v.wait_ge(centred_ready, i + 1)
                    if not (isinstance(b, int) and i < 2):
                        v.wait_ge(t_done, i - 1)
                    v.scalar_tensor_tensor(out=h[:, c % 2, :], in0=centred[:, :], scalar=rstd[:, c % 4, :],
                                           in1=m.rows[:, batch, SA, :], op0=ALU.mult, op1=ALU.add).then_inc(h_ready, 1)

                def low_part(b, c):
                    if not there(b, c):
                        return
                    v.wait_ge(ht_hi, 8 * b + c + 1)
                    v.tensor_tensor(ht[:, c % 2, 1, :, :], ps_t[:, :, :], ht[:, c % 2, 0, :, :], ALU.subtract).then_inc(ht_ready, 1)

                def values(b, c):
                    if not there(b, c):
                        return
                    i = 8 * b + c
                    v.wait_ge(v_done, i + 1)
                    if not (isinstance(b, int) and i < 2):
                        v.wait_ge(vk_done, i - 1)
                    v.tensor_scalar(m.v_sb[:, c % 2, :, 0:P], ps_v[:, :].rearrange("p (g n) -> p g n", g=GRP),
                                    1.0 / SCALE, None, ALU.mult).then_inc(v_ready, 1)
                    v.wait_ge(q_hi, i + 1)
                    v.scalar_tensor_tensor(out=m.qt[:, i, 1, :, :], in0=ps_q[:, :, :], scalar=0.0, in1=m.qt[:, i, 0, :, :],
                                           op0=ALU.max, op1=ALU.subtract).then_inc(q_ready, 1)

                def key_value_sums(b):
                    v.wait_ge(vk_done, 8 * b + 8)
                    if not (isinstance(b, int) and b == 0):
                        v.wait_ge(vk_ready, 1 * b)
                    for g in range(GRP):
                        v.tensor_tensor(vk_tmp[:, g, 0:P], ps_vk[g // 2][:, g % 2, 0:P], m.head_mask[:, :], ALU.mult).then_inc(vk_step, 1)
                        v.tensor_scalar(vk_tmp[:, g, P:VKW], m.heads[:, :], ps_vk[g // 2][:, g % 2, P:P + 1], None, ALU.mult).then_inc(vk_step, 1)
                    v.wait_ge(vk_step, 8 * b + 8)
                    v.tensor_copy(m.vk[:, b, 0, :, :], vk_tmp[:, :, :]).then_inc(vk_hi, 1)
                    v.wait_ge(vk_hi, b + 1)
                    v.tensor_tensor(m.vk[:, b, 1, :, :], vk_tmp[:, :, :], m.vk[:, b, 0, :, :], ALU.subtract).then_inc(vk_ready, 1)

                def piece_low(b, c):
                    if not there(b, c):
                        return
                    i = 8 * b + c
                    v.wait_ge(s_hi, i + 1)
                    v.scalar_tensor_tensor(out=m.sh[:, 1, bass.ds(i * PIECE, PIECE)], in0=sstage[:, c % 2, :], scalar=SCALE,
                                           in1=m.sh[:, 0, bass.ds(i * PIECE, PIECE)], op0=ALU.mult, op1=ALU.subtract).then_inc(s_lo, 1)

                def slot(b, c):
                    stats(b, c + 3)
                    normalise(b, c + 2)
                    low_part(b, c + 1)
                    values(b, c)
                    piece_low(b, c)
                    if c == BT:
                        key_value_sums(b)

                stats(0, 0)
                stats(0, 1)
                stats(0, 2)
                normalise(0, 0)
                normalise(0, 1)
                low_part(0, 0)
                slot(0, 0)
                over_batches(v, slot)

            @block.scalar
            def _(act):
                def high_part(b, c):
                    if not there(b, c):
                        return
                    i = 8 * b + c
                    act.wait_ge(t_done, i + 1)
                    if not (isinstance(b, int) and i < 2):
                        act.wait_ge(q_done, i - 1)
                    act.activation(ht[:, c % 2, 0, :, :], ps_t[:, :, :], ACT.Copy).then_inc(ht_hi, 1)

                def slot(b, c):
                    high_part(b, c + 1)
                    if not there(b, c):
                        return
                    i = 8 * b + c
                    act.wait_ge(k_done, i + 1)
                    if not (isinstance(b, int) and i < 2):
                        act.wait_ge(vk_done, i - 1)
                    act.activation(k_sb[:, c % 2, :], ps_k[:, :], ACT.Relu, scale=1.0 / SCALE).then_inc(k_ready, 1)
                    act.wait_ge(q_done, i + 1)
                    act.activation(m.qt[:, i, 0, :, :], ps_q[:, :, :], ACT.Relu).then_inc(q_hi, 1)
                    act.wait_ge(s_loaded[c % 2], 16 * ((c // 2) + 1 + 4 * b))
                    act.activation(m.sh[:, 0, bass.ds(i * PIECE, PIECE)], sstage[:, c % 2, :], ACT.Copy, scale=SCALE).then_inc(s_hi, 1)

                high_part(0, 0)
                slot(0, 0)
                over_batches(act, slot)

            @block.tensor
            def _(pe):
                def transposes(b, c):
                    if not there(b, c):
                        return
                    i = 8 * b + c
                    pe.wait_ge(h_ready, i + 1)
                    if not (isinstance(b, int) and i < 1):
                        pe.wait_ge(ht_ready, i)
                    for k in range(KC):
                        mm = nc.tensor.transpose(ps_t[:, k, :], h[:, c % 2, k * P:(k + 1) * P], m.ident[:, :])
                    mm.then_inc(t_done, 1)

                def project(b, c):
                    if not there(b, c):
                        return
                    i = 8 * b + c
                    first = isinstance(b, int) and i == 0
                    hk = [(ht[:, c % 2, 0, k, :], ht[:, c % 2, 1, k, :]) for k in range(KC)]
                    w = lambda k, lo, n: (m.wqkv[:, k, 0, lo:lo + n], m.wqkv[:, k, 1, lo:lo + n])
                    pe.wait_ge(ht_ready, i + 1)
                    if not first:
                        pe.wait_ge(k_ready, i)
                    for k in range(KC):
                        mm = split_matmul(nc, ps_k[:, :], hk[k], w(k, C, C), k == 0, k == KC - 1)
                    mm.then_inc(k_done, 1)
                    if not first:
                        pe.wait_ge(v_ready, i)
                    for k in range(KC):
                        mm = split_matmul(nc, ps_v[:, :], hk[k], w(k, 2 * C, C), k == 0, k == KC - 1)
                    mm.then_inc(v_done, 1)
                    if not first:
                        pe.wait_ge(q_ready, i)
                    for g in range(GRP):
                        for k in range(KC):
                            mm = split_matmul(nc, ps_q[:, g, :], w(k, g * P, P), hk[k], k == 0, k == KC - 1)
                    mm.then_inc(q_done, 1)

                def sum_keys_values(b, c):
                    i = 8 * b + c
                    pe.wait_ge(k_ready, i + 1)
                    pe.wait_ge(v_ready, i + 1)
                    if c == 0 and not (isinstance(b, int) and b == 0):
                        pe.wait_ge(vk_ready, b)
                    for g in range(GRP):
                        mm = nc.tensor.matmul(ps_vk[g // 2][:, g % 2, :], k_sb[:, c % 2, g * P:(g + 1) * P],
                                              m.v_sb[:, c % 2, g, 0:P + 1], start=c == 0 and g % 2 == 0,
                                              stop=c == BT - 1, skip_group_check=True)
                    mm.then_inc(vk_done, 1)

                def slot(b, c):
                    transposes(b, c + 1)
                    project(b, c)
                    if c >= 1:
                        sum_keys_values(b, c - 1)

                transposes(0, 0)
                slot(0, 0)
                over_batches(pe, slot)


def back(nc, m):
    with ExitStack() as ctx:
        sb = lambda name, shape, dt: ctx.enter_context(nc.sbuf_tensor(name, shape, dt))
        pb = lambda name, shape: ctx.enter_context(nc.psum_tensor(name, shape, F32))
        sem = m.sem
        xr = sb("xr", [P, 2, C], F32)
        xg = sb("xg", [P, 2, C], F32)
        den = sb("den", [P, 4 * GRP], F32)
        o_sb = sb("o_sb", [P, 2, C], F32)
        ot = sb("ot", [P, 2, 2, KC, P], F16)
        x2 = sb("x2", [P, 2, C], F32)
        t1 = sb("t1", [P, C], F32)
        st = sb("st_b", [P, 2, 6], F32)
        mv = sb("mv_b", [P, 2, 2], F32)
        rstd = sb("rstd_b", [P, 2, 1], F32)
        centred = sb("centred_b", [P, 2, C], F32)
        spare = sb("spare_b", [P, 1], F32)
        h2 = sb("h2", [P, 2, C], F32)
        h2t = sb("h2t", [P, 2, 2, KC, P], F16)
        ps_o = [pb(f"ps_o{j}", [P, 2, VKW]) for j in range(2)]
        ps_y = [pb(f"ps_y{j}", [P, C]) for j in range(2)]
        ps_ot, ps_ht, ps_l = pb("ps_ot", [P, KC, P]), pb("ps_ht", [P, KC, P]), pb("ps_l", [P, E])
        m.rows = sb("rows_b", [P, B, 4, C], F32)
        rows_b0, rows_b = sem("rows_b0"), sem("rows_b")
        xr_loaded = [sem(f"xr_loaded{j}") for j in range(2)]
        xg_ready, o_done, den_ready, rden_ready, o_ready = sem("xg_ready"), sem("o_done"), sem("den_ready"), sem("rden_ready"), sem("o_ready")
        ot_done, ot_hi, ot_ready, y_done, t1_ready, x2_ready = sem("ot_done"), sem("ot_hi"), sem("ot_ready"), sem("y_done"), sem("t1_ready"), sem("x2_ready")
        bn2_done, stats2_ready, eps2_added, rstd2_ready = sem("bn2_done"), sem("stats2_ready"), sem("eps2_added"), sem("rstd2_ready")
        centred2_ready, scaled_ready, h2_ready, h2t_done, h2t_hi, h2t_ready = sem("centred2_ready"), sem("scaled_ready"), sem("h2_ready"), sem("h2t_done"), sem("h2t_hi"), sem("h2t_ready")
        l_done, l_ready = sem("l_done"), sem("l_ready")
        x2_stored = [sem(f"x2_stored{j}") for j in range(2)]
        h2_stored = [sem(f"h2_stored{j}") for j in range(2)]
        h2t_stored = [sem(f"h2t_stored{j}") for j in range(2)]
        LAG_Y, LAG_X2, LAG_H2, LAG_T, LAG_L = 2, 3, 4, 6, 7
        LAST = LAG_L + 1

        def there(t):
            return not isinstance(t, int) or 0 <= t < TILES

        def later(t, n):
            return not isinstance(t, int) or t >= n

        def over_tiles(eng, slot, rows=False):
            if rows:
                eng.wait_ge(rows_b0, 16 * 4)
            for i in range(LAST):
                slot(i, i)
            if rows:
                eng.wait_ge(rows_b, 16 * 4 * (B - 1))
            with eng.Fori(0, (TILES - LAST) // 2) as pair:
                for c in range(2):
                    slot(2 * pair + (LAST + c), LAST + c)
            for i in range(TILES, TILES + LAG_L):
                slot(i, i)

        def uses(t, c):
            return 16 * (t // 2 + 1)

        with nc.Block() as block:
            @block.sync
            def _(sp):
                for b in range(B):
                    for r, src in ((GA, m.mod_d[b, 2 * C:3 * C]), (GAB, m.gab_d[b, :]), (SB, m.mod_d[b, 3 * C:4 * C]),
                                   (CB, m.mod_d[b, 4 * C:5 * C])):
                        sp.dma_start(m.rows[:, b, r, :], src.partition_broadcast(P)).then_inc(rows_b if b else rows_b0, 16)

                def slot(t, c):
                    if there(t):
                        if later(t, 2):
                            sp.wait_ge(xg_ready, t - 1)
                        sp.dma_start(xr[:, c % 2, :], m.x[bass.ds(t * P, P), :]).then_inc(xr_loaded[c % 2], 16)
                    u, d = t - LAG_X2, c - LAG_X2
                    if there(u):
                        sp.wait_ge(x2_ready, u + 1)
                        sp.dma_start(m.x2_d[bass.ds(u * P, P), :], x2[:, d % 2, :]).then_inc(x2_stored[d % 2], 16)
                    u, d = t - LAG_H2 - 1, c - LAG_H2 - 1
                    if there(u):
                        sp.wait_ge(h2_ready, u + 1)
                        sp.dma_start(m.h2_d[bass.ds(u * P, P), :], h2[:, d % 2, :]).then_inc(h2_stored[d % 2], 16)
                    u, d = t - LAG_T, c - LAG_T
                    if there(u):
                        sp.wait_ge(h2t_ready, u + 1)
                        sp.dma_start(m.h2t_d[bass.ds(u, 1), :, :].rearrange("o p n -> (o p) n"),
                                     h2t[:, d % 2, :, :, :].rearrange("p s k n -> p (s k n)")).then_inc(h2t_stored[d % 2], 16)

                over_tiles(sp, slot)
                for s in x2_stored + h2_stored + h2t_stored:
                    sp.wait_ge(s, 16 * TILES // 2)

            @block.gpsimd
            def _(pool):
                def slot(t, c):
                    u, d = t - LAG_H2 - 1, c - LAG_H2 - 1
                    if there(u):
                        pool.wait_ge(scaled_ready, u + 1)
                        if later(u, 2):
                            pool.wait_ge(h2t_done, u - 1)
                            pool.wait_ge(h2_stored[d % 2], uses(u - 2, d))
                        pool.tensor_tensor(h2[:, d % 2, :], centred[:, d % 2, :], m.rows[:, u // BT, SB, :], ALU.add).then_inc(h2_ready, 1)
                    u, d = t - LAG_Y, c - LAG_Y
                    if there(u):
                        pool.wait_ge(xr_loaded[d % 2], uses(u, d))
                        if later(u, 2):
                            pool.wait_ge(x2_ready, u - 1)
                        pool.tensor_tensor(xg[:, d % 2, :], xr[:, d % 2, :], m.rows[:, u // BT, GAB, :], ALU.add).then_inc(xg_ready, 1)
                    u, d = t - LAG_X2, c - LAG_X2
                    if there(u):
                        pool.wait_ge(eps2_added, u + 1)
                        pool.tensor_tensor(rstd[:, d % 2, :], rstd[:, d % 2, :], m.minus_half[:, :], ALU.pow).then_inc(rstd2_ready, 1)

                over_tiles(pool, slot, rows=True)

            @block.vector
            def _(v):
                def divide(t, c):
                    v.wait_ge(o_done, t + 1)
                    if later(t, 1):
                        v.wait_ge(o_ready, 2 * t)
                    for j in range(2):
                        v.tensor_scalar(den[:, 8 * j:8 * j + 8].rearrange("p (g h) -> p g h", g=2), ps_o[j][:, :, P:VKW],
                                        DEN_EPS, None, ALU.add).then_inc(den_ready, 1)
                    v.wait_ge(den_ready, 2 * t + 2)
                    v.reciprocal(den[:, :], den[:, :]).then_inc(rden_ready, 1)
                    v.wait_ge(rden_ready, t + 1)
                    if later(t, 2):
                        v.wait_ge(ot_done, t - 1)
                    for j in range(2):
                        v.tensor_tensor(o_sb[:, c % 2, 2 * j * P:2 * (j + 1) * P].rearrange("p (g h e) -> p g h e", g=2, h=4),
                                        ps_o[j][:, :, 0:P].rearrange("p g (h e) -> p g h e", h=4),
                                        den[:, 8 * j:8 * j + 8].rearrange("p (g h) -> p g h", g=2).unsqueeze(3).to_broadcast([P, 2, 4, HEAD]),
                                        ALU.mult).then_inc(o_ready, 1)

                def slot(t, c):
                    if there(t):
                        divide(t, c)
                    u, d = t - 1, c - 1
                    if there(u):
                        v.wait_ge(ot_hi, u + 1)
                        v.tensor_tensor(ot[:, d % 2, 1, :, :], ps_ot[:, :, :], ot[:, d % 2, 0, :, :], ALU.subtract).then_inc(ot_ready, 1)
                    u, d = t - LAG_T, c - LAG_T
                    if there(u):
                        v.wait_ge(h2t_hi, u + 1)
                        v.tensor_tensor(h2t[:, d % 2, 1, :, :], ps_ht[:, :, :], h2t[:, d % 2, 0, :, :], ALU.subtract).then_inc(h2t_ready, 1)
                    u, d = t - LAG_X2, c - LAG_X2
                    if there(u):
                        v.wait_ge(y_done, u + 1)
                        if later(u, 1):
                            v.wait_ge(x2_ready, u)
                        v.scalar_tensor_tensor(out=t1[:, :], in0=ps_y[d % 2][:, :], scalar=1.0 / SCALE, in1=m.rows[:, u // BT, GA, :],
                                               op0=ALU.mult, op1=ALU.mult).then_inc(t1_ready, 1)
                        v.wait_ge(t1_ready, u + 1)
                        v.wait_ge(xg_ready, u + 1)
                        if later(u, 2):
                            v.wait_ge(centred2_ready, u - 1)
                            v.wait_ge(x2_stored[d % 2], uses(u - 2, d))
                        v.tensor_tensor(x2[:, d % 2, :], t1[:, :], xg[:, d % 2, :], ALU.add).then_inc(x2_ready, 1)
                        v.wait_ge(x2_ready, u + 1)
                        v.bn_stats(st[:, d % 2, :], x2[:, d % 2, :]).then_inc(bn2_done, 1)
                        v.wait_ge(bn2_done, u + 1)
                        if later(u, 2):
                            v.wait_ge(scaled_ready, u - 1)
                        v.memset(spare[:, :], 0.0)
                        v.bn_aggr(mv[:, d % 2, :], st[:, d % 2, :]).then_inc(stats2_ready, 1)
                        v.wait_ge(stats2_ready, u + 1)
                        v.tensor_scalar(rstd[:, d % 2, :], mv[:, d % 2, 1:2], LN_EPS, None, ALU.add).then_inc(eps2_added, 1)
                    u, d = t - LAG_H2, c - LAG_H2
                    if there(u):
                        v.wait_ge(stats2_ready, u + 1)
                        if later(u, 2):
                            v.wait_ge(h2_ready, u - 1)
                        v.scalar_tensor_tensor(out=centred[:, d % 2, :], in0=x2[:, d % 2, :], scalar=mv[:, d % 2, 0:1],
                                               in1=m.rows[:, u // BT, CB, :], op0=ALU.subtract, op1=ALU.mult).then_inc(centred2_ready, 1)

                over_tiles(v, slot, rows=True)

            @block.scalar
            def _(act):
                def slot(t, c):
                    u, d = t - 1, c - 1
                    if there(u):
                        act.wait_ge(ot_done, u + 1)
                        if later(u, 2):
                            act.wait_ge(y_done, u - 1)
                        act.activation(ot[:, d % 2, 0, :, :], ps_ot[:, :, :], ACT.Copy).then_inc(ot_hi, 1)
                    u, d = t - LAG_T, c - LAG_T
                    if there(u):
                        act.wait_ge(h2t_done, u + 1)
                        if later(u, 2):
                            act.wait_ge(l_done, u - 1)
                            act.wait_ge(h2t_stored[d % 2], uses(u - 2, d))
                        act.activation(h2t[:, d % 2, 0, :, :], ps_ht[:, :, :], ACT.Copy).then_inc(h2t_hi, 1)
                    u, d = t - LAG_L, c - LAG_L
                    if there(u):
                        act.wait_ge(l_done, u + 1)
                        act.activation(m.logits[:, u, :], ps_l[:, :], ACT.Copy, scale=1.0 / SCALE).then_inc(l_ready, 1)
                    u, d = t - LAG_H2, c - LAG_H2
                    if there(u):
                        act.wait_ge(centred2_ready, u + 1)
                        act.wait_ge(rstd2_ready, u + 1)
                        act.activation(centred[:, d % 2, :], centred[:, d % 2, :], ACT.Copy, scale=rstd[:, d % 2, :]).then_inc(scaled_ready, 1)

                over_tiles(act, slot)

            @block.tensor
            def _(pe):
                def slot(t, c):
                    if there(t):
                        if later(t, 1):
                            pe.wait_ge(o_ready, 2 * t)
                        for g in range(GRP):
                            mm = split_matmul(nc, ps_o[g // 2][:, g % 2, :], (m.qt[:, t, 0, g, :], m.qt[:, t, 1, g, :]),
                                              (m.vk[:, t // BT, 0, g, :], m.vk[:, t // BT, 1, g, :]), True, True)
                        mm.then_inc(o_done, 1)
                    u, d = t - 1, c - 1
                    if there(u):
                        pe.wait_ge(o_ready, 2 * u + 2)
                        if later(u, 1):
                            pe.wait_ge(ot_ready, u)
                        for k in range(KC):
                            mm = nc.tensor.transpose(ps_ot[:, k, :], o_sb[:, d % 2, k * P:(k + 1) * P], m.ident[:, :])
                        mm.then_inc(ot_done, 1)
                    u, d = t - LAG_T, c - LAG_T
                    if there(u):
                        pe.wait_ge(h2_ready, u + 1)
                        if later(u, 1):
                            pe.wait_ge(h2t_ready, u)
                        for k in range(KC):
                            mm = nc.tensor.transpose(ps_ht[:, k, :], h2[:, d % 2, k * P:(k + 1) * P], m.ident[:, :])
                        mm.then_inc(h2t_done, 1)
                    u, d = t - LAG_Y, c - LAG_Y
                    if there(u):
                        pe.wait_ge(ot_ready, u + 1)
                        if later(u, 2):
                            pe.wait_ge(t1_ready, u - 1)
                        for k in range(KC):
                            mm = split_matmul(nc, ps_y[d % 2][:, :], (ot[:, d % 2, 0, k, :], ot[:, d % 2, 1, k, :]),
                                              (m.wproj[:, k, 0, :], m.wproj[:, k, 1, :]), k == 0, k == KC - 1)
                        mm.then_inc(y_done, 1)
                    u, d = t - LAG_L, c - LAG_L
                    if there(u):
                        pe.wait_ge(h2t_ready, u + 1)
                        if later(u, 1):
                            pe.wait_ge(l_ready, u)
                        for k in range(KC):
                            mm = split_matmul(nc, ps_l[:, :], (h2t[:, d % 2, 0, k, :], h2t[:, d % 2, 1, k, :]),
                                              (m.gate[:, k, 0, :], m.gate[:, k, 1, :]), k == 0, k == KC - 1)
                        mm.then_inc(l_done, 1)

                over_tiles(pe, slot)


def carry_waits(pool, spare):
    pool.tensor_tensor(spare, spare, spare, ALU.add)


def shared_steps(nc, m, ctx, tag, first):
    sb = lambda name, shape, dt: ctx.enter_context(nc.sbuf_tensor(name + tag, shape, dt))
    sem = lambda name: m.sem(name + tag)
    CH = 2 * P
    s = Parts()
    ht = sb("s_ht", [P, 2, 2, 2, KC, P], F16)
    act_sb = sb("s_act", [P, 2, CH], F32)
    at = sb("s_at", [P, SH_TILES, 2, CH], F16)
    xs = sb("s_xs", [P, 2, C], F32)
    t1 = sb("s_t1", [P, C], F32)
    h3c = t1[:, 0:CH]
    s.xs = xs
    ps_h = [ctx.enter_context(nc.psum_tensor(f"s_ps_h{j}{tag}", [P, 2, CH], F32)) for j in range(2)]
    ps_y = [ctx.enter_context(nc.psum_tensor(f"s_ps_y{j}{tag}", [P, C], F32)) for j in range(2)]
    ht_loaded = [sem(f"s_ht_loaded{j}") for j in range(2)]
    up_done, silu_done, h3c_done, act_done, at_hi, at_ready = sem("s_up_done"), sem("s_silu"), sem("s_h3c"), sem("s_act"), sem("s_at_hi"), sem("s_at_ready")
    y_done, t1_done, xs_ready = sem("s_y_done"), sem("s_t1"), sem("s_xs_ready")
    xs_loaded = s.xs_loaded = [sem(f"s_xs_loaded{j}") for j in range(2)]
    xs_stored = s.xs_stored = [sem(f"s_xs_stored{j}") for j in range(2)]
    J = SH_TILES

    def is_first(n, j=0):
        return isinstance(n, int) and n == 0 and j == 0

    def load_h(sp, n, c):
        if not (isinstance(n, int) and n < 2):
            sp.wait_ge(up_done, J * (n - 1))
        for t in range(2):
            sp.dma_start(ht[:, c % 2, t, :, :, :].rearrange("p s k n -> p (s k n)"),
                         m.h2t_d[bass.ds(2 * (n + first) + t, 1), :, :].rearrange("o p n -> (o p) n")).then_inc(ht_loaded[c % 2], 16)

    def load_x(sp, n, c):
        for t in range(2):
            if not is_first(n):
                sp.wait_ge(xs_stored[t], 16 * n)
            sp.dma_start(xs[:, t, :], m.x2_d[bass.ds((2 * (n + first) + t) * P, P), :]).then_inc(xs_loaded[t], 16)

    def store_x(sp, n, c, to):
        for t in range(2):
            sp.wait_ge(xs_ready, 2 * n + t + 1)
            sp.dma_start(to[bass.ds((2 * (n + first) + t) * P, P), :], xs[:, t, :]).then_inc(xs_stored[t], 16)

    def activate(act, n, c, j):
        i = J * n + j
        act.wait_ge(up_done, i + 1)
        if not (isinstance(n, int) and i < 2):
            act.wait_ge(at_ready, i - 1)
        if j < J - 1:
            act.activation(act_sb[:, j % 2, :], ps_h[j % 2][:, 0, :], ACT.Silu, scale=1.0 / SCALE).then_inc(silu_done, 1)
        else:
            if not is_first(n):
                act.wait_ge(xs_ready, 2 * n)
            act.activation(h3c[0:SH_HALF, :], ps_h[j % 2][SH_HALF:P, 0, :], ACT.Copy, scale=1.0 / SCALE).then_inc(h3c_done, 1)
            act.activation(act_sb[0:SH_HALF, j % 2, :], ps_h[j % 2][0:SH_HALF, 0, :], ACT.Silu, scale=1.0 / SCALE).then_inc(silu_done, 1)

    def high(act, n, c, j):
        i = J * n + j
        w = P if j < J - 1 else SH_HALF
        act.wait_ge(act_done, i + 1)
        if j == 0 and not is_first(n):
            act.wait_ge(y_done, 2 * n)
        act.activation(at[0:w, j, 0, :], act_sb[0:w, j % 2, :], ACT.Copy).then_inc(at_hi, 1)

    def multiply(v, n, c, j):
        i = J * n + j
        v.wait_ge(silu_done, i + 1)
        if j < J - 1:
            v.scalar_tensor_tensor(out=act_sb[:, j % 2, :], in0=ps_h[j % 2][:, 1, :], scalar=1.0 / SCALE,
                                   in1=act_sb[:, j % 2, :], op0=ALU.mult, op1=ALU.mult).then_inc(act_done, 1)
        else:
            v.wait_ge(h3c_done, n + 1)
            v.tensor_tensor(act_sb[0:SH_HALF, j % 2, :], h3c[0:SH_HALF, :], act_sb[0:SH_HALF, j % 2, :], ALU.mult).then_inc(act_done, 1)

    def low(v, n, c, j):
        w = P if j < J - 1 else SH_HALF
        v.wait_ge(at_hi, J * n + j + 1)
        v.tensor_tensor(at[0:w, j, 1, :], act_sb[0:w, j % 2, :], at[0:w, j, 0, :], ALU.subtract).then_inc(at_ready, 1)

    def add(v, n, c, t):
        i = 2 * n + t
        v.wait_ge(y_done, i + 1)
        v.wait_ge(act_done, J * (n + 1))
        if not is_first(n, t):
            v.wait_ge(xs_ready, i)
        v.scalar_tensor_tensor(out=t1[:, :], in0=ps_y[t][:, :], scalar=1.0 / SCALE, in1=s.gb_row(n),
                               op0=ALU.mult, op1=ALU.mult).then_inc(t1_done, 1)
        v.wait_ge(t1_done, i + 1)
        s.wait_x(v, n, t)
        v.tensor_tensor(xs[:, t, :], t1[:, :], xs[:, t, :], ALU.add).then_inc(xs_ready, 1)

    def up(pe, n, c, j):
        i = J * n + j
        if j == 0:
            pe.wait_ge(ht_loaded[c % 2], 32 * (n // 2 + 1))
        if not (isinstance(n, int) and i < 2):
            pe.wait_ge(act_done, i - 1)
        parts = 2 if j < J - 1 else 1
        for part in range(parts):
            for k in range(KC):
                lo = k * 2 * SHARED + (2 * j + part) * P
                mm = split_matmul(nc, ps_h[j % 2][:, part, :].rearrange("p (t n) -> p t n", t=2),
                                  (m.sh[:, 0, lo:lo + P], m.sh[:, 1, lo:lo + P]),
                                  (ht[:, c % 2, :, 0, k, :], ht[:, c % 2, :, 1, k, :]), k == 0, k == KC - 1)
        mm.then_inc(up_done, 1)

    def down(pe, n, c):
        for j0, j1 in ((0, J - 1), (J - 1, J)):
            pe.wait_ge(at_ready, J * n + j1)
            for t in range(2):
                if j0 == 0 and not is_first(n):
                    pe.wait_ge(t1_done, 2 * n - 1 + t)
                for j in range(j0, j1):
                    w = P if j < J - 1 else SH_HALF
                    lo = KC * 2 * SHARED + j * C
                    tok = slice(t * P, (t + 1) * P)
                    mm = split_matmul(nc, ps_y[t][:, :], (at[0:w, j, 0, tok], at[0:w, j, 1, tok]),
                                      (m.sh[0:w, 0, lo:lo + C], m.sh[0:w, 1, lo:lo + C]), j == 0, j == J - 1)
                if j1 == J:
                    mm.then_inc(y_done, 1)

    s.load_h, s.load_x, s.store_x, s.activate, s.high, s.multiply, s.low, s.add, s.up, s.down = (
        load_h, load_x, store_x, activate, high, multiply, low, add, up, down)
    return s


def route(nc, m):
    with ExitStack() as ctx:
        sb = lambda name, shape, dt: ctx.enter_context(nc.sbuf_tensor(name, shape, dt))
        sem = m.sem
        s = shared_steps(nc, m, ctx, "_b", 0)
        gb = sb("gb_b", [P, 2, C], F32)
        s.gb_row = lambda n: gb[:, n // 4, :]
        s.wait_x = lambda v, n, t: v.wait_ge(s.xs_loaded[t], 16 * (n + 1))
        RING = 4
        stage = sb("w_stage", [P, RING, C], F32)
        bias = sb("bias", [P, E], F32)
        places = {e: [m.w2[:, e, :, :, :].rearrange("p k s n -> p (k s n)"), 0] for e in (E - 2, E - 1)}

        def view(e, shape, dt, rows=P):
            flat, used = places[e]
            size = shape[0] * (shape[1] if len(shape) > 1 else 1) * (shape[2] if len(shape) > 2 else 1) * (1 if dt == F16 else 2)
            places[e][1] += size
            assert places[e][1] <= 3 * 2 * C
            piece = flat[0:rows, used:used + size]
            piece = piece if dt == F16 else piece.bitcast(dt)
            names = "abc"[:len(shape)]
            return piece.rearrange(f"p ({' '.join(names)}) -> p {' '.join(names)}", **dict(zip(names, shape)))

        scores = view(E - 1, (TILES, E), F32)
        sel = view(E - 1, (TILES, E), F32)
        top = view(E - 1, (TILES, 8), F32)
        index = view(E - 1, (TILES, 8), U32)
        choice = view(E - 1, (TOP, TILES, E), F32)
        both = view(E - 2, (TILES, E), F16)
        before = view(E - 2, (P,), F16)
        ones = view(E - 2, (P,), F16)
        passed = view(E - 2, (SLOT_TILES, E), F32, 1)
        indexf = view(E - 2, (TOP, TILES), F32)
        expert_no = sb("expert_no", [P, E], F32)
        onesf = sb("onesf", [P, TILES], F32)
        wsum = view(E - 2, (TILES,), F32)
        count_i = sb("count_i", [P, E], I32)
        padded = sb("padded", [P, E], F32)
        ends = sb("ends", [P, E], F32)
        starts = sb("starts", [P, E], F32)
        slotf = view(E - 2, (TOP, TILES), F32)
        tile_at = view(E - 2, (SLOT_TILES,), F32, 1)
        eidf = view(E - 2, (SLOT_TILES,), F32, 1)
        token = sb("token", [P, TILES], I32)
        entry = sb("entry", [P, TOP, TILES], I32)
        entry_tile = sb("entry_tile", [P, TOP, TILES], I32)
        sc_idx = sb("sc_idx", [P, 2 * TOP, 1], I32)
        sc_tok = sb("sc_tok", [P, 2 * TOP, 1], I32)
        ps_r = ctx.enter_context(nc.psum_tensor("ps_r", [P, 2, TILES * E], F32))
        gb_loaded = sem("gb_loaded")
        w_loaded = [sem(f"w_loaded{j}") for j in range(RING)]
        w_hi, w_lo = sem("w_hi"), sem("w_lo")
        scores_ready, r_step, both_ready, ranks_done = sem("scores_ready"), sem("r_step"), sem("both_ready"), sem("ranks_done")
        consts, slots_ready = sem("consts"), sem("slots_ready")
        idx_copied = sem("idx_copied")
        scattered = [sem(f"scattered{j}") for j in range(2)]
        table_loaded = sem("table_loaded")
        CHUNKS = TILES // 4
        WP = 2 * KC + 3
        TURN = WP + 1

        def piece(e, q):
            if q < 2 * KC:
                k, which = q // 2, q % 2
                src = (m.w1_d, m.w3_d)[which][bass.ds(e, 1), k * P:(k + 1) * P, :].rearrange("o p n -> (o p) n")
                return src, m.w13[:, e, k, :, which * INTER:(which + 1) * INTER], P, INTER
            k = q - 2 * KC
            rows = min(P, INTER - k * P)
            src = m.w2_d[bass.ds(e, 1), k * P:k * P + rows, :].rearrange("o p n -> (o p) n")
            return src, m.w2[0:rows, e, k, :, :], rows, C

        def over_chunks(eng, chunk):
            for n in (0, 1):
                chunk(n, n)
            with eng.Fori(1, CHUNKS // 2 - 1) as pair:
                for c in range(2):
                    chunk(2 * pair + c, c)
            for c in range(2):
                chunk(CHUNKS - 2 + c, c)

        def pieces_beside(j):
            return range(2 * j, 2 * j + 2)

        with nc.Block() as block:
            @block.sync
            def _(sp):
                for b in range(2):
                    sp.dma_start(gb[:, b, :], m.mod_d[b, 5 * C:6 * C].partition_broadcast(P)).then_inc(gb_loaded, 16)
                sp.dma_start(bias[:, :], m.router_bias.partition_broadcast(P)).then_inc(gb_loaded, 16)
                s.load_h(sp, 0, 0)

                def chunk(n, c):
                    if not (isinstance(n, int) and n == CHUNKS - 1):
                        s.load_h(sp, n + 1, c + 1)
                    s.load_x(sp, n, c)
                    s.store_x(sp, n, c, m.x2s_d)

                over_chunks(sp, chunk)
                for t in range(2):
                    sp.wait_ge(s.xs_stored[t], 16 * CHUNKS)

            @block.scalar
            def _(act):
                def load_piece(n, q):
                    if q >= RING:
                        act.wait_ge(w_lo, WP * n + q - RING + 1)
                    elif not (isinstance(n, int) and n == 0):
                        last = max(range(q, WP, RING))
                        act.wait_ge(w_lo, WP * n - WP + last + 1)
                    src, _, rows, cols = piece(n, q)
                    act.dma_start(stage[0:rows, q % RING, 0:cols], src).then_inc(w_loaded[q % RING], 16)

                def piece_high(n, q):
                    if q + RING - 1 < WP:
                        load_piece(n, q + RING - 1)
                    elif q + RING - 1 >= TURN and not (isinstance(n, int) and n == CHUNKS - 1):
                        load_piece(n + 1, q + RING - 1 - TURN)
                    if q == WP:
                        return
                    _, dst, rows, cols = piece(n, q)
                    act.wait_ge(w_loaded[q % RING], 16 * (n * len(range(q % RING, WP, RING)) + q // RING + 1))
                    act.activation(dst[:, 0, :], stage[0:rows, q % RING, 0:cols], ACT.Copy, scale=SCALE).then_inc(w_hi, 1)

                def chunk(n, c):
                    for j in range(SH_TILES):
                        s.activate(act, n, c, j)
                        s.high(act, n, c, j)
                        for q in pieces_beside(j):
                            piece_high(n, q)

                for q in range(RING - 1):
                    load_piece(0, q)
                act.activation(scores[:, :, :], m.logits[:, :, :], ACT.Sigmoid).then_inc(scores_ready, 1)
                over_chunks(act, chunk)

            @block.vector
            def _(v):
                steps = 0

                def step(instruction):
                    nonlocal steps
                    steps += 1
                    instruction.then_inc(r_step, 1)
                    v.wait_ge(r_step, steps)

                def find_top():
                    v.wait_ge(scores_ready, 1)
                    v.wait_ge(gb_loaded, 48)
                    step(v.tensor_tensor(sel[:, :, :], scores[:, :, :], bias[:, :].unsqueeze(1).to_broadcast([P, TILES, E]), ALU.add))
                    nonlocal steps
                    for t in range(TILES):
                        v.max(top[:, t, :], sel[:, t, :]).then_inc(r_step, 1)
                    steps += TILES
                    v.wait_ge(r_step, steps)

                def find_index():
                    nonlocal steps
                    for t in range(TILES):
                        v.max_index(index[:, t, :], top[:, t, :], sel[:, t, :]).then_inc(r_step, 1)
                    steps += TILES
                    v.wait_ge(r_step, steps)

                def weigh():
                    v.wait_ge(consts, 5)
                    for k in range(TOP):
                        step(v.tensor_copy(indexf[:, k, :], index[:, :, k]))
                        step(v.tensor_tensor(choice[:, k, :, :], expert_no[:, :].unsqueeze(1).to_broadcast([P, TILES, E]),
                                             indexf[:, k, :].unsqueeze(2).to_broadcast([P, TILES, E]), ALU.is_equal))
                        step(v.tensor_tensor(sel[:, :, :], choice[:, k, :, :], scores[:, :, :], ALU.mult))
                        step(v.reduce_sum(m.weight[:, k, :], sel[:, :, :], AX.X))
                    step(v.tensor_tensor(wsum[:, :], m.weight[:, 0, :], m.weight[:, 1, :], ALU.add))
                    step(v.tensor_scalar(wsum[:, :], wsum[:, :], SUM_EPS, None, ALU.max))
                    step(v.reciprocal(wsum[:, :], wsum[:, :]))
                    for k in range(TOP):
                        step(v.tensor_tensor(m.weight[:, k, :], m.weight[:, k, :], wsum[:, :], ALU.mult))
                    v.tensor_tensor(both[:, :, :], choice[:, 0, :, :], choice[:, 1, :, :], ALU.add).then_inc(both_ready, 1)

                def place():
                    v.wait_ge(ranks_done, 2)
                    rank = ps_r[:, 0, :].rearrange("p (t e) -> p t e", e=E)
                    total = ps_r[:, 1, :].rearrange("p (t e) -> p e t", e=E)
                    pos = sel
                    run = top[:, :, :].rearrange("p t e -> p (t e)").rearrange("p (e t) -> p e t", e=E)
                    for e in range(E):
                        step(v.tensor_tensor_scan(run[:, e, :], onesf[:, :], total[:, e, :], 0.0, ALU.mult, ALU.add))
                    step(v.tensor_scalar(padded[:, :], run[:, :, TILES - 1], float(P - 1), None, ALU.add))
                    step(v.tensor_copy(count_i[:, :], padded[:, :]))
                    step(v.tensor_scalar(count_i[:, :], count_i[:, :], -P, None, ALU.bitwise_and))
                    step(v.tensor_copy(padded[:, :], count_i[:, :]))
                    step(v.tensor_tensor_scan(ends[:, :], onesf[:, 0:E], padded[:, :], 0.0, ALU.mult, ALU.add))
                    step(v.tensor_tensor(starts[:, :], ends[:, :], padded[:, :], ALU.subtract))
                    step(v.tensor_tensor(run, run, starts[:, :].unsqueeze(2).to_broadcast([P, E, TILES]), ALU.add))
                    step(v.tensor_tensor(run, run, total, ALU.subtract))
                    step(v.tensor_tensor(pos[:, :, :], rank, run.rearrange("p e t -> p t e"), ALU.add))
                    for k in range(TOP):
                        step(v.tensor_tensor(scores[:, :, :], choice[:, k, :, :], pos[:, :, :], ALU.mult))
                        step(v.reduce_sum(slotf[:, k, :], scores[:, :, :], AX.X))
                    step(v.tensor_copy(m.slot[:, :, :], slotf[:, :, :]))
                    step(v.tensor_scalar(entry[:, :, :], m.slot[:, :, :], P - 1, None, ALU.bitwise_and))
                    step(v.tensor_scalar(entry[:, :, :], entry[:, :, :], float(SLOT_TILES), None, ALU.mult))
                    step(v.tensor_scalar(entry_tile[:, :, :], m.slot[:, :, :], P.bit_length() - 1, None, ALU.logical_shift_right))
                    v.tensor_tensor(entry[:, :, :], entry[:, :, :], entry_tile[:, :, :], ALU.add).then_inc(slots_ready, 1)
                    step(v.tensor_tensor(passed[:, :, :], ends[0:1, :].unsqueeze(1).to_broadcast([1, SLOT_TILES, E]),
                                         tile_at[:, :].unsqueeze(2).to_broadcast([1, SLOT_TILES, E]), ALU.is_le))
                    step(v.reduce_sum(eidf[:, :], passed[:, :, :], AX.X))
                    step(v.tensor_scalar(eidf[:, :], eidf[:, :], float(E - 1), None, ALU.min))
                    step(v.tensor_copy(m.eid[:, :], eidf[:, :]))

                def piece_low(n, c, q):
                    _, dst, rows, cols = piece(n, q)
                    v.wait_ge(w_hi, WP * n + q + 1)
                    v.scalar_tensor_tensor(out=dst[:, 1, :], in0=stage[0:rows, q % RING, 0:cols], scalar=SCALE, in1=dst[:, 0, :],
                                           op0=ALU.mult, op1=ALU.subtract).then_inc(w_lo, 1)

                def chunk(n, c):
                    for j in range(SH_TILES):
                        s.multiply(v, n, c, j)
                        s.low(v, n, c, j)
                        for q in pieces_beside(j):
                            if q < WP:
                                piece_low(n, c, q)
                        if isinstance(n, int):
                            if (n, j) in beside:
                                beside[n, j]()
                    for t in range(2):
                        s.add(v, n, c, t)

                beside = {(0, 0): find_top, (0, 1): find_index, (0, 2): weigh, (1, 0): place}
                over_chunks(v, chunk)

            @block.tensor
            def _(pe):
                def chunk(n, c):
                    for j in range(SH_TILES):
                        s.up(pe, n, c, j)
                    s.down(pe, n, c)
                    if isinstance(n, int) and n == 0:
                        pe.wait_ge(both_ready, 1)
                        pe.wait_ge(consts, 6)
                        for part, lhs in ((0, before), (1, ones)):
                            nc.tensor.matmul(ps_r[:, part, :], lhs[:, :], both[:, :, :].rearrange("p t e -> p (t e)"),
                                             start=True, stop=True).then_inc(ranks_done, 1)

                over_chunks(pe, chunk)

            @block.gpsimd
            def _(pool):
                pool.iota(expert_no[:, :], [[1, E]], base=0, channel_multiplier=0, allow_small_or_imprecise_dtypes=True).then_inc(consts, 1)
                pool.iota(tile_at[:, :], [[P, SLOT_TILES]], base=0, channel_multiplier=0, allow_small_or_imprecise_dtypes=True).then_inc(consts, 1)
                pool.iota(token[:, :], [[P, TILES]], base=0, channel_multiplier=1).then_inc(consts, 1)
                pool.memset(ones[:, :], 1.0).then_inc(consts, 1)
                pool.memset(onesf[:, :], 1.0).then_inc(consts, 1)
                pool.wait_ge(consts, 5)
                pool.affine_select(out=before[:, :], in_=ones[:, :], compare_op=ALU.is_gt, fill=0.0,
                                   base=0, pattern=[[1, P]], channel_multiplier=-1).then_inc(consts, 1)
                pool.wait_ge(consts, 6)
                pool.wait_ge(slots_ready, 1)

                def scatter(pair, c, k):
                    t, r = 2 * pair + c, TOP * c + k
                    if k == 0 and not (isinstance(pair, int) and pair == 0):
                        pool.wait_ge(scattered[c], 16 * TOP * pair)
                    pool.tensor_copy(sc_idx[:, r, :], entry[:, k, bass.ds(t, 1)]).then_inc(idx_copied, 1)
                    pool.tensor_copy(sc_tok[:, r, :], token[:, bass.ds(t, 1)]).then_inc(idx_copied, 1)
                    pool.wait_ge(idx_copied, 2 * (TOP * t + k + 1))
                    carry_waits(pool, m.spare[:, :])
                    pool.indirect_dma_start(m.table, bass.IndirectOffsetOnAxis(ap=sc_idx[:, r, :], axis=0),
                                            sc_tok[:, r, :], None).then_inc(scattered[c], 16)

                for c in range(2):
                    for k in range(TOP):
                        scatter(0, c, k)
                with pool.Fori(1, TILES // 2) as pair:
                    for c in range(2):
                        for k in range(TOP):
                            scatter(pair, c, k)
                for c in range(2):
                    pool.wait_ge(scattered[c], 16 * TOP * TILES // 2)
                pool.dma_start(m.slot_token[:, :], m.table.rearrange("(p t) o -> p (t o)", p=P)).then_inc(table_loaded, 16)
                pool.wait_ge(table_loaded, 16)


def experts(nc, m):
    with ExitStack() as ctx:
        sb = lambda name, shape, dt: ctx.enter_context(nc.sbuf_tensor(name, shape, dt))
        pb = lambda name, shape: ctx.enter_context(nc.psum_tensor(name, shape, F32))
        sem = m.sem
        IT = 3
        g_idx = sb("g_idx", [P, 2, 1], I32)
        g = sb("g", [P, 2, C], F32)
        xt = sb("xt", [P, 2, 2, KC, P], F16)
        a = sb("a", [P, 2, IT * P], F32)
        at = sb("at", [P, 2, 2, IT, P], F16)
        y = sb("y", [P, 2, C], F32)
        ps_x, ps_h1, ps_h3, ps_a, ps_y = pb("ps_x", [P, KC, P]), pb("ps_h1", [P, INTER]), pb("ps_h3", [P, INTER]), pb("ps_a", [P, IT, P]), pb("ps_ey", [P, C])
        g_idx_copied = sem("g_idx_copied")
        gathered = [sem(f"gathered{j}") for j in range(2)]
        xt_done, xt_hi, xt_ready, h1_done, h3_done = sem("xt_done"), sem("xt_hi"), sem("xt_ready"), sem("h1_done"), sem("h3_done")
        e_silu, e_act, a_padded, at_done, e_at_hi, e_at_ready = sem("e_silu"), sem("e_act"), sem("a_padded"), sem("at_done"), sem("e_at_hi"), sem("e_at_ready")
        ey_done, ey_ready = sem("ey_done"), sem("ey_ready")
        y_stored = [sem(f"y_stored{j}") for j in range(2)]

        def later(t, n):
            return not isinstance(t, int) or t >= n

        def there(t):
            return not isinstance(t, int) or 0 <= t < SLOT_TILES

        def over_tiles(eng, slot):
            for t in (0, 1):
                slot(t, t)
            with eng.Fori(1, (SLOT_TILES - 1) // 2) as pair:
                for c in range(2):
                    slot(2 * pair + c, c)
            for t in range(SLOT_TILES - 1 - (SLOT_TILES - 1) % 2, SLOT_TILES + 1):
                slot(t, t)

        with nc.Block() as block:
            @block.gpsimd
            def _(pool):
                def gather(t, c):
                    if not there(t):
                        return
                    if later(t, 2):
                        pool.wait_ge(gathered[c % 2], 16 * (t // 2))
                        pool.wait_ge(xt_done, t - 1)
                    pool.tensor_copy(g_idx[:, c % 2, :], m.slot_token[:, bass.ds(t, 1)]).then_inc(g_idx_copied, 1)
                    pool.wait_ge(g_idx_copied, t + 1)
                    carry_waits(pool, m.spare[:, :])
                    pool.indirect_dma_start(g[:, c % 2, :], None, m.h2_d,
                                            bass.IndirectOffsetOnAxis(ap=g_idx[:, c % 2, :], axis=0)).then_inc(gathered[c % 2], 16)

                over_tiles(pool, gather)

            @block.sync
            def _(sp):
                def slot(t, c):
                    u, d = t - 1, c - 1
                    if there(u):
                        sp.wait_ge(ey_ready, u + 1)
                        sp.dma_start(m.y_d[bass.ds(u * P, P), :], y[:, d % 2, :]).then_inc(y_stored[d % 2], 16)

                over_tiles(sp, slot)
                sp.wait_ge(y_stored[0], 16 * ((SLOT_TILES + 1) // 2))
                sp.wait_ge(y_stored[1], 16 * (SLOT_TILES // 2))

            @block.scalar
            def _(act):
                def x_high(t, c):
                    if not there(t):
                        return
                    act.wait_ge(xt_done, t + 1)
                    if later(t, 2):
                        act.wait_ge(h3_done, t - 1)
                    act.activation(xt[:, c % 2, 0, :, :], ps_x[:, :, :], ACT.Copy).then_inc(xt_hi, 1)

                def slot(t, c):
                    u, d = t - 1, c - 1
                    if there(u):
                        act.wait_ge(at_done, u + 1)
                        if later(u, 2):
                            act.wait_ge(ey_done, u - 1)
                        act.activation(at[:, d % 2, 0, :, :], ps_a[:, :, :], ACT.Copy).then_inc(e_at_hi, 1)
                    x_high(t + 1, c + 1)
                    if there(t):
                        act.wait_ge(h1_done, t + 1)
                        if later(t, 2):
                            act.wait_ge(at_done, t - 1)
                        act.activation(a[:, c % 2, 0:INTER], ps_h1[:, :], ACT.Silu, scale=1.0 / SCALE).then_inc(e_silu, 1)
                    if there(u):
                        act.wait_ge(ey_done, u + 1)
                        if later(u, 2):
                            act.wait_ge(y_stored[d % 2], 16 * (u // 2))
                        act.activation(y[:, d % 2, :], ps_y[:, :], ACT.Copy, scale=1.0 / SCALE).then_inc(ey_ready, 1)

                x_high(0, 0)
                over_tiles(act, slot)

            @block.vector
            def _(v):
                v.memset(a[:, :, INTER:IT * P], 0.0).then_inc(a_padded, 1)

                def x_low(t, c):
                    if not there(t):
                        return
                    v.wait_ge(xt_hi, t + 1)
                    v.tensor_tensor(xt[:, c % 2, 1, :, :], ps_x[:, :, :], xt[:, c % 2, 0, :, :], ALU.subtract).then_inc(xt_ready, 1)

                def slot(t, c):
                    u, d = t - 1, c - 1
                    if there(u):
                        v.wait_ge(e_at_hi, u + 1)
                        v.tensor_tensor(at[:, d % 2, 1, :, :], ps_a[:, :, :], at[:, d % 2, 0, :, :], ALU.subtract).then_inc(e_at_ready, 1)
                    x_low(t + 1, c + 1)
                    if there(t):
                        v.wait_ge(h3_done, t + 1)
                        v.wait_ge(e_silu, t + 1)
                        v.scalar_tensor_tensor(out=a[:, c % 2, 0:INTER], in0=ps_h3[:, :], scalar=1.0 / SCALE, in1=a[:, c % 2, 0:INTER],
                                               op0=ALU.mult, op1=ALU.mult).then_inc(e_act, 1)

                x_low(0, 0)
                over_tiles(v, slot)

            @block.tensor
            def _(pe):
                def transpose_x(t, c):
                    if not there(t):
                        return
                    pe.wait_ge(gathered[c % 2], 16 * (t // 2 + 1))
                    if later(t, 1):
                        pe.wait_ge(xt_ready, t)
                    for k in range(KC):
                        mm = nc.tensor.transpose(ps_x[:, k, :], g[:, c % 2, k * P:(k + 1) * P], m.ident[:, :])
                    mm.then_inc(xt_done, 1)

                def up(t, c):
                    expert = pe.value_load(m.eid[0:1, bass.ds(t, 1)], min_val=0, max_val=E - 1)
                    pe.wait_ge(xt_ready, t + 1)
                    for which, ps, done in ((0, ps_h1, h1_done), (1, ps_h3, h3_done)):
                        if later(t, 1):
                            pe.wait_ge(e_act, t)
                        cols = slice(which * INTER, (which + 1) * INTER)
                        for k in range(KC):
                            mm = split_matmul(nc, ps[:, :], (xt[:, c % 2, 0, k, :], xt[:, c % 2, 1, k, :]),
                                              (m.w13[:, bass.ds(expert, 1), k, 0, cols].rearrange("p o n -> p (o n)"),
                                               m.w13[:, bass.ds(expert, 1), k, 1, cols].rearrange("p o n -> p (o n)")),
                                              k == 0, k == KC - 1)
                        mm.then_inc(done, 1)

                def transpose_a(t, c):
                    pe.wait_ge(a_padded, 1)
                    pe.wait_ge(e_act, t + 1)
                    if later(t, 1):
                        pe.wait_ge(e_at_ready, t)
                    for k in range(IT):
                        mm = nc.tensor.transpose(ps_a[:, k, :], a[:, c % 2, k * P:(k + 1) * P], m.ident[:, :])
                    mm.then_inc(at_done, 1)

                def down(t, c):
                    expert = pe.value_load(m.eid[0:1, bass.ds(t, 1)], min_val=0, max_val=E - 1)
                    pe.wait_ge(e_at_ready, t + 1)
                    if later(t, 1):
                        pe.wait_ge(ey_ready, t)
                    for k in range(IT):
                        w = min(P, INTER - k * P)
                        mm = split_matmul(nc, ps_y[:, :], (at[0:w, c % 2, 0, k, :], at[0:w, c % 2, 1, k, :]),
                                          (m.w2[0:w, bass.ds(expert, 1), k, 0, :].rearrange("p o n -> p (o n)"),
                                           m.w2[0:w, bass.ds(expert, 1), k, 1, :].rearrange("p o n -> p (o n)")),
                                          k == 0, k == IT - 1)
                    mm.then_inc(ey_done, 1)

                def slot(t, c):
                    if there(t - 1):
                        transpose_a(t - 1, c - 1)
                    transpose_x(t + 1, c + 1)
                    if there(t):
                        up(t, c)
                    if there(t - 1):
                        down(t - 1, c - 1)

                transpose_x(0, 0)
                over_tiles(pe, slot)


def combine(nc, m):
    with ExitStack() as ctx:
        sb = lambda name, shape, dt: ctx.enter_context(nc.sbuf_tensor(name, shape, dt))
        sem = m.sem
        CHUNKS = TILES // 4
        PER = 4
        s = shared_steps(nc, m, ctx, "_d", CHUNKS)
        gb = sb("gb_d", [P, B, C], F32)
        s.gb_row = lambda n: gb[:, (n + CHUNKS) // 4, :]
        y_idx = sb("y_idx", [P, PER, TOP, 1], I32)
        y = sb("y_rows", [P, PER, TOP, C], F32)
        xc = sb("xc", [P, 2, C], F32)
        gb_loaded = sem("gb_loaded_d")
        y_idx_copied, combined, merged, c_step = sem("y_idx_copied"), sem("combined"), sem("merged"), sem("c_step")
        y_loaded = [sem(f"y_loaded{j}") for j in range(PER)]
        out_stored = [sem(f"out_stored{j}") for j in range(2)]
        s.wait_x = lambda v, n, t: v.wait_ge(merged, 2 * n + t + 1)

        def tile(n, j):
            return 2 * n + j if j < 2 else 2 * n + j - 2 + TILES // 2

        def over_chunks(eng, chunk):
            for n in (0, 1):
                chunk(n, n)
            with eng.Fori(1, CHUNKS // 2 - 1) as pair:
                for c in range(2):
                    chunk(2 * pair + c, c)
            for c in range(2):
                chunk(CHUNKS - 2 + c, c)

        with nc.Block() as block:
            @block.sync
            def _(sp):
                for b in range(B):
                    sp.dma_start(gb[:, b, :], m.mod_d[b, 5 * C:6 * C].partition_broadcast(P)).then_inc(gb_loaded, 16)
                s.load_h(sp, 0, 0)

                def chunk(n, c):
                    if not (isinstance(n, int) and n == CHUNKS - 1):
                        s.load_h(sp, n + 1, c + 1)
                    s.load_x(sp, n, c)
                    s.store_x(sp, n, c, m.out)

                over_chunks(sp, chunk)
                for t in range(2):
                    sp.wait_ge(s.xs_stored[t], 16 * CHUNKS)

            @block.gpsimd
            def _(pool):
                def fetch(n, j):
                    if not (isinstance(n, int) and n == 0):
                        if j < 2:
                            pool.wait_ge(out_stored[j], 16 * n)
                        else:
                            pool.wait_ge(merged, 2 * n + j - 3)
                    for k in range(TOP):
                        pool.tensor_copy(y_idx[:, j, k, :], m.slot[:, k, bass.ds(tile(n, j), 1)]).then_inc(y_idx_copied, 1)
                    pool.wait_ge(y_idx_copied, TOP * (PER * n + j + 1))
                    carry_waits(pool, m.spare[:, :])
                    for k in range(TOP):
                        pool.indirect_dma_start(y[:, j, k, :], None, m.y_d,
                                                bass.IndirectOffsetOnAxis(ap=y_idx[:, j, k, :], axis=0)).then_inc(y_loaded[j], 16)
                    if j < 2:
                        pool.dma_start(xc[:, j, :], m.x2s_d[bass.ds(tile(n, j) * P, P), :]).then_inc(y_loaded[j], 16)

                def chunk(n, c):
                    for j in range(PER):
                        fetch(n, j)

                over_chunks(pool, chunk)

            @block.scalar
            def _(act):
                def store(n, j):
                    act.wait_ge(combined, 2 * n + j + 1)
                    act.dma_start(m.out[bass.ds(tile(n, j) * P, P), :], y[:, j, 1, :]).then_inc(out_stored[j], 16)

                def chunk(n, c):
                    for j in range(SH_TILES):
                        s.activate(act, n, c, j)
                        s.high(act, n, c, j)
                        if 1 <= j <= 2:
                            store(n, j - 1)

                over_chunks(act, chunk)
                for j in range(2):
                    act.wait_ge(out_stored[j], 16 * CHUNKS)

            @block.vector
            def _(v):
                def combine_tile(n, j):
                    t = tile(n, j)
                    done = 3 * (PER * n + j)
                    v.wait_ge(y_loaded[j], 16 * (TOP + 1 if j < 2 else TOP) * (n + 1))
                    v.tensor_scalar(y[:, j, 0, :], y[:, j, 0, :], m.weight[:, 0, bass.ds(t, 1)], None, ALU.mult).then_inc(c_step, 1)
                    v.wait_ge(c_step, done + 1)
                    v.scalar_tensor_tensor(out=y[:, j, 1, :], in0=y[:, j, 1, :], scalar=m.weight[:, 1, bass.ds(t, 1)],
                                           in1=y[:, j, 0, :], op0=ALU.mult, op1=ALU.add).then_inc(c_step, 1)
                    v.wait_ge(c_step, done + 2)
                    v.tensor_tensor(y[:, j, 1, :], y[:, j, 1, :], gb[:, t // BT, :], ALU.mult).then_inc(c_step, 1)
                    v.wait_ge(c_step, done + 3)
                    if j < 2:
                        v.tensor_tensor(y[:, j, 1, :], y[:, j, 1, :], xc[:, j, :], ALU.add).then_inc(combined, 1)
                    else:
                        v.wait_ge(s.xs_loaded[j - 2], 16 * (n + 1))
                        v.tensor_tensor(s.xs[:, j - 2, :], y[:, j, 1, :], s.xs[:, j - 2, :], ALU.add).then_inc(merged, 1)

                def chunk(n, c):
                    for j in range(SH_TILES):
                        s.multiply(v, n, c, j)
                        s.low(v, n, c, j)
                        if j < PER:
                            combine_tile(n, j)
                    for t in range(2):
                        s.add(v, n, c, t)

                v.wait_ge(gb_loaded, 16 * B)
                over_chunks(v, chunk)

            @block.tensor
            def _(pe):
                def chunk(n, c):
                    for j in range(SH_TILES):
                        s.up(pe, n, c, j)
                    s.down(pe, n, c)

                over_chunks(pe, chunk)


def adaln_block(nc, x, wqkv_t, wproj_t, b_proj, gate_t, router_bias, w1_d, w3_d, w2_d, sh_flat, c_t, wmod_d, out):
    m = Parts()
    m.x, m.wqkv_t, m.wproj_t, m.b_proj, m.gate_t, m.router_bias = x, wqkv_t, wproj_t, b_proj, gate_t, router_bias
    m.w1_d, m.w3_d, m.w2_d, m.sh_flat, m.c_t, m.wmod_d, m.out = w1_d, w3_d, w2_d, sh_flat, c_t, wmod_d, out
    with ExitStack() as ctx:
        m.sem = lambda name: ctx.enter_context(nc.semaphore(name))
        dram = lambda name, shape, dt: nc.dram_tensor(name, shape, dt).ap()
        m.x2_d, m.x2s_d, m.h2_d = dram("x2_d", (T, C), F32), dram("x2s_d", (T, C), F32), dram("h2_d", (T, C), F32)
        m.h2t_d, m.y_d = dram("h2t_d", (TILES, P, 2 * C), F16), dram("y_d", (SLOTS, C), F32)
        m.mod_d, m.gab_d, m.table = dram("mod_d", (B, 6 * C), F32), dram("gab_d", (B, C), F32), dram("table", (SLOTS, 1), I32)

        def sb(name, shape, dt, stack=ctx):
            return stack.enter_context(nc.sbuf_tensor(name, shape, dt))

        m.ident = sb("ident", [P, P], F32)
        m.spare = sb("spare", [P, 1], F32)
        m.logits = sb("logits", [P, TILES, E], F32)
        m.weight = sb("weight", [P, TOP, TILES], F32)
        m.slot = sb("slot", [P, TOP, TILES], I32)
        m.slot_token = sb("slot_token", [P, SLOT_TILES], I32)
        m.eid = sb("eid", [1, SLOT_TILES], I32)
        m.sh = sb("sh", [P, 2, KC * 2 * SHARED + SH_TILES * C], F16)
        with ExitStack() as attention:
            m.gate = sb("gate", [P, KC, 2, E], F16, attention)
            m.heads = sb("heads", [P, 4], F32, attention)
            m.head_mask = sb("head_mask", [P, P], F32, attention)
            m.minus_half = sb("minus_half", [P, 1], F32, attention)
            m.wproj = sb("wproj", [P, KC, 2, C], F16, attention)
            m.vk = sb("vk", [P, B, 2, GRP, VKW], F16, attention)
            m.qt_flat = sb("qt", [P, TILES * 2 * GRP * P], F16, attention)
            m.qt = m.qt_flat[:, :].rearrange("p (t s g n) -> p t s g n", t=TILES, s=2, g=GRP)
            with ExitStack() as projections:
                m.wqkv = sb("wqkv", [P, KC, 2, 3 * C], F16, projections)
                m.v_sb = sb("v_sb", [P, 2, GRP, P + 1], F32, projections)
                m.rows = sb("rows", [P, B, 2, C], F32, projections)
                setup(nc, m)
                front(nc, m)
            back(nc, m)
        with ExitStack() as expert_weights:
            m.w13 = sb("w13", [P, E, KC, 2, 2 * INTER], F16, expert_weights)
            m.w2 = sb("w2", [P, E, 3, 2, C], F16, expert_weights)
            route(nc, m)
            experts(nc, m)
        combine(nc, m)


def kernel(L0_attn_x, L0_attn_w_qkv, L0_attn_w_proj, L0_attn_b_proj, L0_ffn_gate_w, L0_ffn_router_bias, L0_ffn_W1,
           L0_ffn_W3, L0_ffn_W2, L0_ffn_sw1, L0_ffn_sw3, L0_ffn_sw2, L0_c, L0_wmod):
    import numpy as np
    import concourse.bacc as bacc
    from concourse.bass_utils import run_bass_kernel_spmd as run

    def t(a):
        return np.ascontiguousarray(np.asarray(a).T)

    sw1, sw3, sw2 = t(L0_ffn_sw1), t(L0_ffn_sw3), t(L0_ffn_sw2)
    turns = [w[:, j * P:(j + 1) * P] for j in range(SH_TILES) for w in (sw1, sw3)]
    up = np.concatenate(turns, axis=1).reshape(KC, P, 2 * SHARED).transpose(1, 0, 2).reshape(P, -1)
    down = np.zeros((SH_TILES * P, C), sw2.dtype)
    down[:SHARED] = sw2
    down = down.reshape(SH_TILES, P, C).transpose(1, 0, 2).reshape(P, -1)
    arrays = {
        "x": np.ascontiguousarray(L0_attn_x).reshape(T, C), "wqkv_t": t(L0_attn_w_qkv), "wproj_t": t(L0_attn_w_proj),
        "b_proj": np.ascontiguousarray(L0_attn_b_proj), "gate_t": t(L0_ffn_gate_w),
        "router_bias": np.ascontiguousarray(L0_ffn_router_bias), "w1_d": np.ascontiguousarray(L0_ffn_W1),
        "w3_d": np.ascontiguousarray(L0_ffn_W3), "w2_d": np.ascontiguousarray(L0_ffn_W2),
        "sh_flat": np.ascontiguousarray(np.concatenate([up, down], axis=1)), "c_t": t(L0_c),
        "wmod_d": np.ascontiguousarray(L0_wmod),
    }
    nc = bacc.Bacc("TRN2", target_bir_lowering=False, num_devices=1)
    handles = {k: nc.dram_tensor(f"in_{k}", v.shape, mybir.dt.from_np(v.dtype), kind="ExternalInput").ap() for k, v in arrays.items()}
    out = nc.dram_tensor("out_0", (T, C), F32, kind="ExternalOutput").ap()
    adaln_block(nc, out=out, **handles)
    r = run(nc, [{f"in_{k}": v for k, v in arrays.items()}], core_ids=[0])
    return r.results[0]["out_0"].reshape(B, N, C)
```

```python
from contextlib import ExitStack

import concourse.bass as bass
from concourse import mybir

F32 = mybir.dt.float32
F16 = mybir.dt.float16
I32 = mybir.dt.int32
U32 = mybir.dt.uint32
ALU = mybir.AluOpType
ACT = mybir.ActivationFunctionType
AX = mybir.AxisListType

P = 128
B, N, C = 4, 1024, 512
HEAD = 32
T = B * N
TILES = T // P
BT = N // P
KC = C // P
E, TOP = 8, 2
INTER = 352
SHARED = 704
SH_TILES = 6
SH_HALF = SHARED - 5 * P
DOWN_AT = 2
SLOT_TILES = (T * TOP + E * (P - 1)) // P
SLOTS = SLOT_TILES * P
SCALE = 64.0
VK_SCALE = 1.0 / 64.0
GRP = 4
VKW = P + 4
LN_EPS, DEN_EPS, SUM_EPS = 1e-5, 1e-15, 1e-12
SA, CA = range(2)
GA, GAB, SB, CB = range(4)
PIECE = (KC * 2 * SHARED + SH_TILES * C) // TILES


class Parts:
    pass


def split_matmul(nc, out, lhs, rhs, first, last):
    (lh, ll), (rh, rl) = lhs, rhs
    nc.tensor.matmul(out, lh, rh, start=first, stop=False, skip_group_check=True)
    nc.tensor.matmul(out, lh, rl, start=False, stop=False, skip_group_check=True)
    return nc.tensor.matmul(out, ll, rh, start=False, stop=last, skip_group_check=True)


def front(nc, m):
    with ExitStack() as ctx:
        sb = lambda name, shape, dt: ctx.enter_context(nc.sbuf_tensor(name, shape, dt))
        pb = lambda name, shape: ctx.enter_context(nc.psum_tensor(name, shape, F32))
        sem = m.sem
        xb = sb("xb", [P, 4, C], F32)
        st = sb("st", [P, 4, 6], F32)
        mv = sb("mv", [P, 4, 2], F32)
        rstd = sb("rstd", [P, 4, 1], F32)
        centred = sb("centred", [P, C], F32)
        spare = sb("spare_f", [P, 1], F32)
        h = sb("h", [P, 2, C], F32)
        ht = sb("ht", [P, 2, 2, KC, P], F16)
        k_sb = sb("k_sb", [P, 2, C], F32)
        vk_tmp = sb("vk_tmp", [P, GRP, VKW], F32)
        ps_t, ps_k, ps_v, ps_q = pb("ps_t", [P, KC, P]), pb("ps_k", [P, C]), pb("ps_v", [P, C]), pb("ps_q", [P, GRP, P])
        ps_vk = [pb(f"ps_vk{j}", [P, 2, P + 1]) for j in range(2)]
        sstage = sb("sstage", [P, 2, PIECE], F32)
        ct = sb("ct", [P, KC, B], F32)
        sct = sb("sct", [P, KC, B], F32)
        wmod_size, mod_size = KC * 6 * C * 2, 6 * C * 2
        wmod = m.qt_flat[:, 0:wmod_size].bitcast(F32).rearrange("p (k n) -> p k n", k=KC)
        mod = m.qt_flat[0:B, wmod_size:wmod_size + mod_size].bitcast(F32)
        gate_tmp = m.qt_flat[0:B, wmod_size + mod_size:wmod_size + mod_size + 4 * C].bitcast(F32)
        RING = 6
        stage = sb("stage", [P, RING, C], F32)
        bproj = sb("bproj", [B, C], F32)
        gstage = sb("gstage", [P, KC, E], F32)
        zero = sb("zero", [P, SLOT_TILES], I32)
        ps_m = [pb(f"ps_m{j}", [B, C]) for j in range(2)]
        ps_mod = [ps_m[0][:, :], ps_m[1][:, :], ps_t[0:B, :, :].rearrange("p k n -> p (k n)"), ps_k[0:B, :], ps_v[0:B, :],
                  ps_q[0:B, :, :].rearrange("p k n -> p (k n)")]
        c_loaded, silu_done = sem("c_loaded"), sem("silu_done")
        wmod_loaded = [sem(f"wmod_loaded{k}") for k in range(KC)]
        stage_loaded = [sem(f"stage_loaded{k}") for k in range(RING)]
        stage_hi, stage_lo = sem("stage_hi"), sem("stage_lo")
        small_loaded, mod_done, mod_copied = sem("small_loaded"), sem("mod_done"), sem("mod_copied")
        front_mod, front_stored, back_stored = sem("front_mod"), sem("front_stored"), sem("back_stored")
        rows_loaded, pool_step = sem("rows_loaded"), sem("pool_step")
        pieces = [(m.wqkv_t[k * P:(k + 1) * P, w * C:(w + 1) * C], m.wqkv[:, k, :, w * C:(w + 1) * C]) for w in (1, 2, 0) for k in range(KC)]
        pieces += [(m.wproj_t[k * P:(k + 1) * P, :], m.wproj[:, k, :, :]) for k in range(KC)]
        K_PIECES, V_PIECES, Q_PIECES, P_PIECES = (range(w * KC, (w + 1) * KC) for w in range(4))
        CONSTS = 10
        x_loaded = [sem(f"x_loaded{j}") for j in range(4)]
        s_loaded = [sem(f"s_loaded{j}") for j in range(2)]
        s_hi, s_lo = sem("s_hi"), sem("s_lo")
        bn_done, stats_ready, eps_added, rstd_ready = sem("bn_done"), sem("stats_ready"), sem("eps_added"), sem("rstd_ready")
        centred_ready, h_ready, t_done, ht_hi, ht_ready = sem("centred_ready"), sem("h_ready"), sem("t_done"), sem("ht_hi"), sem("ht_ready")
        k_done, v_done, q_done = sem("k_done"), sem("v_done"), sem("q_done")
        k_ready, v_ready, q_hi, q_ready = sem("k_ready"), sem("v_ready"), sem("q_hi"), sem("q_ready")
        vk_done, vk_step, vk_hi, vk_ready = sem("vk_done"), sem("vk_step"), sem("vk_hi"), sem("vk_ready")

        def there(b, c):
            return not isinstance(b, int) or 8 * b + c < TILES

        def over_batches(eng, slot):
            with eng.Fori(0, B - 1) as b:
                for c in range(1, BT + 1):
                    slot(b, c)
            for c in range(1, BT + 1):
                slot(B - 1, c)

        with nc.Block() as block:
            @block.sync
            def _(sp):
                def load(b, c):
                    if not there(b, c):
                        return
                    i = 8 * b + c
                    if not (isinstance(b, int) and i < 4):
                        sp.wait_ge(centred_ready, i - 3)
                    sp.dma_start(xb[:, c % 4, :], m.x[bass.ds(i * P, P), :]).then_inc(x_loaded[c % 4], 16)

                def load_piece(b, c):
                    if not there(b, c):
                        return
                    i = 8 * b + c
                    if not (isinstance(b, int) and i < 2):
                        sp.wait_ge(s_lo, i - 1)
                    sp.dma_start(sstage[:, c % 2, :], m.sh_flat[:, bass.ds(i * PIECE, PIECE)]).then_inc(s_loaded[c % 2], 16)

                def slot(b, c):
                    load(b, c + 3)
                    load_piece(b, c)

                sp.dma_start(ct[:, :, :], m.c_t.rearrange("(k p) b -> p k b", p=P)).then_inc(c_loaded, 16)
                for c in range(3):
                    load(0, c)
                for part, cols in enumerate((slice(0, 2 * C), slice(2 * C, 6 * C))):
                    for k in range(KC):
                        sp.dma_start(wmod[:, k, cols], m.wmod_d[k * P:(k + 1) * P, cols]).then_inc(wmod_loaded[2 * part + k // 2], 16)
                sp.dma_start(bproj[:, :], m.b_proj.partition_broadcast(B)).then_inc(small_loaded, 16)
                sp.dma_start(gstage[:, :, :], m.gate_t.rearrange("(k p) e -> p k e", p=P)).then_inc(small_loaded, 16)
                for n, (src, _) in enumerate(pieces):
                    if n >= RING:
                        sp.wait_ge(stage_lo, n - RING + 1)
                    sp.dma_start(stage[:, n % RING, :], src).then_inc(stage_loaded[n % RING], 16)
                    if n == Q_PIECES[-1]:
                        load(0, 3)
                        load_piece(0, 0)
                over_batches(sp, slot)

            @block.gpsimd
            def _(pool):
                def reciprocal_deviation(b, c):
                    if not there(b, c):
                        return
                    i = 8 * b + c
                    pool.wait_ge(eps_added, i + 1)
                    pool.tensor_tensor(rstd[:, c % 4, :], rstd[:, c % 4, :], m.minus_half[:, :], ALU.pow).then_inc(rstd_ready, 1)

                steps = 0

                def step(instruction):
                    nonlocal steps
                    steps += 1
                    instruction.then_inc(pool_step, 1)
                    pool.wait_ge(pool_step, steps)

                step(pool.memset(m.ident[:, :], 0.0))
                step(pool.affine_select(out=m.ident[:, :], in_=m.ident[:, :], compare_op=ALU.not_equal, fill=1.0,
                                        base=0, pattern=[[-1, P]], channel_multiplier=1))
                step(pool.memset(m.heads[:, :], VK_SCALE))
                step(pool.affine_select(out=m.heads[:, :], in_=m.heads[:, :], compare_op=ALU.is_ge, fill=0.0,
                                        base=0, pattern=[[-HEAD, 4]], channel_multiplier=1))
                step(pool.affine_select(out=m.heads[:, :], in_=m.heads[:, :], compare_op=ALU.is_ge, fill=0.0,
                                        base=HEAD - 1, pattern=[[HEAD, 4]], channel_multiplier=-1))
                step(pool.tensor_copy(m.head_mask[:, :].rearrange("p (h e) -> p h e", h=4),
                                      m.heads[:, :].unsqueeze(2).to_broadcast([P, 4, HEAD])))
                step(pool.memset(m.minus_half[:, :], -0.5))
                step(pool.memset(m.spare[:, :], 0.0))
                step(pool.memset(m.v_sb[:, :, :, P:P + 1], 1.0))
                step(pool.memset(zero[:, :], 0))
                assert steps == CONSTS
                pool.dma_start(m.table.rearrange("(p t) o -> p (t o)", p=P), zero[:, :]).then_inc(back_stored, 16)
                for c in range(3):
                    reciprocal_deviation(0, c)
                pool.wait_ge(mod_copied, 4)
                mag, sgn = gate_tmp[:, 0:C], gate_tmp[:, C:2 * C]
                cb = mod[:, 4 * C:5 * C]
                step(pool.tensor_scalar(cb, cb, 1.0, None, ALU.add))
                for j in (5, 2):
                    g = mod[:, j * C:(j + 1) * C]
                    step(pool.tensor_scalar(sgn, g, 0.0, 2.0, ALU.is_ge, ALU.mult))
                    step(pool.tensor_scalar(sgn, sgn, -1.0, None, ALU.add))
                    step(pool.tensor_tensor(mag, g, sgn, ALU.mult))
                    step(pool.tensor_scalar(mag, mag, 0.25, None, ALU.max))
                    step(pool.tensor_tensor(g, mag, sgn, ALU.mult))
                pool.wait_ge(small_loaded, 32)
                step(pool.tensor_tensor(mag, mod[:, 2 * C:3 * C], bproj[:, :], ALU.mult))
                pool.dma_start(m.mod_d[:, 2 * C:6 * C], mod[:, 2 * C:6 * C]).then_inc(back_stored, 16)
                pool.dma_start(m.gab_d, mag).then_inc(back_stored, 16)
                pool.wait_ge(back_stored, 48)
                reciprocal_deviation(0, 3)
                over_batches(pool, lambda b, c: reciprocal_deviation(b, c + 3))

            @block.vector
            def _(v):
                def stats(b, c):
                    if not there(b, c):
                        return
                    i = 8 * b + c
                    v.wait_ge(x_loaded[c % 4], 16 * ((c // 4) + 1 + 2 * b))
                    if not (isinstance(b, int) and i < 4):
                        v.wait_ge(h_ready, i - 3)
                    v.bn_stats(st[:, c % 4, :], xb[:, c % 4, :]).then_inc(bn_done, 1)
                    v.wait_ge(bn_done, i + 1)
                    v.memset(spare[:, :], 0.0)
                    v.bn_aggr(mv[:, c % 4, :], st[:, c % 4, :]).then_inc(stats_ready, 1)
                    v.wait_ge(stats_ready, i + 1)
                    v.tensor_scalar(rstd[:, c % 4, :], mv[:, c % 4, 1:2], LN_EPS, None, ALU.add).then_inc(eps_added, 1)

                def normalise(b, c):
                    if not there(b, c):
                        return
                    i = 8 * b + c
                    batch = b + c // BT
                    v.wait_ge(stats_ready, i + 1)
                    if not (isinstance(b, int) and i < 1):
                        v.wait_ge(h_ready, i)
                    v.scalar_tensor_tensor(out=centred[:, :], in0=xb[:, c % 4, :], scalar=mv[:, c % 4, 0:1],
                                           in1=m.rows[:, batch, CA, :], op0=ALU.subtract, op1=ALU.mult).then_inc(centred_ready, 1)
                    v.wait_ge(rstd_ready, i + 1)
                    v.wait_ge(centred_ready, i + 1)
                    if not (isinstance(b, int) and i < 2):
                        v.wait_ge(t_done, i - 1)
                    v.scalar_tensor_tensor(out=h[:, c % 2, :], in0=centred[:, :], scalar=rstd[:, c % 4, :],
                                           in1=m.rows[:, batch, SA, :], op0=ALU.mult, op1=ALU.add).then_inc(h_ready, 1)

                def low_part(b, c):
                    if not there(b, c):
                        return
                    v.wait_ge(ht_hi, 8 * b + c + 1)
                    v.tensor_tensor(ht[:, c % 2, 1, :, :], ps_t[:, :, :], ht[:, c % 2, 0, :, :], ALU.subtract).then_inc(ht_ready, 1)

                def values(b, c):
                    if not there(b, c):
                        return
                    i = 8 * b + c
                    v.wait_ge(v_done, i + 1)
                    if not (isinstance(b, int) and i < 2):
                        v.wait_ge(vk_done, i - 1)
                    v.tensor_scalar(m.v_sb[:, c % 2, :, 0:P], ps_v[:, :].rearrange("p (g n) -> p g n", g=GRP),
                                    1.0 / SCALE, None, ALU.mult).then_inc(v_ready, 1)
                    v.wait_ge(q_hi, i + 1)
                    v.scalar_tensor_tensor(out=m.qt[:, i, 1, :, :], in0=ps_q[:, :, :], scalar=0.0, in1=m.qt[:, i, 0, :, :],
                                           op0=ALU.max, op1=ALU.subtract).then_inc(q_ready, 1)

                def key_value_sums(b):
                    v.wait_ge(vk_done, 8 * b + 8)
                    if not (isinstance(b, int) and b == 0):
                        v.wait_ge(vk_ready, 1 * b)
                    for g in range(GRP):
                        v.tensor_tensor(vk_tmp[:, g, 0:P], ps_vk[g // 2][:, g % 2, 0:P], m.head_mask[:, :], ALU.mult).then_inc(vk_step, 1)
                        v.tensor_scalar(vk_tmp[:, g, P:VKW], m.heads[:, :], ps_vk[g // 2][:, g % 2, P:P + 1], None, ALU.mult).then_inc(vk_step, 1)
                    v.wait_ge(vk_step, 8 * b + 8)
                    v.tensor_copy(m.vk[:, b, 0, :, :], vk_tmp[:, :, :]).then_inc(vk_hi, 1)
                    v.wait_ge(vk_hi, b + 1)
                    v.tensor_tensor(m.vk[:, b, 1, :, :], vk_tmp[:, :, :], m.vk[:, b, 0, :, :], ALU.subtract).then_inc(vk_ready, 1)

                def piece_low(b, c):
                    if not there(b, c):
                        return
                    i = 8 * b + c
                    v.wait_ge(s_hi, i + 1)
                    v.scalar_tensor_tensor(out=m.sh[:, 1, bass.ds(i * PIECE, PIECE)], in0=sstage[:, c % 2, :], scalar=SCALE,
                                           in1=m.sh[:, 0, bass.ds(i * PIECE, PIECE)], op0=ALU.mult, op1=ALU.subtract).then_inc(s_lo, 1)

                def slot(b, c):
                    stats(b, c + 3)
                    normalise(b, c + 2)
                    low_part(b, c + 1)
                    values(b, c)
                    piece_low(b, c)
                    if c == BT:
                        key_value_sums(b)

                def split_low(pieces_now):
                    for n in pieces_now:
                        dst = pieces[n][1]
                        v.wait_ge(stage_hi, n + 1)
                        v.scalar_tensor_tensor(out=dst[:, 1, :], in0=stage[:, n % RING, :], scalar=SCALE, in1=dst[:, 0, :],
                                               op0=ALU.mult, op1=ALU.subtract).then_inc(stage_lo, 1)

                for c in range(3):
                    stats(0, c)
                v.wait_ge(mod_done, 2)
                v.tensor_copy(mod[:, 0:C], ps_mod[0]).then_inc(front_mod, 1)
                v.tensor_scalar(mod[:, C:2 * C], ps_mod[1], 1.0, None, ALU.add).then_inc(front_mod, 1)
                v.wait_ge(rows_loaded, 16 * 2 * B)
                normalise(0, 0)
                normalise(0, 1)
                split_low(K_PIECES)
                low_part(0, 0)
                split_low(V_PIECES)
                split_low(Q_PIECES)
                slot(0, 0)
                split_low(P_PIECES)
                v.wait_ge(stage_hi, len(pieces) + 1)
                v.scalar_tensor_tensor(out=m.gate[:, :, 1, :], in0=gstage[:, :, :], scalar=SCALE, in1=m.gate[:, :, 0, :],
                                       op0=ALU.mult, op1=ALU.subtract).then_inc(stage_lo, 1)
                over_batches(v, slot)

            @block.scalar
            def _(act):
                def high_part(b, c):
                    if not there(b, c):
                        return
                    i = 8 * b + c
                    act.wait_ge(t_done, i + 1)
                    if not (isinstance(b, int) and i < 2):
                        act.wait_ge(q_done, i - 1)
                    act.activation(ht[:, c % 2, 0, :, :], ps_t[:, :, :], ACT.Copy).then_inc(ht_hi, 1)

                def slot(b, c):
                    high_part(b, c + 1)
                    if not there(b, c):
                        return
                    i = 8 * b + c
                    act.wait_ge(k_done, i + 1)
                    if not (isinstance(b, int) and i < 2):
                        act.wait_ge(vk_done, i - 1)
                    act.activation(k_sb[:, c % 2, :], ps_k[:, :], ACT.Relu, scale=1.0 / SCALE).then_inc(k_ready, 1)
                    act.wait_ge(q_done, i + 1)
                    act.activation(m.qt[:, i, 0, :, :], ps_q[:, :, :], ACT.Relu).then_inc(q_hi, 1)
                    act.wait_ge(s_loaded[c % 2], 16 * ((c // 2) + 1 + 4 * b))
                    act.activation(m.sh[:, 0, bass.ds(i * PIECE, PIECE)], sstage[:, c % 2, :], ACT.Copy, scale=SCALE).then_inc(s_hi, 1)

                def split_high(pieces_now):
                    for n in pieces_now:
                        act.wait_ge(stage_loaded[n % RING], 16 * (n // RING + 1))
                        act.activation(pieces[n][1][:, 0, :], stage[:, n % RING, :], ACT.Copy, scale=SCALE).then_inc(stage_hi, 1)

                act.wait_ge(c_loaded, 16)
                act.activation(sct[:, :, :], ct[:, :, :], ACT.Silu).then_inc(silu_done, 1)
                act.wait_ge(front_mod, 2)
                act.dma_start(m.mod_d[:, 0:2 * C], mod[:, 0:2 * C]).then_inc(front_stored, 16)
                act.wait_ge(front_stored, 16)
                for b in range(B):
                    for r, src in ((SA, m.mod_d[b, 0:C]), (CA, m.mod_d[b, C:2 * C])):
                        act.dma_start(m.rows[:, b, r, :], src.partition_broadcast(P)).then_inc(rows_loaded, 16)
                for j in range(2, 6):
                    act.wait_ge(mod_done, j + 1)
                    act.activation(mod[:, j * C:(j + 1) * C], ps_mod[j], ACT.Copy).then_inc(mod_copied, 1)
                split_high(K_PIECES)
                high_part(0, 0)
                split_high(V_PIECES)
                split_high(Q_PIECES)
                slot(0, 0)
                split_high(P_PIECES)
                act.wait_ge(small_loaded, 32)
                act.activation(m.gate[:, :, 0, :], gstage[:, :, :], ACT.Copy, scale=SCALE).then_inc(stage_hi, 1)
                over_batches(act, slot)

            @block.tensor
            def _(pe):
                def transposes(b, c):
                    if not there(b, c):
                        return
                    i = 8 * b + c
                    pe.wait_ge(h_ready, i + 1)
                    if not (isinstance(b, int) and i < 1):
                        pe.wait_ge(ht_ready, i)
                    for k in range(KC):
                        mm = nc.tensor.transpose(ps_t[:, k, :], h[:, c % 2, k * P:(k + 1) * P], m.ident[:, :])
                    mm.then_inc(t_done, 1)

                def project(b, c):
                    if not there(b, c):
                        return
                    i = 8 * b + c
                    first = isinstance(b, int) and i == 0
                    hk = [(ht[:, c % 2, 0, k, :], ht[:, c % 2, 1, k, :]) for k in range(KC)]
                    w = lambda k, lo, n: (m.wqkv[:, k, 0, lo:lo + n], m.wqkv[:, k, 1, lo:lo + n])
                    pe.wait_ge(ht_ready, i + 1)
                    if first:
                        pe.wait_ge(stage_lo, K_PIECES[-1] + 1)
                    else:
                        pe.wait_ge(k_ready, i)
                    for k in range(KC):
                        mm = split_matmul(nc, ps_k[:, :], hk[k], w(k, C, C), k == 0, k == KC - 1)
                    mm.then_inc(k_done, 1)
                    if first:
                        pe.wait_ge(stage_lo, V_PIECES[-1] + 1)
                    else:
                        pe.wait_ge(v_ready, i)
                    for k in range(KC):
                        mm = split_matmul(nc, ps_v[:, :], hk[k], w(k, 2 * C, C), k == 0, k == KC - 1)
                    mm.then_inc(v_done, 1)
                    if first:
                        pe.wait_ge(stage_lo, Q_PIECES[-1] + 1)
                    else:
                        pe.wait_ge(q_ready, i)
                    for g in range(GRP):
                        for k in range(KC):
                            mm = split_matmul(nc, ps_q[:, g, :], w(k, g * P, P), hk[k], k == 0, k == KC - 1)
                    mm.then_inc(q_done, 1)

                def sum_keys_values(b, c):
                    i = 8 * b + c
                    pe.wait_ge(k_ready, i + 1)
                    pe.wait_ge(v_ready, i + 1)
                    if c == 0 and not (isinstance(b, int) and b == 0):
                        pe.wait_ge(vk_ready, b)
                    for g in range(GRP):
                        mm = nc.tensor.matmul(ps_vk[g // 2][:, g % 2, :], k_sb[:, c % 2, g * P:(g + 1) * P],
                                              m.v_sb[:, c % 2, g, 0:P + 1], start=c == 0 and g % 2 == 0,
                                              stop=c == BT - 1, skip_group_check=True)
                    mm.then_inc(vk_done, 1)

                def slot(b, c):
                    transposes(b, c + 1)
                    project(b, c)
                    if c >= 1:
                        sum_keys_values(b, c - 1)

                pe.wait_ge(silu_done, 1)
                for part, js in enumerate((range(0, 2), range(2, 6))):
                    for k in range(KC):
                        pe.wait_ge(wmod_loaded[2 * part + k // 2], 32)
                        for j in js:
                            mm = nc.tensor.matmul(ps_mod[j], sct[:, k, :], wmod[:, k, j * C:(j + 1) * C],
                                                  start=k == 0, stop=k == KC - 1)
                            if k == KC - 1:
                                mm.then_inc(mod_done, 1)
                pe.wait_ge(pool_step, CONSTS)
                pe.wait_ge(mod_copied, 4)
                transposes(0, 0)
                slot(0, 0)
                over_batches(pe, slot)


def back(nc, m):
    with ExitStack() as ctx:
        sb = lambda name, shape, dt: ctx.enter_context(nc.sbuf_tensor(name, shape, dt))
        pb = lambda name, shape: ctx.enter_context(nc.psum_tensor(name, shape, F32))
        sem = m.sem
        xr = sb("xr", [P, 2, C], F32)
        xg = sb("xg", [P, 2, C], F32)
        den = sb("den", [P, 4 * GRP], F32)
        o_sb = sb("o_sb", [P, 2, C], F32)
        ot = sb("ot", [P, 2, 2, KC, P], F16)
        x2 = sb("x2", [P, 2, C], F32)
        t1 = sb("t1", [P, C], F32)
        st = sb("st_b", [P, 2, 6], F32)
        mv = sb("mv_b", [P, 2, 2], F32)
        rstd = sb("rstd_b", [P, 2, 1], F32)
        centred = sb("centred_b", [P, 2, C], F32)
        spare = sb("spare_b", [P, 1], F32)
        h2 = sb("h2", [P, 2, C], F32)
        h2t = sb("h2t", [P, 2, 2, KC, P], F16)
        ps_o = [pb(f"ps_o{j}", [P, 2, VKW]) for j in range(2)]
        ps_y = [pb(f"ps_y{j}", [P, C]) for j in range(2)]
        ps_ot, ps_ht, ps_l = pb("ps_ot", [P, KC, P]), pb("ps_ht", [P, KC, P]), pb("ps_l", [P, E])
        m.rows = sb("rows_b", [P, B, 4, C], F32)
        rows_b0, rows_b = sem("rows_b0"), sem("rows_b")
        xr_loaded = [sem(f"xr_loaded{j}") for j in range(2)]
        xg_ready, o_done, den_ready, rden_ready, o_ready = sem("xg_ready"), sem("o_done"), sem("den_ready"), sem("rden_ready"), sem("o_ready")
        ot_done, ot_hi, ot_ready, y_done, t1_ready, x2_ready = sem("ot_done"), sem("ot_hi"), sem("ot_ready"), sem("y_done"), sem("t1_ready"), sem("x2_ready")
        bn2_done, stats2_ready, eps2_added, rstd2_ready = sem("bn2_done"), sem("stats2_ready"), sem("eps2_added"), sem("rstd2_ready")
        centred2_ready, scaled_ready, h2_ready, h2t_done, h2t_hi, h2t_ready = sem("centred2_ready"), sem("scaled_ready"), sem("h2_ready"), sem("h2t_done"), sem("h2t_hi"), sem("h2t_ready")
        l_done, l_ready = sem("l_done"), sem("l_ready")
        x2_stored = [sem(f"x2_stored{j}") for j in range(2)]
        h2_stored = [sem(f"h2_stored{j}") for j in range(2)]
        h2t_stored = [sem(f"h2t_stored{j}") for j in range(2)]
        LAG_Y, LAG_X2, LAG_H2, LAG_T, LAG_L = 2, 3, 4, 6, 7
        LAST = LAG_L + 1

        def there(t):
            return not isinstance(t, int) or 0 <= t < TILES

        def later(t, n):
            return not isinstance(t, int) or t >= n

        def over_tiles(eng, slot, rows=False):
            if rows:
                eng.wait_ge(rows_b0, 16 * 4)
            for i in range(LAST):
                slot(i, i)
            if rows:
                eng.wait_ge(rows_b, 16 * 4 * (B - 1))
            with eng.Fori(0, (TILES - LAST) // 2) as pair:
                for c in range(2):
                    slot(2 * pair + (LAST + c), LAST + c)
            for i in range(TILES, TILES + LAG_L):
                slot(i, i)

        def uses(t, c):
            return 16 * (t // 2 + 1)

        with nc.Block() as block:
            @block.sync
            def _(sp):
                for b in range(B):
                    for r, src in ((GA, m.mod_d[b, 2 * C:3 * C]), (GAB, m.gab_d[b, :]), (SB, m.mod_d[b, 3 * C:4 * C]),
                                   (CB, m.mod_d[b, 4 * C:5 * C])):
                        sp.dma_start(m.rows[:, b, r, :], src.partition_broadcast(P)).then_inc(rows_b if b else rows_b0, 16)

                def slot(t, c):
                    if there(t):
                        if later(t, 2):
                            sp.wait_ge(xg_ready, t - 1)
                        sp.dma_start(xr[:, c % 2, :], m.x[bass.ds(t * P, P), :]).then_inc(xr_loaded[c % 2], 16)
                    u, d = t - LAG_X2, c - LAG_X2
                    if there(u):
                        sp.wait_ge(x2_ready, u + 1)
                        sp.dma_start(m.x2_d[bass.ds(u * P, P), :], x2[:, d % 2, :]).then_inc(x2_stored[d % 2], 16)
                    u, d = t - LAG_H2 - 1, c - LAG_H2 - 1
                    if there(u):
                        sp.wait_ge(h2_ready, u + 1)
                        sp.dma_start(m.h2_d[bass.ds(u * P, P), :], h2[:, d % 2, :]).then_inc(h2_stored[d % 2], 16)
                    u, d = t - LAG_T, c - LAG_T
                    if there(u):
                        sp.wait_ge(h2t_ready, u + 1)
                        sp.dma_start(m.h2t_d[bass.ds(u, 1), :, :].rearrange("o p n -> (o p) n"),
                                     h2t[:, d % 2, :, :, :].rearrange("p s k n -> p (s k n)")).then_inc(h2t_stored[d % 2], 16)

                over_tiles(sp, slot)
                for s in x2_stored + h2_stored + h2t_stored:
                    sp.wait_ge(s, 16 * TILES // 2)

            @block.gpsimd
            def _(pool):
                def slot(t, c):
                    u, d = t - LAG_H2 - 1, c - LAG_H2 - 1
                    if there(u):
                        pool.wait_ge(scaled_ready, u + 1)
                        if later(u, 2):
                            pool.wait_ge(h2t_done, u - 1)
                            pool.wait_ge(h2_stored[d % 2], uses(u - 2, d))
                        pool.tensor_tensor(h2[:, d % 2, :], centred[:, d % 2, :], m.rows[:, u // BT, SB, :], ALU.add).then_inc(h2_ready, 1)
                    u, d = t - LAG_Y, c - LAG_Y
                    if there(u):
                        pool.wait_ge(xr_loaded[d % 2], uses(u, d))
                        if later(u, 2):
                            pool.wait_ge(x2_ready, u - 1)
                        pool.tensor_tensor(xg[:, d % 2, :], xr[:, d % 2, :], m.rows[:, u // BT, GAB, :], ALU.add).then_inc(xg_ready, 1)
                    u, d = t - LAG_X2, c - LAG_X2
                    if there(u):
                        pool.wait_ge(eps2_added, u + 1)
                        pool.tensor_tensor(rstd[:, d % 2, :], rstd[:, d % 2, :], m.minus_half[:, :], ALU.pow).then_inc(rstd2_ready, 1)

                over_tiles(pool, slot, rows=True)

            @block.vector
            def _(v):
                def divide(t, c):
                    v.wait_ge(o_done, t + 1)
                    if later(t, 1):
                        v.wait_ge(o_ready, 2 * t)
                    for j in range(2):
                        v.tensor_scalar(den[:, 8 * j:8 * j + 8].rearrange("p (g h) -> p g h", g=2), ps_o[j][:, :, P:VKW],
                                        DEN_EPS, None, ALU.add).then_inc(den_ready, 1)
                    v.wait_ge(den_ready, 2 * t + 2)
                    v.reciprocal(den[:, :], den[:, :]).then_inc(rden_ready, 1)
                    v.wait_ge(rden_ready, t + 1)
                    if later(t, 2):
                        v.wait_ge(ot_done, t - 1)
                    for j in range(2):
                        v.tensor_tensor(o_sb[:, c % 2, 2 * j * P:2 * (j + 1) * P].rearrange("p (g h e) -> p g h e", g=2, h=4),
                                        ps_o[j][:, :, 0:P].rearrange("p g (h e) -> p g h e", h=4),
                                        den[:, 8 * j:8 * j + 8].rearrange("p (g h) -> p g h", g=2).unsqueeze(3).to_broadcast([P, 2, 4, HEAD]),
                                        ALU.mult).then_inc(o_ready, 1)

                def slot(t, c):
                    if there(t):
                        divide(t, c)
                    u, d = t - 1, c - 1
                    if there(u):
                        v.wait_ge(ot_hi, u + 1)
                        v.tensor_tensor(ot[:, d % 2, 1, :, :], ps_ot[:, :, :], ot[:, d % 2, 0, :, :], ALU.subtract).then_inc(ot_ready, 1)
                    u, d = t - LAG_T, c - LAG_T
                    if there(u):
                        v.wait_ge(h2t_hi, u + 1)
                        v.tensor_tensor(h2t[:, d % 2, 1, :, :], ps_ht[:, :, :], h2t[:, d % 2, 0, :, :], ALU.subtract).then_inc(h2t_ready, 1)
                    u, d = t - LAG_X2, c - LAG_X2
                    if there(u):
                        v.wait_ge(y_done, u + 1)
                        if later(u, 1):
                            v.wait_ge(x2_ready, u)
                        v.scalar_tensor_tensor(out=t1[:, :], in0=ps_y[d % 2][:, :], scalar=1.0 / SCALE, in1=m.rows[:, u // BT, GA, :],
                                               op0=ALU.mult, op1=ALU.mult).then_inc(t1_ready, 1)
                        v.wait_ge(t1_ready, u + 1)
                        v.wait_ge(xg_ready, u + 1)
                        if later(u, 2):
                            v.wait_ge(centred2_ready, u - 1)
                            v.wait_ge(x2_stored[d % 2], uses(u - 2, d))
                        v.tensor_tensor(x2[:, d % 2, :], t1[:, :], xg[:, d % 2, :], ALU.add).then_inc(x2_ready, 1)
                        v.wait_ge(x2_ready, u + 1)
                        v.bn_stats(st[:, d % 2, :], x2[:, d % 2, :]).then_inc(bn2_done, 1)
                        v.wait_ge(bn2_done, u + 1)
                        if later(u, 2):
                            v.wait_ge(scaled_ready, u - 1)
                        v.memset(spare[:, :], 0.0)
                        v.bn_aggr(mv[:, d % 2, :], st[:, d % 2, :]).then_inc(stats2_ready, 1)
                        v.wait_ge(stats2_ready, u + 1)
                        v.tensor_scalar(rstd[:, d % 2, :], mv[:, d % 2, 1:2], LN_EPS, None, ALU.add).then_inc(eps2_added, 1)
                    u, d = t - LAG_H2, c - LAG_H2
                    if there(u):
                        v.wait_ge(stats2_ready, u + 1)
                        if later(u, 2):
                            v.wait_ge(h2_ready, u - 1)
                        v.scalar_tensor_tensor(out=centred[:, d % 2, :], in0=x2[:, d % 2, :], scalar=mv[:, d % 2, 0:1],
                                               in1=m.rows[:, u // BT, CB, :], op0=ALU.subtract, op1=ALU.mult).then_inc(centred2_ready, 1)

                over_tiles(v, slot, rows=True)

            @block.scalar
            def _(act):
                def slot(t, c):
                    u, d = t - 1, c - 1
                    if there(u):
                        act.wait_ge(ot_done, u + 1)
                        if later(u, 2):
                            act.wait_ge(y_done, u - 1)
                        act.activation(ot[:, d % 2, 0, :, :], ps_ot[:, :, :], ACT.Copy).then_inc(ot_hi, 1)
                    u, d = t - LAG_T, c - LAG_T
                    if there(u):
                        act.wait_ge(h2t_done, u + 1)
                        if later(u, 2):
                            act.wait_ge(l_done, u - 1)
                            act.wait_ge(h2t_stored[d % 2], uses(u - 2, d))
                        act.activation(h2t[:, d % 2, 0, :, :], ps_ht[:, :, :], ACT.Copy).then_inc(h2t_hi, 1)
                    u, d = t - LAG_L, c - LAG_L
                    if there(u):
                        act.wait_ge(l_done, u + 1)
                        act.activation(m.logits[:, u, :], ps_l[:, :], ACT.Copy, scale=1.0 / SCALE).then_inc(l_ready, 1)
                    u, d = t - LAG_H2, c - LAG_H2
                    if there(u):
                        act.wait_ge(centred2_ready, u + 1)
                        act.wait_ge(rstd2_ready, u + 1)
                        act.activation(centred[:, d % 2, :], centred[:, d % 2, :], ACT.Copy, scale=rstd[:, d % 2, :]).then_inc(scaled_ready, 1)

                over_tiles(act, slot)

            @block.tensor
            def _(pe):
                def slot(t, c):
                    if there(t):
                        if later(t, 1):
                            pe.wait_ge(o_ready, 2 * t)
                        for g in range(GRP):
                            mm = split_matmul(nc, ps_o[g // 2][:, g % 2, :], (m.qt[:, t, 0, g, :], m.qt[:, t, 1, g, :]),
                                              (m.vk[:, t // BT, 0, g, :], m.vk[:, t // BT, 1, g, :]), True, True)
                        mm.then_inc(o_done, 1)
                    u, d = t - 1, c - 1
                    if there(u):
                        pe.wait_ge(o_ready, 2 * u + 2)
                        if later(u, 1):
                            pe.wait_ge(ot_ready, u)
                        for k in range(KC):
                            mm = nc.tensor.transpose(ps_ot[:, k, :], o_sb[:, d % 2, k * P:(k + 1) * P], m.ident[:, :])
                        mm.then_inc(ot_done, 1)
                    u, d = t - LAG_T, c - LAG_T
                    if there(u):
                        pe.wait_ge(h2_ready, u + 1)
                        if later(u, 1):
                            pe.wait_ge(h2t_ready, u)
                        for k in range(KC):
                            mm = nc.tensor.transpose(ps_ht[:, k, :], h2[:, d % 2, k * P:(k + 1) * P], m.ident[:, :])
                        mm.then_inc(h2t_done, 1)
                    u, d = t - LAG_Y, c - LAG_Y
                    if there(u):
                        pe.wait_ge(ot_ready, u + 1)
                        if later(u, 2):
                            pe.wait_ge(t1_ready, u - 1)
                        for k in range(KC):
                            mm = split_matmul(nc, ps_y[d % 2][:, :], (ot[:, d % 2, 0, k, :], ot[:, d % 2, 1, k, :]),
                                              (m.wproj[:, k, 0, :], m.wproj[:, k, 1, :]), k == 0, k == KC - 1)
                        mm.then_inc(y_done, 1)
                    u, d = t - LAG_L, c - LAG_L
                    if there(u):
                        pe.wait_ge(h2t_ready, u + 1)
                        if later(u, 1):
                            pe.wait_ge(l_ready, u)
                        for k in range(KC):
                            mm = split_matmul(nc, ps_l[:, :], (h2t[:, d % 2, 0, k, :], h2t[:, d % 2, 1, k, :]),
                                              (m.gate[:, k, 0, :], m.gate[:, k, 1, :]), k == 0, k == KC - 1)
                        mm.then_inc(l_done, 1)

                over_tiles(pe, slot)


def carry_waits(pool, spare):
    pool.tensor_tensor(spare, spare, spare, ALU.add)


def shared_steps(nc, m, ctx, tag, first):
    sb = lambda name, shape, dt: ctx.enter_context(nc.sbuf_tensor(name + tag, shape, dt))
    sem = lambda name: m.sem(name + tag)
    CH = 2 * P
    BANKS = 3
    s = Parts()
    ht = sb("s_ht", [P, 2, 2, 2, KC, P], F16)
    act_sb = sb("s_act", [P, 2, CH], F32)
    at = sb("s_at", [P, SH_TILES, 2, CH], F16)
    xs = sb("s_xs", [P, 2, C], F32)
    t1 = sb("s_t1", [P, C], F32)
    h3c = t1[:, 0:CH]
    s.xs = xs
    ps_h = [ctx.enter_context(nc.psum_tensor(f"s_ps_h{j}{tag}", [P, 2, CH], F32)) for j in range(BANKS)]
    ps_y = [ctx.enter_context(nc.psum_tensor(f"s_ps_y{j}{tag}", [P, C], F32)) for j in range(2)]
    ht_loaded = [sem(f"s_ht_loaded{j}") for j in range(2)]
    up_done, silu_done, h3c_done, act_done, at_hi, at_ready = sem("s_up_done"), sem("s_silu"), sem("s_h3c"), sem("s_act"), sem("s_at_hi"), sem("s_at_ready")
    y_done, t1_done, xs_ready = sem("s_y_done"), sem("s_t1"), sem("s_xs_ready")
    xs_loaded = s.xs_loaded = sem("s_xs_loaded")
    xs_stored = s.xs_stored = [sem(f"s_xs_stored{j}") for j in range(2)]
    J = SH_TILES

    def is_first(n, j=0):
        return isinstance(n, int) and n == 0 and j == 0

    def load_h(sp, n, c):
        if not (isinstance(n, int) and n < 2):
            sp.wait_ge(up_done, J * (n - 1))
        for t in range(2):
            sp.dma_start(ht[:, c % 2, t, :, :, :].rearrange("p s k n -> p (s k n)"),
                         m.h2t_d[bass.ds(2 * (n + first) + t, 1), :, :].rearrange("o p n -> (o p) n")).then_inc(ht_loaded[c % 2], 16)

    def load_x(sp, n, c):
        for t in range(2):
            if not is_first(n):
                sp.wait_ge(xs_stored[t], 16 * n)
            sp.dma_start(xs[:, t, :], m.x2_d[bass.ds((2 * (n + first) + t) * P, P), :]).then_inc(xs_loaded, 16)

    def store_x(sp, n, c, to):
        for t in range(2):
            sp.wait_ge(xs_ready, 2 * n + t + 1)
            sp.dma_start(to[bass.ds((2 * (n + first) + t) * P, P), :], xs[:, t, :]).then_inc(xs_stored[t], 16)

    def activate(act, n, c, j):
        i = J * n + j
        act.wait_ge(up_done, i + 1)
        if not (isinstance(n, int) and i < 2):
            act.wait_ge(at_ready, i - 1)
        if j < J - 1:
            act.activation(act_sb[:, j % 2, :], ps_h[j % BANKS][:, 0, :], ACT.Silu, scale=1.0 / SCALE).then_inc(silu_done, 1)
        else:
            if not is_first(n):
                act.wait_ge(xs_ready, 2 * n)
            act.activation(h3c[0:SH_HALF, :], ps_h[j % BANKS][SH_HALF:P, 0, :], ACT.Copy, scale=1.0 / SCALE).then_inc(h3c_done, 1)
            act.activation(act_sb[0:SH_HALF, j % 2, :], ps_h[j % BANKS][0:SH_HALF, 0, :], ACT.Silu, scale=1.0 / SCALE).then_inc(silu_done, 1)

    def high(act, n, j):
        if is_first(n, j):
            return
        n, j = (n, j - 1) if j else (n - 1, J - 1)
        i = J * n + j
        w = P if j < J - 1 else SH_HALF
        act.wait_ge(act_done, i + 1)
        if j == 0 and not is_first(n):
            act.wait_ge(y_done, 2 * n)
        act.activation(at[0:w, j, 0, :], act_sb[0:w, j % 2, :], ACT.Copy).then_inc(at_hi, 1)

    def multiply(v, n, c, j):
        i = J * n + j
        v.wait_ge(silu_done, i + 1)
        if j < J - 1:
            v.scalar_tensor_tensor(out=act_sb[:, j % 2, :], in0=ps_h[j % BANKS][:, 1, :], scalar=1.0 / SCALE,
                                   in1=act_sb[:, j % 2, :], op0=ALU.mult, op1=ALU.mult).then_inc(act_done, 1)
        else:
            v.wait_ge(h3c_done, n + 1)
            v.tensor_tensor(act_sb[0:SH_HALF, j % 2, :], h3c[0:SH_HALF, :], act_sb[0:SH_HALF, j % 2, :], ALU.mult).then_inc(act_done, 1)

    def low(v, n, j):
        if is_first(n, j):
            return
        n, j = (n, j - 1) if j else (n - 1, J - 1)
        w = P if j < J - 1 else SH_HALF
        v.wait_ge(at_hi, J * n + j + 1)
        v.tensor_tensor(at[0:w, j, 1, :], act_sb[0:w, j % 2, :], at[0:w, j, 0, :], ALU.subtract).then_inc(at_ready, 1)

    def add(v, n, t):
        i = 2 * n + t
        v.wait_ge(y_done, i + 1)
        v.wait_ge(act_done, J * (n + 1))
        if not is_first(n, t):
            v.wait_ge(xs_ready, i)
        v.scalar_tensor_tensor(out=t1[:, :], in0=ps_y[t][:, :], scalar=1.0 / SCALE, in1=s.gb_row(n),
                               op0=ALU.mult, op1=ALU.mult).then_inc(t1_done, 1)
        v.wait_ge(t1_done, i + 1)
        s.wait_x(v, n, t)
        v.tensor_tensor(xs[:, t, :], t1[:, :], xs[:, t, :], ALU.add).then_inc(xs_ready, 1)

    def up(pe, n, c, j):
        i = J * n + j
        if j == 0:
            pe.wait_ge(ht_loaded[c % 2], 32 * (n // 2 + 1))
        if not (isinstance(n, int) and i < BANKS):
            pe.wait_ge(act_done, i - BANKS + 1)
        parts = 2 if j < J - 1 else 1
        for part in range(parts):
            for k in range(KC):
                lo = k * 2 * SHARED + (2 * j + part) * P
                mm = split_matmul(nc, ps_h[j % BANKS][:, part, :].rearrange("p (t n) -> p t n", t=2),
                                  (m.sh[:, 0, lo:lo + P], m.sh[:, 1, lo:lo + P]),
                                  (ht[:, c % 2, :, 0, k, :], ht[:, c % 2, :, 1, k, :]), k == 0, k == KC - 1)
        mm.then_inc(up_done, 1)

    def down(pe, n):
        pe.wait_ge(at_ready, J * (n + 1))
        for t in range(2):
            if not is_first(n):
                pe.wait_ge(t1_done, 2 * n - 1 + t)
            for j in range(J):
                w = P if j < J - 1 else SH_HALF
                lo = KC * 2 * SHARED + j * C
                tok = slice(t * P, (t + 1) * P)
                mm = split_matmul(nc, ps_y[t][:, :], (at[0:w, j, 0, tok], at[0:w, j, 1, tok]),
                                  (m.sh[0:w, 0, lo:lo + C], m.sh[0:w, 1, lo:lo + C]), j == 0, j == J - 1)
            mm.then_inc(y_done, 1)

    s.load_h, s.load_x, s.store_x, s.activate, s.high, s.multiply, s.low, s.add, s.up, s.down = (
        load_h, load_x, store_x, activate, high, multiply, low, add, up, down)
    return s


def route(nc, m):
    with ExitStack() as ctx:
        sb = lambda name, shape, dt: ctx.enter_context(nc.sbuf_tensor(name, shape, dt))
        sem = m.sem
        s = shared_steps(nc, m, ctx, "_b", 0)
        gb = sb("gb_b", [P, 2, C], F32)
        s.gb_row = lambda n: gb[:, n // 4, :]
        s.wait_x = lambda v, n, t: v.wait_ge(s.xs_loaded, 32 * (n + 1))
        RING = 4
        stage = sb("w_stage", [P, RING, C], F32)
        bias = sb("bias", [P, E], F32)
        places = {e: [m.w2[:, e, :, :, :].rearrange("p k s n -> p (k s n)"), 0] for e in (E - 2, E - 1)}

        def view(e, shape, dt, rows=P):
            flat, used = places[e]
            size = shape[0] * (shape[1] if len(shape) > 1 else 1) * (shape[2] if len(shape) > 2 else 1) * (1 if dt == F16 else 2)
            places[e][1] += size
            assert places[e][1] <= 3 * 2 * C
            piece = flat[0:rows, used:used + size]
            piece = piece if dt == F16 else piece.bitcast(dt)
            names = "abc"[:len(shape)]
            return piece.rearrange(f"p ({' '.join(names)}) -> p {' '.join(names)}", **dict(zip(names, shape)))

        scores = view(E - 1, (TILES, E), F32)
        sel = view(E - 1, (TILES, E), F32)
        top = view(E - 1, (TILES, 8), F32)
        index = view(E - 1, (TILES, 8), U32)
        choice = view(E - 1, (TOP, TILES, E), F32)
        both = view(E - 2, (TILES, E), F16)
        before = view(E - 2, (P,), F16)
        ones = view(E - 2, (P,), F16)
        passed = view(E - 2, (SLOT_TILES, E), F32, 1)
        indexf = view(E - 2, (TOP, TILES), F32)
        expert_no = sb("expert_no", [P, E], F32)
        onesf = sb("onesf", [P, TILES], F32)
        wsum = view(E - 2, (TILES,), F32)
        count_i = sb("count_i", [P, E], I32)
        padded = sb("padded", [P, E], F32)
        ends = sb("ends", [P, E], F32)
        starts = sb("starts", [P, E], F32)
        slotf = view(E - 2, (TOP, TILES), F32)
        tile_at = view(E - 2, (SLOT_TILES,), F32, 1)
        eidf = view(E - 2, (SLOT_TILES,), F32, 1)
        token = sb("token", [P, TILES], I32)
        entry = sb("entry", [P, TOP, TILES], I32)
        entry_tile = sb("entry_tile", [P, TOP, TILES], I32)
        sc_idx = sb("sc_idx", [P, 2 * TOP, 1], I32)
        sc_tok = sb("sc_tok", [P, 2 * TOP, 1], I32)
        ps_r = ctx.enter_context(nc.psum_tensor("ps_r", [P, 2, TILES * E], F32))
        gb_loaded = sem("gb_loaded")
        w_loaded = [sem(f"w_loaded{j}") for j in range(RING)]
        w_hi, w_lo = sem("w_hi"), sem("w_lo")
        scores_ready, r_step, both_ready, ranks_done = sem("scores_ready"), sem("r_step"), sem("both_ready"), sem("ranks_done")
        consts, slots_ready = sem("consts"), sem("slots_ready")
        idx_copied = sem("idx_copied")
        scattered = [sem(f"scattered{j}") for j in range(2)]
        table_loaded = sem("table_loaded")
        CHUNKS = TILES // 4
        WP = 2 * KC + 3
        TURN = WP + 1

        def piece(e, q):
            if q < 2 * KC:
                k, which = q // 2, q % 2
                src = (m.w1_d, m.w3_d)[which][bass.ds(e, 1), k * P:(k + 1) * P, :].rearrange("o p n -> (o p) n")
                return src, m.w13[:, e, k, :, which * INTER:(which + 1) * INTER], P, INTER
            k = q - 2 * KC
            rows = min(P, INTER - k * P)
            src = m.w2_d[bass.ds(e, 1), k * P:k * P + rows, :].rearrange("o p n -> (o p) n")
            return src, m.w2[0:rows, e, k, :, :], rows, C

        def there(n):
            return not isinstance(n, int) or 0 <= n < CHUNKS

        def over_chunks(eng, chunk, lag=0):
            for n in (0, 1):
                chunk(n, n)
            with eng.Fori(1, CHUNKS // 2 - 1) as pair:
                for c in range(2):
                    chunk(2 * pair + c, c)
            for c in range(2 + lag):
                chunk(CHUNKS - 2 + c, c)

        pieces_beside = [range(0, 2), range(2, 7), range(7, 8), range(8, 9), range(9, 10), range(10, TURN)]

        with nc.Block() as block:
            @block.sync
            def _(sp):
                for b in range(2):
                    sp.dma_start(gb[:, b, :], m.mod_d[b, 5 * C:6 * C].partition_broadcast(P)).then_inc(gb_loaded, 16)
                sp.dma_start(bias[:, :], m.router_bias.partition_broadcast(P)).then_inc(gb_loaded, 16)
                s.load_h(sp, 0, 0)

                def chunk(n, c):
                    if not (isinstance(n, int) and n == CHUNKS - 1):
                        s.load_h(sp, n + 1, c + 1)
                    s.load_x(sp, n, c)
                    s.store_x(sp, n, c, m.x2s_d)

                over_chunks(sp, chunk)
                for t in range(2):
                    sp.wait_ge(s.xs_stored[t], 16 * CHUNKS)

            @block.scalar
            def _(act):
                def load_piece(n, q):
                    if q >= RING:
                        act.wait_ge(w_lo, WP * n + q - RING + 1)
                    elif not (isinstance(n, int) and n == 0):
                        last = max(range(q, WP, RING))
                        act.wait_ge(w_lo, WP * n - WP + last + 1)
                    src, _, rows, cols = piece(n, q)
                    act.dma_start(stage[0:rows, q % RING, 0:cols], src).then_inc(w_loaded[q % RING], 16)

                def piece_high(n, q):
                    if q + RING - 1 < WP:
                        load_piece(n, q + RING - 1)
                    elif q + RING - 1 >= TURN and not (isinstance(n, int) and n == CHUNKS - 1):
                        load_piece(n + 1, q + RING - 1 - TURN)
                    if q == WP:
                        return
                    _, dst, rows, cols = piece(n, q)
                    act.wait_ge(w_loaded[q % RING], 16 * (n * len(range(q % RING, WP, RING)) + q // RING + 1))
                    act.activation(dst[:, 0, :], stage[0:rows, q % RING, 0:cols], ACT.Copy, scale=SCALE).then_inc(w_hi, 1)

                def chunk(n, c):
                    for j in range(SH_TILES):
                        if there(n):
                            s.activate(act, n, c, j)
                        if j != DOWN_AT - 1 and (there(n) or j == 0):
                            s.high(act, n, j)
                        if there(n):
                            for q in pieces_beside[j]:
                                piece_high(n, q)
                        if j == DOWN_AT - 1 and there(n):
                            s.high(act, n, j)

                for q in range(RING - 1):
                    load_piece(0, q)
                act.activation(scores[:, :, :], m.logits[:, :, :], ACT.Sigmoid).then_inc(scores_ready, 1)
                over_chunks(act, chunk, lag=1)

            @block.vector
            def _(v):
                steps = 0

                def step(instruction):
                    nonlocal steps
                    steps += 1
                    instruction.then_inc(r_step, 1)
                    v.wait_ge(r_step, steps)

                def find_top():
                    v.wait_ge(scores_ready, 1)
                    v.wait_ge(gb_loaded, 48)
                    step(v.tensor_tensor(sel[:, :, :], scores[:, :, :], bias[:, :].unsqueeze(1).to_broadcast([P, TILES, E]), ALU.add))
                    nonlocal steps
                    for t in range(TILES):
                        v.max(top[:, t, :], sel[:, t, :]).then_inc(r_step, 1)
                    steps += TILES
                    v.wait_ge(r_step, steps)

                def find_index():
                    nonlocal steps
                    for t in range(TILES):
                        v.max_index(index[:, t, :], top[:, t, :], sel[:, t, :]).then_inc(r_step, 1)
                    steps += TILES
                    v.wait_ge(r_step, steps)

                def weigh():
                    v.wait_ge(consts, 5)
                    for k in range(TOP):
                        step(v.tensor_copy(indexf[:, k, :], index[:, :, k]))
                        step(v.tensor_tensor(choice[:, k, :, :], expert_no[:, :].unsqueeze(1).to_broadcast([P, TILES, E]),
                                             indexf[:, k, :].unsqueeze(2).to_broadcast([P, TILES, E]), ALU.is_equal))
                        step(v.tensor_tensor(sel[:, :, :], choice[:, k, :, :], scores[:, :, :], ALU.mult))
                        step(v.reduce_sum(m.weight[:, k, :], sel[:, :, :], AX.X))
                    step(v.tensor_tensor(wsum[:, :], m.weight[:, 0, :], m.weight[:, 1, :], ALU.add))
                    step(v.tensor_scalar(wsum[:, :], wsum[:, :], SUM_EPS, None, ALU.max))
                    step(v.reciprocal(wsum[:, :], wsum[:, :]))
                    for k in range(TOP):
                        step(v.tensor_tensor(m.weight[:, k, :], m.weight[:, k, :], wsum[:, :], ALU.mult))
                    v.tensor_tensor(both[:, :, :], choice[:, 0, :, :], choice[:, 1, :, :], ALU.add).then_inc(both_ready, 1)

                rank = ps_r[:, 0, :].rearrange("p (t e) -> p t e", e=E)
                total = ps_r[:, 1, :].rearrange("p (t e) -> p e t", e=E)
                pos = sel
                run = top[:, :, :].rearrange("p t e -> p (t e)").rearrange("p (e t) -> p e t", e=E)

                def add_runs():
                    v.wait_ge(ranks_done, 2)
                    for e in range(E):
                        step(v.tensor_tensor_scan(run[:, e, :], onesf[:, :], total[:, e, :], 0.0, ALU.mult, ALU.add))
                    step(v.tensor_scalar(padded[:, :], run[:, :, TILES - 1], float(P - 1), None, ALU.add))
                    step(v.tensor_copy(count_i[:, :], padded[:, :]))
                    step(v.tensor_scalar(count_i[:, :], count_i[:, :], -P, None, ALU.bitwise_and))
                    step(v.tensor_copy(padded[:, :], count_i[:, :]))
                    step(v.tensor_tensor_scan(ends[:, :], onesf[:, 0:E], padded[:, :], 0.0, ALU.mult, ALU.add))
                    step(v.tensor_tensor(starts[:, :], ends[:, :], padded[:, :], ALU.subtract))

                def place():
                    step(v.tensor_tensor(run, run, starts[:, :].unsqueeze(2).to_broadcast([P, E, TILES]), ALU.add))
                    step(v.tensor_tensor(run, run, total, ALU.subtract))
                    step(v.tensor_tensor(pos[:, :, :], rank, run.rearrange("p e t -> p t e"), ALU.add))
                    for k in range(TOP):
                        step(v.tensor_tensor(scores[:, :, :], choice[:, k, :, :], pos[:, :, :], ALU.mult))
                        step(v.reduce_sum(slotf[:, k, :], scores[:, :, :], AX.X))
                    step(v.tensor_copy(m.slot[:, :, :], slotf[:, :, :]))
                    step(v.tensor_scalar(entry[:, :, :], m.slot[:, :, :], P - 1, None, ALU.bitwise_and))
                    step(v.tensor_scalar(entry[:, :, :], entry[:, :, :], float(SLOT_TILES), None, ALU.mult))
                    step(v.tensor_scalar(entry_tile[:, :, :], m.slot[:, :, :], P.bit_length() - 1, None, ALU.logical_shift_right))
                    v.tensor_tensor(entry[:, :, :], entry[:, :, :], entry_tile[:, :, :], ALU.add).then_inc(slots_ready, 1)

                def name_tiles():
                    step(v.tensor_tensor(passed[:, :, :], ends[0:1, :].unsqueeze(1).to_broadcast([1, SLOT_TILES, E]),
                                         tile_at[:, :].unsqueeze(2).to_broadcast([1, SLOT_TILES, E]), ALU.is_le))
                    step(v.reduce_sum(eidf[:, :], passed[:, :, :], AX.X))
                    step(v.tensor_scalar(eidf[:, :], eidf[:, :], float(E - 1), None, ALU.min))
                    step(v.tensor_copy(m.eid[:, :], eidf[:, :]))

                def piece_low(n, q):
                    _, dst, rows, cols = piece(n, q)
                    v.wait_ge(w_hi, WP * n + q + 1)
                    v.scalar_tensor_tensor(out=dst[:, 1, :], in0=stage[0:rows, q % RING, 0:cols], scalar=SCALE, in1=dst[:, 0, :],
                                           op0=ALU.mult, op1=ALU.subtract).then_inc(w_lo, 1)

                def chunk(n, c):
                    for j in range(SH_TILES):
                        if there(n):
                            s.multiply(v, n, c, j)
                        if j != DOWN_AT - 1 and (there(n) or j == 0):
                            s.low(v, n, j)
                        if there(n):
                            for q in pieces_beside[j]:
                                if q < WP:
                                    piece_low(n, q)
                        if isinstance(n, int) and (n, j) in beside:
                            beside[n, j]()
                        if j == DOWN_AT - 1 and there(n - 1):
                            for t in range(2):
                                s.add(v, n - 1, t)
                        if j == DOWN_AT - 1 and there(n):
                            s.low(v, n, j)

                beside = {(0, 1): find_top, (0, 3): find_index, (0, 5): weigh, (1, 1): add_runs, (1, 3): place, (1, 4): name_tiles}
                over_chunks(v, chunk, lag=1)

            @block.tensor
            def _(pe):
                def chunk(n, c):
                    for j in range(SH_TILES):
                        if there(n):
                            s.up(pe, n, c, j)
                        if isinstance(n, int) and (n, j) == (1, 1):
                            pe.wait_ge(both_ready, 1)
                            pe.wait_ge(consts, 6)
                            for part, lhs in ((0, before), (1, ones)):
                                nc.tensor.matmul(ps_r[:, part, :], lhs[:, :], both[:, :, :].rearrange("p t e -> p (t e)"),
                                                 start=True, stop=True).then_inc(ranks_done, 1)
                        if j == DOWN_AT - 1 and there(n - 1):
                            s.down(pe, n - 1)

                over_chunks(pe, chunk, lag=1)

            @block.gpsimd
            def _(pool):
                pool.iota(expert_no[:, :], [[1, E]], base=0, channel_multiplier=0, allow_small_or_imprecise_dtypes=True).then_inc(consts, 1)
                pool.iota(tile_at[:, :], [[P, SLOT_TILES]], base=0, channel_multiplier=0, allow_small_or_imprecise_dtypes=True).then_inc(consts, 1)
                pool.iota(token[:, :], [[P, TILES]], base=0, channel_multiplier=1).then_inc(consts, 1)
                pool.memset(ones[:, :], 1.0).then_inc(consts, 1)
                pool.memset(onesf[:, :], 1.0).then_inc(consts, 1)
                pool.wait_ge(consts, 5)
                pool.affine_select(out=before[:, :], in_=ones[:, :], compare_op=ALU.is_gt, fill=0.0,
                                   base=0, pattern=[[1, P]], channel_multiplier=-1).then_inc(consts, 1)
                pool.wait_ge(consts, 6)
                pool.wait_ge(slots_ready, 1)

                def scatter(pair, c, k):
                    t, r = 2 * pair + c, TOP * c + k
                    if k == 0 and not (isinstance(pair, int) and pair == 0):
                        pool.wait_ge(scattered[c], 16 * TOP * pair)
                    pool.tensor_copy(sc_idx[:, r, :], entry[:, k, bass.ds(t, 1)]).then_inc(idx_copied, 1)
                    pool.tensor_copy(sc_tok[:, r, :], token[:, bass.ds(t, 1)]).then_inc(idx_copied, 1)
                    pool.wait_ge(idx_copied, 2 * (TOP * t + k + 1))
                    carry_waits(pool, m.spare[:, :])
                    pool.indirect_dma_start(m.table, bass.IndirectOffsetOnAxis(ap=sc_idx[:, r, :], axis=0),
                                            sc_tok[:, r, :], None).then_inc(scattered[c], 16)

                for c in range(2):
                    for k in range(TOP):
                        scatter(0, c, k)
                with pool.Fori(1, TILES // 2) as pair:
                    for c in range(2):
                        for k in range(TOP):
                            scatter(pair, c, k)
                for c in range(2):
                    pool.wait_ge(scattered[c], 16 * TOP * TILES // 2)
                pool.dma_start(m.slot_token[:, :], m.table.rearrange("(p t) o -> p (t o)", p=P)).then_inc(table_loaded, 16)
                pool.wait_ge(table_loaded, 16)


def experts(nc, m):
    with ExitStack() as ctx:
        sb = lambda name, shape, dt: ctx.enter_context(nc.sbuf_tensor(name, shape, dt))
        pb = lambda name, shape: ctx.enter_context(nc.psum_tensor(name, shape, F32))
        sem = m.sem
        IT = 3
        g_idx = sb("g_idx", [P, 2, 1], I32)
        g = sb("g", [P, 2, C], F32)
        xt = sb("xt", [P, 2, 2, KC, P], F16)
        a = sb("a", [P, 2, IT * P], F32)
        at = sb("at", [P, 2, 2, IT, P], F16)
        y = sb("y", [P, 2, C], F32)
        ps_x, ps_h1, ps_h3, ps_a, ps_y = pb("ps_x", [P, KC, P]), pb("ps_h1", [P, INTER]), pb("ps_h3", [P, INTER]), pb("ps_a", [P, IT, P]), pb("ps_ey", [P, C])
        g_idx_copied = sem("g_idx_copied")
        gathered = [sem(f"gathered{j}") for j in range(2)]
        xt_done, xt_hi, xt_ready, h1_done, h3_done = sem("xt_done"), sem("xt_hi"), sem("xt_ready"), sem("h1_done"), sem("h3_done")
        e_silu, e_act, a_padded, at_done, e_at_hi, e_at_ready = sem("e_silu"), sem("e_act"), sem("a_padded"), sem("at_done"), sem("e_at_hi"), sem("e_at_ready")
        ey_done, ey_ready = sem("ey_done"), sem("ey_ready")
        y_stored = [sem(f"y_stored{j}") for j in range(2)]

        def later(t, n):
            return not isinstance(t, int) or t >= n

        def there(t):
            return not isinstance(t, int) or 0 <= t < SLOT_TILES

        def over_tiles(eng, slot):
            for t in (0, 1):
                slot(t, t)
            with eng.Fori(1, (SLOT_TILES - 1) // 2) as pair:
                for c in range(2):
                    slot(2 * pair + c, c)
            for t in range(SLOT_TILES - 1 - (SLOT_TILES - 1) % 2, SLOT_TILES + 1):
                slot(t, t)

        with nc.Block() as block:
            @block.gpsimd
            def _(pool):
                def gather(t, c):
                    if not there(t):
                        return
                    if later(t, 2):
                        pool.wait_ge(gathered[c % 2], 16 * (t // 2))
                        pool.wait_ge(xt_done, t - 1)
                    pool.tensor_copy(g_idx[:, c % 2, :], m.slot_token[:, bass.ds(t, 1)]).then_inc(g_idx_copied, 1)
                    pool.wait_ge(g_idx_copied, t + 1)
                    carry_waits(pool, m.spare[:, :])
                    pool.indirect_dma_start(g[:, c % 2, :], None, m.h2_d,
                                            bass.IndirectOffsetOnAxis(ap=g_idx[:, c % 2, :], axis=0)).then_inc(gathered[c % 2], 16)

                over_tiles(pool, gather)

            @block.sync
            def _(sp):
                def slot(t, c):
                    u, d = t - 1, c - 1
                    if there(u):
                        sp.wait_ge(ey_ready, u + 1)
                        sp.dma_start(m.y_d[bass.ds(u * P, P), :], y[:, d % 2, :]).then_inc(y_stored[d % 2], 16)

                over_tiles(sp, slot)
                sp.wait_ge(y_stored[0], 16 * ((SLOT_TILES + 1) // 2))
                sp.wait_ge(y_stored[1], 16 * (SLOT_TILES // 2))

            @block.scalar
            def _(act):
                def x_high(t, c):
                    if not there(t):
                        return
                    act.wait_ge(xt_done, t + 1)
                    if later(t, 2):
                        act.wait_ge(h3_done, t - 1)
                    act.activation(xt[:, c % 2, 0, :, :], ps_x[:, :, :], ACT.Copy).then_inc(xt_hi, 1)

                def slot(t, c):
                    u, d = t - 1, c - 1
                    if there(u):
                        act.wait_ge(at_done, u + 1)
                        if later(u, 2):
                            act.wait_ge(ey_done, u - 1)
                        act.activation(at[:, d % 2, 0, :, :], ps_a[:, :, :], ACT.Copy).then_inc(e_at_hi, 1)
                    x_high(t + 1, c + 1)
                    if there(t):
                        act.wait_ge(h1_done, t + 1)
                        if later(t, 2):
                            act.wait_ge(at_done, t - 1)
                        act.activation(a[:, c % 2, 0:INTER], ps_h1[:, :], ACT.Silu, scale=1.0 / SCALE).then_inc(e_silu, 1)
                    if there(u):
                        act.wait_ge(ey_done, u + 1)
                        if later(u, 2):
                            act.wait_ge(y_stored[d % 2], 16 * (u // 2))
                        act.activation(y[:, d % 2, :], ps_y[:, :], ACT.Copy, scale=1.0 / SCALE).then_inc(ey_ready, 1)

                x_high(0, 0)
                over_tiles(act, slot)

            @block.vector
            def _(v):
                v.memset(a[:, :, INTER:IT * P], 0.0).then_inc(a_padded, 1)

                def x_low(t, c):
                    if not there(t):
                        return
                    v.wait_ge(xt_hi, t + 1)
                    v.tensor_tensor(xt[:, c % 2, 1, :, :], ps_x[:, :, :], xt[:, c % 2, 0, :, :], ALU.subtract).then_inc(xt_ready, 1)

                def slot(t, c):
                    u, d = t - 1, c - 1
                    if there(u):
                        v.wait_ge(e_at_hi, u + 1)
                        v.tensor_tensor(at[:, d % 2, 1, :, :], ps_a[:, :, :], at[:, d % 2, 0, :, :], ALU.subtract).then_inc(e_at_ready, 1)
                    x_low(t + 1, c + 1)
                    if there(t):
                        v.wait_ge(h3_done, t + 1)
                        v.wait_ge(e_silu, t + 1)
                        v.scalar_tensor_tensor(out=a[:, c % 2, 0:INTER], in0=ps_h3[:, :], scalar=1.0 / SCALE, in1=a[:, c % 2, 0:INTER],
                                               op0=ALU.mult, op1=ALU.mult).then_inc(e_act, 1)

                x_low(0, 0)
                over_tiles(v, slot)

            @block.tensor
            def _(pe):
                def transpose_x(t, c):
                    if not there(t):
                        return
                    pe.wait_ge(gathered[c % 2], 16 * (t // 2 + 1))
                    if later(t, 1):
                        pe.wait_ge(xt_ready, t)
                    for k in range(KC):
                        mm = nc.tensor.transpose(ps_x[:, k, :], g[:, c % 2, k * P:(k + 1) * P], m.ident[:, :])
                    mm.then_inc(xt_done, 1)

                def up(t, c):
                    expert = pe.value_load(m.eid[0:1, bass.ds(t, 1)], min_val=0, max_val=E - 1)
                    pe.wait_ge(xt_ready, t + 1)
                    for which, ps, done in ((0, ps_h1, h1_done), (1, ps_h3, h3_done)):
                        if later(t, 1):
                            pe.wait_ge(e_act, t)
                        cols = slice(which * INTER, (which + 1) * INTER)
                        for k in range(KC):
                            mm = split_matmul(nc, ps[:, :], (xt[:, c % 2, 0, k, :], xt[:, c % 2, 1, k, :]),
                                              (m.w13[:, bass.ds(expert, 1), k, 0, cols].rearrange("p o n -> p (o n)"),
                                               m.w13[:, bass.ds(expert, 1), k, 1, cols].rearrange("p o n -> p (o n)")),
                                              k == 0, k == KC - 1)
                        mm.then_inc(done, 1)

                def transpose_a(t, c):
                    pe.wait_ge(a_padded, 1)
                    pe.wait_ge(e_act, t + 1)
                    if later(t, 1):
                        pe.wait_ge(e_at_ready, t)
                    for k in range(IT):
                        mm = nc.tensor.transpose(ps_a[:, k, :], a[:, c % 2, k * P:(k + 1) * P], m.ident[:, :])
                    mm.then_inc(at_done, 1)

                def down(t, c):
                    expert = pe.value_load(m.eid[0:1, bass.ds(t, 1)], min_val=0, max_val=E - 1)
                    pe.wait_ge(e_at_ready, t + 1)
                    if later(t, 1):
                        pe.wait_ge(ey_ready, t)
                    for k in range(IT):
                        w = min(P, INTER - k * P)
                        mm = split_matmul(nc, ps_y[:, :], (at[0:w, c % 2, 0, k, :], at[0:w, c % 2, 1, k, :]),
                                          (m.w2[0:w, bass.ds(expert, 1), k, 0, :].rearrange("p o n -> p (o n)"),
                                           m.w2[0:w, bass.ds(expert, 1), k, 1, :].rearrange("p o n -> p (o n)")),
                                          k == 0, k == IT - 1)
                    mm.then_inc(ey_done, 1)

                def slot(t, c):
                    if there(t - 1):
                        transpose_a(t - 1, c - 1)
                    transpose_x(t + 1, c + 1)
                    if there(t):
                        up(t, c)
                    if there(t - 1):
                        down(t - 1, c - 1)

                transpose_x(0, 0)
                over_tiles(pe, slot)


def combine(nc, m):
    with ExitStack() as ctx:
        sb = lambda name, shape, dt: ctx.enter_context(nc.sbuf_tensor(name, shape, dt))
        sem = m.sem
        CHUNKS = TILES // 4
        PER = 4
        s = shared_steps(nc, m, ctx, "_d", CHUNKS)
        gb = sb("gb_d", [P, B, C], F32)
        s.gb_row = lambda n: gb[:, (n + CHUNKS) // 4, :]
        y_idx = sb("y_idx", [P, PER, TOP, 1], I32)
        y = sb("y_rows", [P, PER, TOP, C], F32)
        xc = sb("xc", [P, 2, C], F32)
        gb_loaded = sem("gb_loaded_d")
        y_idx_copied, combined, merged, c_step = sem("y_idx_copied"), sem("combined"), sem("merged"), sem("c_step")
        y_loaded = [sem(f"y_loaded{j}") for j in range(PER)]
        out_stored = [sem(f"out_stored{j}") for j in range(2)]
        s.wait_x = lambda v, n, t: v.wait_ge(merged, 2 * n + t + 1)

        combined_beside = [(), (0, 1), (), (2,), (3,), ()]

        def tile(n, j):
            return 2 * n + j if j < 2 else 2 * n + j - 2 + TILES // 2

        def there(n):
            return not isinstance(n, int) or 0 <= n < CHUNKS

        def over_chunks(eng, chunk, lag=0):
            for n in (0, 1):
                chunk(n, n)
            with eng.Fori(1, CHUNKS // 2 - 1) as pair:
                for c in range(2):
                    chunk(2 * pair + c, c)
            for c in range(2 + lag):
                chunk(CHUNKS - 2 + c, c)

        with nc.Block() as block:
            @block.sync
            def _(sp):
                for b in range(B):
                    sp.dma_start(gb[:, b, :], m.mod_d[b, 5 * C:6 * C].partition_broadcast(P)).then_inc(gb_loaded, 16)
                s.load_h(sp, 0, 0)

                def chunk(n, c):
                    if not (isinstance(n, int) and n == CHUNKS - 1):
                        s.load_h(sp, n + 1, c + 1)
                    s.load_x(sp, n, c)
                    s.store_x(sp, n, c, m.out)

                over_chunks(sp, chunk)
                for t in range(2):
                    sp.wait_ge(s.xs_stored[t], 16 * CHUNKS)

            @block.gpsimd
            def _(pool):
                def fetch(n, j):
                    if not (isinstance(n, int) and n == 0):
                        if j < 2:
                            pool.wait_ge(out_stored[j], 16 * n)
                        else:
                            pool.wait_ge(merged, 2 * n + j - 3)
                    for k in range(TOP):
                        pool.tensor_copy(y_idx[:, j, k, :], m.slot[:, k, bass.ds(tile(n, j), 1)]).then_inc(y_idx_copied, 1)
                    pool.wait_ge(y_idx_copied, TOP * (PER * n + j + 1))
                    carry_waits(pool, m.spare[:, :])
                    for k in range(TOP):
                        pool.indirect_dma_start(y[:, j, k, :], None, m.y_d,
                                                bass.IndirectOffsetOnAxis(ap=y_idx[:, j, k, :], axis=0)).then_inc(y_loaded[j], 16)
                    if j < 2:
                        pool.dma_start(xc[:, j, :], m.x2s_d[bass.ds(tile(n, j) * P, P), :]).then_inc(y_loaded[j], 16)

                def chunk(n, c):
                    for j in range(PER):
                        fetch(n, j)

                over_chunks(pool, chunk)

            @block.scalar
            def _(act):
                def store(n, j):
                    act.wait_ge(combined, 2 * n + j + 1)
                    act.dma_start(m.out[bass.ds(tile(n, j) * P, P), :], y[:, j, 1, :]).then_inc(out_stored[j], 16)

                def chunk(n, c):
                    for j in range(SH_TILES):
                        if there(n):
                            s.activate(act, n, c, j)
                            if 1 <= j <= 2:
                                store(n, j - 1)
                        if there(n) or j == 0:
                            s.high(act, n, j)

                over_chunks(act, chunk, lag=1)
                for j in range(2):
                    act.wait_ge(out_stored[j], 16 * CHUNKS)

            @block.vector
            def _(v):
                def combine_tile(n, j):
                    t = tile(n, j)
                    done = 3 * (PER * n + j)
                    v.wait_ge(y_loaded[j], 16 * (TOP + 1 if j < 2 else TOP) * (n + 1))
                    v.tensor_scalar(y[:, j, 0, :], y[:, j, 0, :], m.weight[:, 0, bass.ds(t, 1)], None, ALU.mult).then_inc(c_step, 1)
                    v.wait_ge(c_step, done + 1)
                    v.scalar_tensor_tensor(out=y[:, j, 1, :], in0=y[:, j, 1, :], scalar=m.weight[:, 1, bass.ds(t, 1)],
                                           in1=y[:, j, 0, :], op0=ALU.mult, op1=ALU.add).then_inc(c_step, 1)
                    v.wait_ge(c_step, done + 2)
                    v.tensor_tensor(y[:, j, 1, :], y[:, j, 1, :], gb[:, t // BT, :], ALU.mult).then_inc(c_step, 1)
                    v.wait_ge(c_step, done + 3)
                    if j < 2:
                        v.tensor_tensor(y[:, j, 1, :], y[:, j, 1, :], xc[:, j, :], ALU.add).then_inc(combined, 1)
                    else:
                        v.wait_ge(s.xs_loaded, 32 * (n + 1))
                        v.tensor_tensor(s.xs[:, j - 2, :], y[:, j, 1, :], s.xs[:, j - 2, :], ALU.add).then_inc(merged, 1)

                def chunk(n, c):
                    for j in range(SH_TILES):
                        if there(n):
                            s.multiply(v, n, c, j)
                            for b in combined_beside[j]:
                                combine_tile(n, b)
                        if j == DOWN_AT - 1 and there(n - 1):
                            for t in range(2):
                                s.add(v, n - 1, t)
                        if there(n) or j == 0:
                            s.low(v, n, j)

                v.wait_ge(gb_loaded, 16 * B)
                over_chunks(v, chunk, lag=1)

            @block.tensor
            def _(pe):
                def chunk(n, c):
                    for j in range(SH_TILES):
                        if there(n):
                            s.up(pe, n, c, j)
                        if j == DOWN_AT - 1 and there(n - 1):
                            s.down(pe, n - 1)

                over_chunks(pe, chunk, lag=1)


def adaln_block(nc, x, wqkv_t, wproj_t, b_proj, gate_t, router_bias, w1_d, w3_d, w2_d, sh_flat, c_t, wmod_d, out):
    m = Parts()
    m.x, m.wqkv_t, m.wproj_t, m.b_proj, m.gate_t, m.router_bias = x, wqkv_t, wproj_t, b_proj, gate_t, router_bias
    m.w1_d, m.w3_d, m.w2_d, m.sh_flat, m.c_t, m.wmod_d, m.out = w1_d, w3_d, w2_d, sh_flat, c_t, wmod_d, out
    with ExitStack() as ctx:
        m.sem = lambda name: ctx.enter_context(nc.semaphore(name))
        dram = lambda name, shape, dt: nc.dram_tensor(name, shape, dt).ap()
        m.x2_d, m.x2s_d, m.h2_d = dram("x2_d", (T, C), F32), dram("x2s_d", (T, C), F32), dram("h2_d", (T, C), F32)
        m.h2t_d, m.y_d = dram("h2t_d", (TILES, P, 2 * C), F16), dram("y_d", (SLOTS, C), F32)
        m.mod_d, m.gab_d, m.table = dram("mod_d", (B, 6 * C), F32), dram("gab_d", (B, C), F32), dram("table", (SLOTS, 1), I32)

        def sb(name, shape, dt, stack=ctx):
            return stack.enter_context(nc.sbuf_tensor(name, shape, dt))

        m.ident = sb("ident", [P, P], F32)
        m.spare = sb("spare", [P, 1], F32)
        m.logits = sb("logits", [P, TILES, E], F32)
        m.weight = sb("weight", [P, TOP, TILES], F32)
        m.slot = sb("slot", [P, TOP, TILES], I32)
        m.slot_token = sb("slot_token", [P, SLOT_TILES], I32)
        m.eid = sb("eid", [1, SLOT_TILES], I32)
        m.sh = sb("sh", [P, 2, KC * 2 * SHARED + SH_TILES * C], F16)
        with ExitStack() as attention:
            m.gate = sb("gate", [P, KC, 2, E], F16, attention)
            m.heads = sb("heads", [P, 4], F32, attention)
            m.head_mask = sb("head_mask", [P, P], F32, attention)
            m.minus_half = sb("minus_half", [P, 1], F32, attention)
            m.wproj = sb("wproj", [P, KC, 2, C], F16, attention)
            m.vk = sb("vk", [P, B, 2, GRP, VKW], F16, attention)
            m.qt_flat = sb("qt", [P, TILES * 2 * GRP * P], F16, attention)
            m.qt = m.qt_flat[:, :].rearrange("p (t s g n) -> p t s g n", t=TILES, s=2, g=GRP)
            with ExitStack() as projections:
                m.wqkv = sb("wqkv", [P, KC, 2, 3 * C], F16, projections)
                m.v_sb = sb("v_sb", [P, 2, GRP, P + 1], F32, projections)
                m.rows = sb("rows", [P, B, 2, C], F32, projections)
                front(nc, m)
            back(nc, m)
        with ExitStack() as expert_weights:
            m.w13 = sb("w13", [P, E, KC, 2, 2 * INTER], F16, expert_weights)
            m.w2 = sb("w2", [P, E, 3, 2, C], F16, expert_weights)
            route(nc, m)
            experts(nc, m)
        combine(nc, m)


def kernel(L0_attn_x, L0_attn_w_qkv, L0_attn_w_proj, L0_attn_b_proj, L0_ffn_gate_w, L0_ffn_router_bias, L0_ffn_W1,
           L0_ffn_W3, L0_ffn_W2, L0_ffn_sw1, L0_ffn_sw3, L0_ffn_sw2, L0_c, L0_wmod):
    import numpy as np
    import concourse.bacc as bacc
    from concourse.bass_utils import run_bass_kernel_spmd as run

    def t(a):
        return np.ascontiguousarray(np.asarray(a).T)

    sw1, sw3, sw2 = t(L0_ffn_sw1), t(L0_ffn_sw3), t(L0_ffn_sw2)
    turns = [w[:, j * P:(j + 1) * P] for j in range(SH_TILES) for w in (sw1, sw3)]
    up = np.concatenate(turns, axis=1).reshape(KC, P, 2 * SHARED).transpose(1, 0, 2).reshape(P, -1)
    down = np.zeros((SH_TILES * P, C), sw2.dtype)
    down[:SHARED] = sw2
    down = down.reshape(SH_TILES, P, C).transpose(1, 0, 2).reshape(P, -1)
    arrays = {
        "x": np.ascontiguousarray(L0_attn_x).reshape(T, C), "wqkv_t": t(L0_attn_w_qkv), "wproj_t": t(L0_attn_w_proj),
        "b_proj": np.ascontiguousarray(L0_attn_b_proj), "gate_t": t(L0_ffn_gate_w),
        "router_bias": np.ascontiguousarray(L0_ffn_router_bias), "w1_d": np.ascontiguousarray(L0_ffn_W1),
        "w3_d": np.ascontiguousarray(L0_ffn_W3), "w2_d": np.ascontiguousarray(L0_ffn_W2),
        "sh_flat": np.ascontiguousarray(np.concatenate([up, down], axis=1)), "c_t": t(L0_c),
        "wmod_d": np.ascontiguousarray(L0_wmod),
    }
    nc = bacc.Bacc("TRN2", target_bir_lowering=False, num_devices=1)
    handles = {k: nc.dram_tensor(f"in_{k}", v.shape, mybir.dt.from_np(v.dtype), kind="ExternalInput").ap() for k, v in arrays.items()}
    out = nc.dram_tensor("out_0", (T, C), F32, kind="ExternalOutput").ap()
    adaln_block(nc, out=out, **handles)
    r = run(nc, [{f"in_{k}": v for k, v in arrays.items()}], core_ids=[0])
    return r.results[0]["out_0"].reshape(B, N, C)
```
